# Optimizing a Trainium2 kernel written in Bass

```python
import numpy as np
import jax
import jax.numpy as jnp

def _softmax(x, axis=-1):
    return jax.nn.softmax(x, axis=axis)

def _gelu(x):
    return jax.nn.gelu(x, approximate=True)

def _silu(x):
    return jax.nn.silu(x)

def _sigmoid(x):
    return jax.nn.sigmoid(x)

def _layernorm(x, axis=-1, eps=1e-05):
    m = jnp.mean(x, axis=axis, keepdims=True)
    v = jnp.var(x, axis=axis, keepdims=True)
    return (x - m) / jnp.sqrt(v + eps)

def _scatter_add(tgt, idx, src, axis=0):
    return tgt.at[idx].add(src)

def _segment_sum(src, seg, n):
    return jax.ops.segment_sum(src, seg, n)
kernel_name = 'mk_lm_tower_d1_tok_ids768_r4_d7879d'

def setup_inputs(seed: int=0):
    np.random.seed(seed)
    _w = jnp.asarray

    def _rec_inputs():
        import jax
        import jax.numpy as jnp
        _rk = jax.random.key(seed)
        x = jax.random.randint(jax.random.fold_in(_rk, 1), (8, 256), 0, 12564, jnp.int32)
        return x
    x = _rec_inputs()

    def _L0_tok_setup():
        import jax, jax.numpy as jnp
        import numpy as np
        VOCAB = 50257
        EMBED_DIM = 192
        N_SUBPOS = 3
        REPEAT = 2
        SUB_DIM = EMBED_DIM // (REPEAT + 1)

        def positional_encoding(max_len, d_model):
            depth = d_model // 2
            positions = jnp.arange(max_len, dtype=jnp.float32)[:, None]
            depths = (jnp.arange(depth, dtype=jnp.float32) / depth)[None, :]
            angle_rates = 1.0 / 10000.0 ** depths
            angle_rads = positions * angle_rates
            return jnp.concatenate([jnp.sin(angle_rads), jnp.cos(angle_rads)], axis=-1)
        key = jax.random.key(seed)
        k1, k2, k3, k4 = jax.random.split(key, 4)
        tokens = jax.random.randint(k1, (16, 512), 0, VOCAB, dtype=jnp.int32)
        emb_table = jax.random.normal(k2, (VOCAB, SUB_DIM), dtype=jnp.float32) * 0.02
        spos0 = jax.random.normal(k3, (N_SUBPOS, SUB_DIM), dtype=jnp.float32) * 0.02
        spos1 = jax.random.normal(k4, (N_SUBPOS, SUB_DIM), dtype=jnp.float32) * 0.02
        return {'tokens': tokens, 'emb_table': emb_table, 'spos0': spos0, 'spos1': spos1}
    _L0_tok_all = _L0_tok_setup()
    _L0_tok_in = {k: v for k, v in _L0_tok_all.items() if k in ('emb_table', 'spos0', 'spos1')}
    del _L0_tok_all

    def _L0_attn_setup():
        import jax, jax.numpy as jnp
        import numpy as np
        BSZ, SEQ, D_MODEL = (2, 512, 192)
        EXPAND, D_STATE, D_CONV = (2, 16, 3)
        D_INNER = EXPAND * D_MODEL
        DT_RANK = (D_MODEL + 15) // 16
        EPS = 1e-05

        def layernorm(x, g, b):
            mu = jnp.mean(x, axis=-1, keepdims=True)
            var = jnp.mean((x - mu) ** 2, axis=-1, keepdims=True)
            return (x - mu) * jax.lax.rsqrt(var + EPS) * g + b

        def depthwise_conv1d(x, w, b):
            K = w.shape[1]
            pad = (K - 1) // 2
            L = x.shape[1]
            xp = jnp.pad(x, ((0, 0), (pad, pad), (0, 0)))
            y = sum((xp[:, k:k + L, :] * w[:, k] for k in range(K)))
            return y + b

        def selective_scan(u, delta, A, Bm, Cm):

            def step(h, xs):
                d_t, u_t, B_t, C_t = xs
                dA = jnp.exp(d_t[..., None] * A)
                h = dA * h + (d_t * u_t)[..., None] * B_t[:, None, :]
                y = jnp.einsum('bdn,bn->bd', h, C_t)
                return (h, y)
            B_, L_, d_ = u.shape
            h0 = jnp.zeros((B_, d_, A.shape[1]), u.dtype)
            xs = (delta.transpose(1, 0, 2), u.transpose(1, 0, 2), Bm.transpose(1, 0, 2), Cm.transpose(1, 0, 2))
            _, ys = jax.lax.scan(step, h0, xs)
            return ys.transpose(1, 0, 2)

        def ssm_direction(u, x_proj_w, dt_w, dt_b, A_log, D_skip):
            proj = u @ x_proj_w
            dt = jax.nn.softplus(proj[..., :DT_RANK] @ dt_w + dt_b)
            Bm = proj[..., DT_RANK:DT_RANK + D_STATE]
            Cm = proj[..., DT_RANK + D_STATE:]
            A = -jnp.exp(A_log)
            y = selective_scan(u, dt, A, Bm, Cm)
            return y + u * D_skip
        key = jax.random.key(seed)
        ks = jax.random.split(key, 12)
        s = 0.02
        R2N = DT_RANK + 2 * D_STATE
        return {'x': jax.random.normal(ks[0], (BSZ, SEQ, D_MODEL), jnp.float32), 'gamma_in': jnp.ones((D_MODEL,), jnp.float32), 'beta_in': jnp.zeros((D_MODEL,), jnp.float32), 'W_in': jax.random.normal(ks[1], (D_MODEL, 2 * D_INNER), jnp.float32) * s, 'conv_w': jax.random.normal(ks[2], (D_INNER, D_CONV), jnp.float32) * 0.3, 'conv_b': jnp.zeros((D_INNER,), jnp.float32), 'x_proj_w': jax.random.normal(ks[3], (2, D_INNER, R2N), jnp.float32) * s, 'dt_w': jax.random.normal(ks[4], (2, DT_RANK, D_INNER), jnp.float32) * s, 'dt_b': jax.random.normal(ks[5], (2, D_INNER), jnp.float32) * 0.1 - 4.0, 'A_log': jnp.log(jnp.broadcast_to(jnp.arange(1, D_STATE + 1, dtype=jnp.float32), (2, D_INNER, D_STATE))), 'D_skip': jnp.ones((2, D_INNER), jnp.float32), 'merge_w': jnp.full((2,), 0.5, jnp.float32), 'gamma_out': jnp.ones((D_INNER,), jnp.float32), 'beta_out': jnp.zeros((D_INNER,), jnp.float32), 'W_out': jax.random.normal(ks[6], (D_INNER, D_MODEL), jnp.float32) * s}
    _L0_attn_all = _L0_attn_setup()
    _L0_attn_in = {k: v for k, v in _L0_attn_all.items() if k in ('gamma_in', 'beta_in', 'W_in', 'conv_w', 'conv_b', 'x_proj_w', 'dt_w', 'dt_b', 'A_log', 'D_skip', 'merge_w', 'gamma_out', 'beta_out', 'W_out')}
    del _L0_attn_all

    def _L0_ffn_setup():
        import jax, jax.numpy as jnp
        import numpy as np
        B, T, C, H, E, TOPK, DR = (2, 512, 192, 768, 8, 2, 24)

        def _normalize(v, axis=-1, eps=1e-12):
            return v / jnp.maximum(jnp.linalg.norm(v, axis=axis, keepdims=True), eps)
        key = jax.random.key(seed)
        ks = jax.random.split(key, 16)
        std = 0.02
        n = lambda k, shape, s=std: (s * jax.random.normal(k, shape)).astype(jnp.float32)
        emb = jax.random.normal(ks[3], (E, DR), dtype=jnp.float32)
        emb = emb / (jnp.linalg.norm(emb, axis=-1, keepdims=True) + 1e-08)
        return {'x': jax.random.normal(ks[0], (B, T, C), dtype=jnp.float32), 'router_w': n(ks[1], (E, C)), 'probe_w': n(ks[2], (DR, C)), 'router_emb': emb, 'fatigue': jnp.zeros((E,), jnp.float32), 'energy': jnp.ones((E,), jnp.float32), 'w_fast1': n(ks[4], (E, C, H)), 'w_slow1': n(ks[5], (E, C, H)), 'h_fast1': n(ks[6], (E, C, H), 0.005), 'm_gate1': jax.random.uniform(ks[7], (E,), dtype=jnp.float32), 'b1': jnp.zeros((E, H), jnp.float32), 'w_fast2': n(ks[8], (E, H, C)), 'w_slow2': n(ks[9], (E, H, C)), 'h_fast2': n(ks[10], (E, H, C), 0.005), 'm_gate2': jax.random.uniform(ks[11], (E,), dtype=jnp.float32), 'b2': jnp.zeros((E, C), jnp.float32)}
    _L0_ffn_all = _L0_ffn_setup()
    _L0_ffn_in = {k: v for k, v in _L0_ffn_all.items() if k in ('router_w', 'probe_w', 'router_emb', 'fatigue', 'energy', 'w_fast1', 'w_slow1', 'h_fast1', 'm_gate1', 'b1', 'w_fast2', 'w_slow2', 'h_fast2', 'm_gate2', 'b2')}
    del _L0_ffn_all
    return {'x': x, 'L0_tok_emb_table': _L0_tok_in['emb_table'], 'L0_tok_spos0': _L0_tok_in['spos0'], 'L0_tok_spos1': _L0_tok_in['spos1'], 'L0_attn_gamma_in': _L0_attn_in['gamma_in'], 'L0_attn_beta_in': _L0_attn_in['beta_in'], 'L0_attn_W_in': _L0_attn_in['W_in'], 'L0_attn_conv_w': _L0_attn_in['conv_w'], 'L0_attn_conv_b': _L0_attn_in['conv_b'], 'L0_attn_x_proj_w': _L0_attn_in['x_proj_w'], 'L0_attn_dt_w': _L0_attn_in['dt_w'], 'L0_attn_dt_b': _L0_attn_in['dt_b'], 'L0_attn_A_log': _L0_attn_in['A_log'], 'L0_attn_D_skip': _L0_attn_in['D_skip'], 'L0_attn_merge_w': _L0_attn_in['merge_w'], 'L0_attn_gamma_out': _L0_attn_in['gamma_out'], 'L0_attn_beta_out': _L0_attn_in['beta_out'], 'L0_attn_W_out': _L0_attn_in['W_out'], 'L0_ffn_router_w': _L0_ffn_in['router_w'], 'L0_ffn_probe_w': _L0_ffn_in['probe_w'], 'L0_ffn_router_emb': _L0_ffn_in['router_emb'], 'L0_ffn_fatigue': _L0_ffn_in['fatigue'], 'L0_ffn_energy': _L0_ffn_in['energy'], 'L0_ffn_w_fast1': _L0_ffn_in['w_fast1'], 'L0_ffn_w_slow1': _L0_ffn_in['w_slow1'], 'L0_ffn_h_fast1': _L0_ffn_in['h_fast1'], 'L0_ffn_m_gate1': _L0_ffn_in['m_gate1'], 'L0_ffn_b1': _L0_ffn_in['b1'], 'L0_ffn_w_fast2': _L0_ffn_in['w_fast2'], 'L0_ffn_w_slow2': _L0_ffn_in['w_slow2'], 'L0_ffn_h_fast2': _L0_ffn_in['h_fast2'], 'L0_ffn_m_gate2': _L0_ffn_in['m_gate2'], 'L0_ffn_b2': _L0_ffn_in['b2']}

def reference(x, L0_tok_emb_table, L0_tok_spos0, L0_tok_spos1, L0_attn_gamma_in, L0_attn_beta_in, L0_attn_W_in, L0_attn_conv_w, L0_attn_conv_b, L0_attn_x_proj_w, L0_attn_dt_w, L0_attn_dt_b, L0_attn_A_log, L0_attn_D_skip, L0_attn_merge_w, L0_attn_gamma_out, L0_attn_beta_out, L0_attn_W_out, L0_ffn_router_w, L0_ffn_probe_w, L0_ffn_router_emb, L0_ffn_fatigue, L0_ffn_energy, L0_ffn_w_fast1, L0_ffn_w_slow1, L0_ffn_h_fast1, L0_ffn_m_gate1, L0_ffn_b1, L0_ffn_w_fast2, L0_ffn_w_slow2, L0_ffn_h_fast2, L0_ffn_m_gate2, L0_ffn_b2):
    import jax
    import jax.numpy as jnp

    def _L0_tok_ref(tokens, emb_table, spos0, spos1):
        import jax, jax.numpy as jnp
        import numpy as np
        VOCAB = 50257
        EMBED_DIM = 192
        N_SUBPOS = 3
        REPEAT = 2
        SUB_DIM = EMBED_DIM // (REPEAT + 1)

        def positional_encoding(max_len, d_model):
            depth = d_model // 2
            positions = jnp.arange(max_len, dtype=jnp.float32)[:, None]
            depths = (jnp.arange(depth, dtype=jnp.float32) / depth)[None, :]
            angle_rates = 1.0 / 10000.0 ** depths
            angle_rads = positions * angle_rates
            return jnp.concatenate([jnp.sin(angle_rads), jnp.cos(angle_rads)], axis=-1)
        emb = emb_table[tokens]
        parts = [emb]
        for i, spos in enumerate((spos0, spos1)):
            sel = jax.nn.softmax(emb[..., i * N_SUBPOS:(i + 1) * N_SUBPOS], axis=-1)
            parts.append(jnp.einsum('bsk,kd->bsd', sel, spos))
        x = jnp.concatenate(parts, axis=-1)
        seq_len = tokens.shape[1]
        x = x * jnp.sqrt(jnp.float32(EMBED_DIM)) + positional_encoding(seq_len, EMBED_DIM)
        return x

    def _L0_attn_ref(x, gamma_in, beta_in, W_in, conv_w, conv_b, x_proj_w, dt_w, dt_b, A_log, D_skip, merge_w, gamma_out, beta_out, W_out):
        import jax, jax.numpy as jnp
        import numpy as np
        BSZ, SEQ, D_MODEL = (2, 512, 192)
        EXPAND, D_STATE, D_CONV = (2, 16, 3)
        D_INNER = EXPAND * D_MODEL
        DT_RANK = (D_MODEL + 15) // 16
        EPS = 1e-05

        def layernorm(x, g, b):
            mu = jnp.mean(x, axis=-1, keepdims=True)
            var = jnp.mean((x - mu) ** 2, axis=-1, keepdims=True)
            return (x - mu) * jax.lax.rsqrt(var + EPS) * g + b

        def depthwise_conv1d(x, w, b):
            K = w.shape[1]
            pad = (K - 1) // 2
            L = x.shape[1]
            xp = jnp.pad(x, ((0, 0), (pad, pad), (0, 0)))
            y = sum((xp[:, k:k + L, :] * w[:, k] for k in range(K)))
            return y + b

        def selective_scan(u, delta, A, Bm, Cm):

            def step(h, xs):
                d_t, u_t, B_t, C_t = xs
                dA = jnp.exp(d_t[..., None] * A)
                h = dA * h + (d_t * u_t)[..., None] * B_t[:, None, :]
                y = jnp.einsum('bdn,bn->bd', h, C_t)
                return (h, y)
            B_, L_, d_ = u.shape
            h0 = jnp.zeros((B_, d_, A.shape[1]), u.dtype)
            xs = (delta.transpose(1, 0, 2), u.transpose(1, 0, 2), Bm.transpose(1, 0, 2), Cm.transpose(1, 0, 2))
            _, ys = jax.lax.scan(step, h0, xs)
            return ys.transpose(1, 0, 2)

        def ssm_direction(u, x_proj_w, dt_w, dt_b, A_log, D_skip):
            proj = u @ x_proj_w
            dt = jax.nn.softplus(proj[..., :DT_RANK] @ dt_w + dt_b)
            Bm = proj[..., DT_RANK:DT_RANK + D_STATE]
            Cm = proj[..., DT_RANK + D_STATE:]
            A = -jnp.exp(A_log)
            y = selective_scan(u, dt, A, Bm, Cm)
            return y + u * D_skip
        residual = x
        xz = layernorm(x, gamma_in, beta_in) @ W_in
        xi, z = jnp.split(xz, 2, axis=-1)
        u = jax.nn.silu(depthwise_conv1d(xi, conv_w, conv_b))
        y_f = ssm_direction(u, x_proj_w[0], dt_w[0], dt_b[0], A_log[0], D_skip[0])
        u_r = jnp.flip(u, axis=1)
        y_b = jnp.flip(ssm_direction(u_r, x_proj_w[1], dt_w[1], dt_b[1], A_log[1], D_skip[1]), axis=1)
        y = merge_w[0] * y_f + merge_w[1] * y_b
        y = layernorm(y, gamma_out, beta_out) * jax.nn.silu(z)
        out = y @ W_out + residual
        return out

    def _L0_ffn_ref(x, router_w, probe_w, router_emb, fatigue, energy, w_fast1, w_slow1, h_fast1, m_gate1, b1, w_fast2, w_slow2, h_fast2, m_gate2, b2):
        import jax, jax.numpy as jnp
        import numpy as np
        B, T, C, H, E, TOPK, DR = (2, 512, 192, 768, 8, 2, 24)

        def _normalize(v, axis=-1, eps=1e-12):
            return v / jnp.maximum(jnp.linalg.norm(v, axis=axis, keepdims=True), eps)
        Bd, Td, Cd = x.shape
        logits = jnp.einsum('btc,ec->bte', x, router_w)
        tok_proxy = x.mean(axis=-1, keepdims=True)
        router_gain = jnp.linalg.norm(router_emb, axis=-1)
        base_bias = 0.02 * tok_proxy
        gain_bias = 0.02 * tok_proxy * router_gain
        tok_unit = _normalize(jnp.einsum('btc,dc->btd', x, probe_w))
        align_bias = 0.02 * jnp.einsum('btd,ed->bte', tok_unit, _normalize(router_emb))
        logits = logits + base_bias + gain_bias + align_bias + 0.1 * energy - 0.1 * fatigue
        g, idx = jax.lax.top_k(logits, TOPK)
        gates = jax.nn.softmax(g, axis=-1)
        N = Bd * Td
        gates_full = jnp.zeros((N, E), x.dtype).at[jnp.arange(N)[:, None], idx.reshape(N, TOPK)].set(gates.reshape(N, TOPK))
        flat_x = x.reshape(N, Cd)

        def body(acc, p):
            wf1, ws1, hf1, mg1, bb1, wf2, ws2, hf2, mg2, bb2, ge = p
            W1 = wf1 + mg1 * ws1 + hf1
            h = jnp.square(jnp.maximum(flat_x @ W1 + bb1, 0.0))
            W2 = wf2 + mg2 * ws2 + hf2
            y = h @ W2 + bb2
            return (acc + ge[:, None] * y, None)
        out, _ = jax.lax.scan(body, jnp.zeros((N, Cd), x.dtype), (w_fast1, w_slow1, h_fast1, m_gate1, b1, w_fast2, w_slow2, h_fast2, m_gate2, b2, gates_full.T))
        return out.reshape(Bd, Td, Cd)
    h = _L0_tok_ref(x, L0_tok_emb_table, L0_tok_spos0, L0_tok_spos1)
    h = h + _L0_attn_ref(_layernorm(h, axis=-1), L0_attn_gamma_in, L0_attn_beta_in, L0_attn_W_in, L0_attn_conv_w, L0_attn_conv_b, L0_attn_x_proj_w, L0_attn_dt_w, L0_attn_dt_b, L0_attn_A_log, L0_attn_D_skip, L0_attn_merge_w, L0_attn_gamma_out, L0_attn_beta_out, L0_attn_W_out)
    h = h + _L0_ffn_ref(_layernorm(h, axis=-1), L0_ffn_router_w, L0_ffn_probe_w, L0_ffn_router_emb, L0_ffn_fatigue, L0_ffn_energy, L0_ffn_w_fast1, L0_ffn_w_slow1, L0_ffn_h_fast1, L0_ffn_m_gate1, L0_ffn_b1, L0_ffn_w_fast2, L0_ffn_w_slow2, L0_ffn_h_fast2, L0_ffn_m_gate2, L0_ffn_b2)
    return h

_drawn_inputs = setup_inputs


def setup_inputs(seed=0):
    import zlib

    import numpy as np

    out = dict(_drawn_inputs(seed))
    spreads = {'L0_attn_gamma_in': (1.0, 0.6),
     'L0_attn_beta_in': (0.0, 0.8),
     'L0_attn_conv_b': (0.0, 0.366),
     'L0_attn_D_skip': (1.0, 0.6),
     'L0_attn_merge_w': (0.5, 0.6),
     'L0_attn_gamma_out': (1.0, 0.6),
     'L0_attn_beta_out': (0.0, 0.8),
     'L0_ffn_fatigue': (0.0, 0.754),
     'L0_ffn_energy': (1.0, 0.6),
     'L0_ffn_b1': (0.0, 0.655),
     'L0_ffn_b2': (0.0, 0.8)}
    factors = {'L0_attn_x_proj_w': 64.0,
     'L0_attn_dt_w': 64.0,
     'L0_attn_dt_b': 64.0,
     'L0_attn_A_log': 8.0,
     'L0_ffn_probe_w': 8.0,
     'L0_ffn_router_emb': 8.0,
     'L0_ffn_w_slow1': 4.651,
     'L0_ffn_h_fast1': 6.709,
     'L0_ffn_m_gate1': 8.0,
     'L0_ffn_w_slow2': 3.35,
     'L0_ffn_h_fast2': 7.755,
     'L0_ffn_m_gate2': 7.515}
    for name, (base, spread) in spreads.items():
        noise = np.random.default_rng([zlib.crc32(name.encode()), seed]).standard_normal(out[name].shape)
        drawn = base * np.exp(spread * noise) if base else spread * noise
        out[name] = jnp.asarray(drawn.astype(out[name].dtype))
    for name, factor in factors.items():
        out[name] = (out[name] * factor).astype(out[name].dtype)
    return out
```

```python
import concourse.bass as bass
from concourse import mybir
from contextlib import ExitStack

FP32 = mybir.dt.float32
BF16 = mybir.dt.bfloat16
I32 = mybir.dt.int32
U32 = mybir.dt.uint32
ALU = mybir.AluOpType
ACT = mybir.ActivationFunctionType
AX = mybir.AxisListType

P = 128
BATCH, SEQ = 8, 256
TOK = BATCH * SEQ
TILES = TOK // P
SUB = 64
NPOS = 3
C = 192
KT, KC = 2, C // 2
DI = 384
DB = DI // P
NS = 16
RANK = 12
GT = 512
NG = TOK // GT
TG = GT // P
SG = GT // SEQ
NQ, QN = 4, 4
E, H = 8, 768
HB = H // P
DR = 24
RC = E + DR + 1 + E
EPS = 1e-5
CH_CONV, CH_CB, CH_DTB, CH_ALOG, CH_D = 0, 3, 4, 6, 38
CH = 40
PER_QUAD = 2 * DB


class Steps:

    def __init__(self, eng, sem, base=0):
        self.eng, self.sem, self.base, self.n = eng, sem, base, 0

    def __call__(self, ins):
        ins.then_inc(self.sem, 1)
        self.n += 1

    def wait(self):
        self.eng.wait_ge(self.sem, self.base + self.n)

    def then(self, ins):
        self(ins)
        self.wait()


def build(nc, tok, emb, spos, pos, chan, w_in, gb_in, xproj, dt_w, gb_out, w_out, merge, w_route, emb_t,
          energy, fatigue, gates12, b1, b2, wf1, ws1, hf1, wf2, ws2, hf2, out):
    ctx = ExitStack()
    with ctx:
        def sb(name, shape, dt=FP32):
            return ctx.enter_context(nc.sbuf_tensor(name, shape, dt))

        def sem(name):
            return ctx.enter_context(nc.semaphore(name))

        tok_sb = sb("tok_sb", [P, TILES], I32)
        ident = sb("ident", [P, P])
        pick = sb("pick", [96, 32], BF16)
        pos_sb = sb("pos_sb", [P, 2, C])
        spos_sb = sb("spos_sb", [P, 2, NPOS, SUB])
        chan_sb = sb("chan_sb", [P, DB, CH])
        neg_a = sb("neg_a", [P, DB, 2, NS])
        d_merged = sb("d_merged", [P, DB])
        w_in_sb = sb("w_in_sb", [KC, KT, 2 * DI])
        gb_in_sb = sb("gb_in_sb", [KC, KT, 2])
        w_low = sb("w_low", [P, DB, 64])
        w_bc = sb("w_bc", [P, 2, DB, 96])
        dt_w_sb = sb("dt_w_sb", [64, DI])
        gb_out_sb = sb("gb_out_sb", [P, 2, DI])
        w_out_sb = sb("w_out_sb", [P, DB, C])
        merge_sb = sb("merge_sb", [P, 2])
        w_route_sb = sb("w_route_sb", [KC, KT, RC])
        w_probe = sb("w_probe", [DR, C])
        emb_t_sb = sb("emb_t_sb", [DR, E])
        energy_sb = sb("energy_sb", [P, E])
        fatigue_sb = sb("fatigue_sb", [P, E])
        mg_sb = sb("mg_sb", [P, 2, E])
        b1_sb = sb("b1_sb", [P, E, HB])
        b2_sb = sb("b2_sb", [E, C])

        ln_in = sb("ln_in", [P, TILES, C])
        resid = sb("resid", [P, TILES, C])
        stats = sb("stats", [P, TILES, 6])
        mv = sb("mv", [P, TILES, 2])
        rs = sb("rs", [P, TILES])
        mv2 = sb("mv2", [P, TILES, 2])
        rs2 = sb("rs2", [P, TILES])
        eps_sb = sb("eps_sb", [P, 1])
        nt1 = sb("nt1", [P, TILES])
        nt2 = sb("nt2", [P, TILES])
        x_t = sb("x_t", [KC, KT, TOK])
        routed = sb("routed", [P, TILES, RC])

        ARENA = 32512
        arena = sb("arena", [P, ARENA])
        used = [0]

        def cut(shape, dt=FP32, parts=P):
            n = 1
            for s in shape:
                n *= s
            words = n if dt != BF16 else n // 2
            v = arena[0:parts, used[0]:used[0] + words]
            used[0] += words
            assert used[0] <= ARENA, used[0]
            if dt != FP32:
                v = v.bitcast(dt)
            if len(shape) == 2:
                v = v.rearrange("p (a b) -> p a b", b=shape[1])
            if len(shape) == 3:
                v = v.rearrange("p (a b c) -> p a b c", b=shape[1], c=shape[2])
            if len(shape) == 4:
                v = v.rearrange("p (a b c d) -> p a b c d", b=shape[1], c=shape[2], d=shape[3])
            return v

        rows = cut([TILES, SUB])
        sel_d = cut([TILES, 2, NPOS])
        sel_e = cut([TILES, 2, NPOS])
        sel_w = cut([TILES, 2, NPOS])
        sel_m = cut([TILES, 2])
        sel_s = cut([TILES, 2])
        sel_r = cut([TILES, 2])
        mix = [cut([TILES, SUB]) for _ in range(2)]
        used[0] = 0
        xn = cut([TG, C])
        xn_t = cut([KT, GT], parts=KC)
        sz = cut([TG, DI])
        u = cut([DB, GT])
        bc_split = [cut([GT], BF16, parts=96) for _ in range(2)]
        dt_sb = [cut([DB, GT]) for _ in range(2)]
        dtu = [cut([DB, GT]) for _ in range(2)]
        ud = cut([DB, GT])
        b_bc = [cut([QN, GT]) for _ in range(2)]
        decay = [[cut([QN, GT]) for _ in range(2)] for _ in range(2)]
        state = [cut([QN, GT]) for _ in range(DB)]
        conv = state[2][:, 0:DB, :]
        low = decay[0][0][0:64, 3, :]
        bc_rest = decay[0][1][0:96, 3, :]
        bc_hi = decay[1][0][0:96, 3, 0:GT // 2].bitcast(BF16)
        bc_mid = decay[1][0][0:96, 3, GT // 2:GT].bitcast(BF16)
        sp_abs = [state[0][:, 0:3, :], state[1][:, 0:3, :]]
        sp_pos = [decay[0][0][:, 0:3, :], decay[0][1][:, 0:3, :]]
        sp_e = [decay[1][0][:, 0:3, :], decay[1][1][:, 0:3, :]]
        sp_w = [b_bc[0][:, 0:3, :], b_bc[1][:, 0:3, :]]
        sp_l = sp_abs
        y_n = ud.rearrange("p a b -> p (a b)").rearrange("p (t d) -> p t d", d=DI)
        y_t = conv
        x_g = xn
        x_g_t = xn_t
        used[0] = 0
        raw1 = [[cut([KT, H], parts=KC) for _ in range(3)] for _ in range(2)]
        raw2 = [[cut([HB, C]) for _ in range(3)] for _ in range(2)]
        w1 = [cut([KT, H], parts=KC) for _ in range(2)]
        w2 = [cut([HB, C]) for _ in range(2)]
        h_pos = [cut([GT]) for _ in range(2)]
        h_sq = [cut([HB, GT]) for _ in range(2)]

        gate_t = cut([TOK], parts=E)

        rt = {n: sb("rt_" + n, [P, TILES, E]) for n in ("a", "b", "logit", "top", "hot0", "hot1", "gate")}
        rt_sq = sb("rt_sq", [P, TILES, DR])
        rt_1 = {n: sb("rt1_" + n, [P, TILES]) for n in ("n2", "n", "m", "r", "tp", "d", "e", "s", "g0", "g1")}
        rt_i = sb("rt_i", [P, TILES, E], U32)
        rt_f = sb("rt_f", [P, TILES, E])
        iota_e = sb("iota_e", [P, E])
        iota_i = sb("iota_i", [P, E], I32)
        gain = sb("gain", [P, E])
        gain_r = sb("gain_r", [P, E])
        gain_p = sb("gain_p", [P, E])
        gain_1 = sb("gain_1", [P, E])
        bias_e = sb("bias_e", [P, E])
        emb_sq = sb("emb_sq", [DR, E])
        ones = sb("ones", [DR, P])

        ps = ctx.enter_context(nc.psum_tensor("ps", [P, 8, 512], FP32))
        Y, BCAST, BB = 0, 3, 7
        y_ps = ps[:, Y:Y + DB, :].rearrange("p a b -> p (a b)")
        y_ps_t = y_ps.rearrange("p (t d) -> p t d", d=DI)

        s_tok = sem("tokens_loaded")
        s_front = sem("front_loaded")
        s_par = sem("params_loaded")
        s_rows = sem("rows_gathered")
        s_ident = sem("ident_ready")
        s_setup_v = sem("setup_vector")
        v_step = sem("vector_step")
        a_step = sem("scalar_step")
        p_step = sem("pool_step")
        s_sel_d = sem("select_logits_ready")
        s_sel_e = sem("select_exp_ready")
        s_sel_w = sem("select_weights_ready")
        s_cp = sem("row_copied")
        s_mix1 = sem("second_mix_ready")
        s_ln = sem("variance_ready")
        s_rstd = sem("rstd_ready")
        s_lnin = sem("ln_in_ready")
        s_res = sem("resid_ready")
        s_nega = sem("decay_rate_exp_ready")
        s_xn = sem("xn_ready")
        s_xn_ps = sem("xn_transposed")
        s_xn_t = sem("xn_t_ready")
        s_xi = sem("xi_ready")
        s_z = sem("z_ready")
        s_sz = sem("sz_ready")
        s_conv = sem("conv_ready")
        s_u = sem("u_ready")
        s_low_ps = sem("low_rank_product")
        s_low = sem("low_ready")
        s_bc_ps = sem("bc_product")
        s_split = sem("bc_split_ready")
        s_dt_ps = sem("dt_product")
        s_pos = sem("softplus_pos_ready")
        s_e = sem("softplus_exp_ready")
        s_c = sem("softplus_corr_ready")
        s_rc = sem("softplus_pos_corrected")
        s_l = sem("softplus_log_ready")
        s_x = sem("dtu_ready")
        s_ud = sem("ud_ready")
        s_b_ps = sem("b_broadcast_product")
        s_b = sem("b_broadcast_ready")
        s_c_ps = sem("c_broadcast_ready")
        s_decay = sem("decay_ready")
        s_in = sem("scan_input_ready")
        s_scan = sem("scan_done")
        s_mul = sem("c_multiplied")
        s_sum = sem("y_summed")
        s_yn = sem("y_normed")
        s_yt_ps = sem("y_transposed")
        s_yt = sem("y_t_ready")
        s_o_ps = sem("out_product")
        s_xg = sem("x_g_ready")
        s_xg_ps = sem("x_g_transposed")
        s_xg_t = sem("x_g_t_ready")
        s_r_ps = sem("router_product")
        s_r = sem("router_sums_kept")
        s_group = sem("group_done")
        s_nrm = sem("norms_summed")
        s_nrm_r = sem("norms_rooted")
        s_gd = sem("gate_difference_ready")
        s_ge = sem("gate_exp_ready")
        s_gate = sem("gates_ready")
        s_gt_ps = sem("gates_transposed")
        s_gt = sem("gates_t_ready")
        s_gb = sem("gated_b2_product")
        s_acc = sem("accumulator_started")
        s_raw = [sem("raw_weights_loaded_0"), sem("raw_weights_loaded_1")]
        s_w = sem("weights_ready")
        s_h_ps = sem("hidden_product")
        s_hr = sem("hidden_relu")
        s_h = sem("hidden_ready")
        s_o2 = sem("expert_product")
        s_added = sem("expert_added")
        s_esq = sem("embedding_squared")
        s_rset = sem("router_setup_product")
        s_wr = sem("router_weights_ready")
        s_wtmp = sem("weights_half_combined")
        s_h1 = sem("weights_first_combined")
        s_store = sem("stored")
        s_passed = sem("waits_passed")
        FRONT_LOADS, PAR_LOADS = 2, 24
        DT_BANKS = ((0, 1, 2), (5, 6, 7))

        def alone(eng):
            eng.sem_inc(s_passed, 1)

        block = ctx.enter_context(nc.Block())

        @block.sync
        def _(sp):
            sp.dma_start(tok_sb[:], tok).then_inc(s_tok, 16)
            sp.dma_start(spos_sb[:].rearrange("p a b c -> p (a b c)"), spos.to_broadcast([P, 2 * NPOS * SUB])).then_inc(s_front, 16)
            sp.dma_start(pos_sb[:], pos).then_inc(s_front, 16)
            n = 0

            def load(dst, src):
                sp.dma_start(dst, src).then_inc(s_par, 16)

            sp.wait_ge(s_setup_v, 1)
            loads = [(chan_sb[:], chan), (w_in_sb[:], w_in), (gb_in_sb[:], gb_in),
                     (dt_w_sb[0:RANK, :], dt_w[0]), (dt_w_sb[32:32 + RANK, :], dt_w[1]),
                     (merge_sb[:], merge.to_broadcast([P, 2])), (w_out_sb[:], w_out),
                     (gb_out_sb[:].rearrange("p a b -> p (a b)"), gb_out.to_broadcast([P, 2 * DI]))]
            for d in range(2):
                loads.append((w_low[:, :, 32 * d:32 * d + RANK], xproj[:, d, :, 0:RANK]))
                for r in range(3):
                    loads.append((w_bc[:, d, :, 32 * r:32 * r + 2 * NS], xproj[:, d, :, RANK:RANK + 2 * NS]))
            loads += [(w_route_sb[:, :, 0:E + DR], w_route), (emb_t_sb[:], emb_t[0:DR, 0:E]), (w_probe[:], emb_t[0:DR, E:E + C]),
                      (energy_sb[:], energy.to_broadcast([P, E])), (fatigue_sb[:], fatigue.to_broadcast([P, E])),
                      (mg_sb[:].rearrange("p a b -> p (a b)"), gates12.to_broadcast([P, 2 * E])),
                      (b1_sb[:], b1), (b2_sb[:], b2)]
            for dst, src in loads:
                load(dst, src)
                n += 1
            assert n == PAR_LOADS, n
            sp.wait_ge(s_group, NG)
            sp.wait_ge(s_r, NG)

            def load_expert(e, half):
                for k, (a, b) in enumerate(((wf1, wf2), (ws1, ws2), (hf1, hf2))):
                    sp.dma_start(raw1[half][k], a[bass.ds(e, 1), :, :, :].rearrange("e p a b -> (e p) a b")).then_inc(s_raw[half], 16)
                    sp.dma_start(raw2[half][k], b[bass.ds(e, 1), :, :, :].rearrange("e p a b -> (e p) a b")).then_inc(s_raw[half], 16)
            load_expert(0, 0)
            load_expert(1, 1)
            with sp.Fori(1, E // 2) as pair:
                for half in range(2):
                    sp.wait_ge(s_w, 2 * pair + half - 1)
                    load_expert(2 * pair + half, half)
            sp.wait_ge(s_added, 4 * E)
            sp.dma_start(out.rearrange("(t p) c -> p t c", p=P), resid[:]).then_inc(s_store, 16)
            sp.wait_ge(s_store, 16)

        @block.gpsimd
        def _(pool):
            g_ = nc.gpsimd
            st = Steps(pool, p_step)
            pool.wait_ge(s_tok, 16)
            for t in range(TILES):
                g_.indirect_dma_start(out=rows[:, t, :], out_offset=None, in_=emb,
                                      in_offset=bass.IndirectOffsetOnAxis(ap=tok_sb[:, t:t + 1].bitcast(U32), axis=0)).then_inc(s_rows, 16)
            st(g_.memset(ident[:], 0.0))
            st(g_.memset(pick[:], 0.0))
            st.wait()
            g_.affine_select(out=ident[:], in_=ident[:], compare_op=ALU.not_equal, fill=1.0, base=0,
                             pattern=[[-1, P]], channel_multiplier=1).then_inc(s_ident, 1)
            for r in range(3):
                st.then(g_.affine_select(out=pick[:], in_=pick[:], compare_op=ALU.not_equal, fill=1.0, base=-32 * r,
                                         pattern=[[-1, 32]], channel_multiplier=1))
            g_.iota(iota_i[:], pattern=[[1, E]], base=0, channel_multiplier=0).then_inc(s_ident, 1)
            pool.wait_ge(s_sel_w, 1)
            pool.wait_ge(s_front, 16 * FRONT_LOADS)
            dst = ln_in[:, :, 2 * SUB:3 * SUB]
            for k in range(NPOS):
                o = dst if k == 0 else mix[1]
                st.then(g_.tensor_tensor(o, spos_sb[:, 1:2, k, :].to_broadcast([P, TILES, SUB]),
                                         sel_w[:, :, 1, k:k + 1].to_broadcast([P, TILES, SUB]), ALU.mult))
                if k:
                    ins = g_.tensor_tensor(dst, dst, mix[1], ALU.add)
                    if k == NPOS - 1:
                        ins.then_inc(s_mix1, 1)
                    else:
                        st.then(ins)
            pool.wait_ge(s_lnin, 1)
            g_.tensor_tensor(resid[:], resid[:], ln_in[:], ALU.add).then_inc(s_res, 1)
            POOL_BASE = st.n
            pool.sem_inc(s_in, PER_QUAD)
            with pool.Fori(0, NG) as g:
                for d in range(2):
                    pool.wait_ge(s_c, 2 * g + d + 1)
                    g_.tensor_tensor(sp_pos[d], sp_pos[d], sp_w[d], ALU.subtract).then_inc(s_rc, 1)
                pool.wait_ge(s_x, 2 * g + 2)
                alone(pool)

                def items(G):
                    for k in range(PER_QUAD):
                        d, blk = divmod(k, DB)
                        if blk == 0:
                            pool.wait_ge(s_b, 8 * G + 4 * d + 4)
                        pool.wait_ge(s_sum, PER_QUAD * G + k + 1)
                        g_.tensor_tensor(state[blk], dtu[d][:, blk:blk + 1, :].to_broadcast([P, QN, GT]),
                                         b_bc[d], ALU.mult).then_inc(s_in, 1)
                with pool.Fori(0, NQ) as q:
                    items(g * NQ + q)

        @block.vector
        def _(dve):
            v = nc.vector
            st = Steps(dve, v_step)
            v.memset(w_low[:], 0.0)
            v.memset(w_route_sb[:, :, E + DR:E + DR + 1], 1.0)
            v.memset(eps_sb[:], EPS)
            v.memset(ones[:], 1.0).then_inc(s_setup_v, 1)
            dve.wait_ge(s_rows, 16 * TILES)
            six = rows[:, :, 0:2 * NPOS].rearrange("p t (i k) -> p t i k", k=NPOS)
            st.then(v.tensor_reduce(sel_m, six, AX.X, ALU.max))
            v.tensor_tensor(sel_d, six, sel_m.unsqueeze(3).to_broadcast([P, TILES, 2, NPOS]), ALU.subtract).then_inc(s_sel_d, 1)
            dve.wait_ge(s_sel_e, 1)
            st.then(v.tensor_reduce(sel_s, sel_e, AX.X, ALU.add))
            st.then(v.reciprocal(sel_r, sel_s))
            v.tensor_tensor(sel_w, sel_e, sel_r.unsqueeze(3).to_broadcast([P, TILES, 2, NPOS]), ALU.mult).then_inc(s_sel_w, 1)
            dve.wait_ge(s_sel_w, 1)
            dve.wait_ge(s_front, 16 * FRONT_LOADS)
            dst = ln_in[:, :, SUB:2 * SUB]
            for k in range(NPOS):
                o = dst if k == 0 else mix[0]
                st.then(v.tensor_tensor(o, spos_sb[:, 0:1, k, :].to_broadcast([P, TILES, SUB]),
                                        sel_w[:, :, 0, k:k + 1].to_broadcast([P, TILES, SUB]), ALU.mult))
                if k:
                    st.then(v.tensor_tensor(dst, dst, mix[0], ALU.add))
            dve.wait_ge(s_cp, 1)
            dve.wait_ge(s_mix1, 1)
            st.then(v.scalar_tensor_tensor(
                resid[:].rearrange("p (b t) c -> p b (t c)", t=2), ln_in[:].rearrange("p (b t) c -> p b (t c)", t=2),
                float(C) ** 0.5, pos_sb[:].rearrange("p t c -> p (t c)").unsqueeze(1).to_broadcast([P, BATCH, 2 * C]),
                ALU.mult, ALU.add))

            def moments(src, t0, n, done):
                for t in range(n):
                    st(v.bn_stats(stats[:, t0 + t, :], src(t)))
                st.wait()
                for t in range(n):
                    last = v.bn_aggr(mv[:, t0 + t, :], stats[:, t0 + t, :])
                last.then_inc(s_ln, 1)

            def newton(t0, n):
                var, r, a, b = mv[:, t0:t0 + n, 1], rs[:, t0:t0 + n], nt1[:, t0:t0 + n], nt2[:, t0:t0 + n]
                st.then(v.tensor_tensor(a, r, r, ALU.mult))
                st.then(v.scalar_tensor_tensor(b, var, EPS, a, ALU.add, ALU.mult))
                st.then(v.tensor_scalar(a, b, -0.5, 1.5, ALU.mult, ALU.add))
                st.then(v.tensor_tensor(r, r, a, ALU.mult))

            moments(lambda t: resid[:, t, :], 0, TILES, s_ln)
            dve.wait_ge(s_rstd, 1)
            newton(0, TILES)
            for t in range(TILES):
                last = v.tensor_scalar(ln_in[:, t, :], resid[:, t, :], mv[:, t, 0:1], rs[:, t:t + 1], ALU.subtract, ALU.mult)
            last.then_inc(s_lnin, 1)
            dve.wait_ge(s_lnin, 1)
            moments(lambda t: ln_in[:, t, :], 0, TILES, s_ln)
            dve.wait_ge(s_rstd, 2)
            newton(0, TILES)
            dve.wait_ge(s_par, 16 * (PAR_LOADS))
            dve.wait_ge(s_nega, 1)
            st(v.tensor_scalar(neg_a[:], neg_a[:], -1.0, None, ALU.mult))
            st.then(v.tensor_scalar(d_merged[:], chan_sb[:, :, CH_D], merge_sb[:, 0:1], None, ALU.mult))
            st(v.scalar_tensor_tensor(d_merged[:], chan_sb[:, :, CH_D + 1], merge_sb[:, 1:2], d_merged[:], ALU.mult, ALU.add))
            dve.wait_ge(s_res, 1)
            st.wait()
            v.tensor_tensor(emb_sq[:], emb_t_sb[:], emb_t_sb[:], ALU.mult).then_inc(s_esq, 1)
            dve.wait_ge(s_rset, 1)
            st(v.tensor_copy(gain_1[:], ps[:, 7, 0:E]))
            v.tensor_copy(w_route_sb[:, :, E + DR + 1:RC], ps[0:KC, 5:5 + KT, 0:E]).then_inc(s_wr, 1)
            st(v.tensor_copy(mv2[:], mv[:]))
            st.then(v.tensor_copy(rs2[:], rs[:]))
            base_setup = st.n
            PER = 49
            dve.sem_inc(s_scan, PER_QUAD)
            with dve.Fori(0, NG) as g:
                st = Steps(dve, v_step, base_setup + g * PER)
                for t in range(TG):
                    i = g * TG + t
                    last = v.tensor_scalar(xn[:, t, :], ln_in[:, bass.ds(i, 1), :].rearrange("p a c -> p (a c)"),
                                           mv2[:, bass.ds(i, 1), 0:1].rearrange("p a c -> p (a c)"), rs2[:, bass.ds(i, 1)],
                                           ALU.subtract, ALU.mult)
                last.then_inc(s_xn, 1)
                for blk in range(DB):
                    dve.wait_ge(s_xi, DB * g + blk + 1)
                    cv = conv[:, blk, :].rearrange("p (s t) -> p s t", t=SEQ)
                    xi = ps[:, blk, :].rearrange("p (s t) -> p s t", t=SEQ)
                    st.then(v.tensor_scalar(conv[:, blk, :], ps[:, blk, :], chan_sb[:, blk, 1:2], chan_sb[:, blk, CH_CB:CH_CB + 1],
                                            ALU.mult, ALU.add))
                    st.then(v.scalar_tensor_tensor(cv[:, :, 1:SEQ], xi[:, :, 0:SEQ - 1], chan_sb[:, blk, 0:1],
                                                   cv[:, :, 1:SEQ], ALU.mult, ALU.add))
                    last = v.scalar_tensor_tensor(cv[:, :, 0:SEQ - 1], xi[:, :, 1:SEQ], chan_sb[:, blk, 2:3],
                                                  cv[:, :, 0:SEQ - 1], ALU.mult, ALU.add)
                    last.then_inc(s_conv, 1)
                for d in range(2):
                    bank = ps[0:96, 3 + d, :]
                    dve.wait_ge(s_bc_ps, 2 * g + d + 1)
                    if d:
                        st.wait()
                    st(v.tensor_copy(bc_split[d][0:32, :], bank[0:32, :]))
                    st.then(v.tensor_copy(bc_hi, bank))
                    st.then(v.tensor_tensor(bc_rest, bank, bc_hi, ALU.subtract))
                    st(v.tensor_copy(bc_split[d][32:64, :], bc_rest[32:64, :]))
                    st.then(v.tensor_copy(bc_mid[64:96, :], bc_rest[64:96, :]))
                    last = v.tensor_tensor(bc_split[d][64:96, :], bc_rest[64:96, :], bc_mid[64:96, :], ALU.subtract)
                    last.then_inc(s_split, 1)
                    dve.wait_ge(s_split, 2 * g + d + 1)
                for d in range(2):
                    dve.wait_ge(s_e, 2 * g + d + 1)
                    st.then(v.tensor_scalar(sp_w[d], sp_e[d], 1.0, None, ALU.add))
                    v.scalar_tensor_tensor(sp_w[d], sp_w[d], -1.0, sp_e[d], ALU.add, ALU.subtract).then_inc(s_c, 1)
                for blk in range(DB):
                    last = v.tensor_scalar(ud[:, blk, :], u[:, blk, :], d_merged[:, blk:blk + 1], None, ALU.mult)
                last.then_inc(s_ud, 1)
                for d in range(2):
                    dve.wait_ge(s_l, 2 * g + d + 1)
                    dve.wait_ge(s_rc, 2 * g + d + 1)
                    st.then(v.tensor_tensor(dt_sb[d], sp_pos[d], sp_l[d], ALU.add))
                    v.tensor_tensor(dtu[d], dt_sb[d], u, ALU.mult).then_inc(s_x, 1)
                dve.wait_ge(s_x, 2 * g + 2)
                for d in range(2):
                    for b in range(2):
                        first = decay[d][b].rearrange("p n (s t) -> p n s t", t=SEQ)[:, :, :, 0 if d == 0 else SEQ - 1]
                        last = v.memset(first, 0.0)
                        st(last)
                st.wait()
                alone(dve)

                def scan(k, G):
                    d, blk = divmod(k, DB)
                    i = PER_QUAD * G + k
                    dve.wait_ge(s_decay, i + 1)
                    dve.wait_ge(s_in, i + 1 + PER_QUAD)
                    a, x = (m.rearrange("p n t -> p (n t)") for m in (decay[d][blk % 2], state[blk]))
                    if d:
                        a, x = a[:, ::-1], x[:, ::-1]
                    v.tensor_tensor_scan(x, a, x, 0.0, ALU.mult, ALU.add).then_inc(s_scan, 1)

                def times_c(k, G):
                    d, blk = divmod(k, DB)
                    i = PER_QUAD * G + k
                    dve.wait_ge(s_scan, i + 1 + PER_QUAD)
                    if blk == 0:
                        dve.wait_ge(s_c_ps, 2 * G + d + 1)
                    v.tensor_tensor(state[blk], state[blk], ps[:, BCAST:BCAST + QN, :], ALU.mult).then_inc(s_mul, 1)

                with dve.Fori(0, NQ) as q:
                    G = g * NQ + q
                    scan(0, G)
                    for k in range(1, PER_QUAD):
                        scan(k, G)
                        times_c(k - 1, G)
                    times_c(PER_QUAD - 1, G)

                dve.wait_ge(s_sum, 3 + NQ * PER_QUAD * (g + 1))
                alone(dve)
                for t in range(TG):
                    st(v.bn_stats(stats[:, t, :], y_ps_t[:, t, :]))
                st.wait()
                alone(dve)
                for t in range(TG):
                    last = v.bn_aggr(mv[:, t, :], stats[:, t, :])
                last.then_inc(s_ln, 1)
                dve.wait_ge(s_ln, 2 + 2 * g + 1)
                for t in range(TG):
                    st(v.scalar_tensor_tensor(y_n[:, t, :], y_ps_t[:, t, :], mv[:, t, 0:1], gb_out_sb[:, 0, :],
                                              ALU.subtract, ALU.mult))
                dve.wait_ge(s_rstd, 2 + 2 * g + 1)
                st.wait()
                newton(0, TG)
                for t in range(TG):
                    st(v.scalar_tensor_tensor(y_n[:, t, :], y_n[:, t, :], rs[:, t:t + 1], gb_out_sb[:, 1, :],
                                              ALU.mult, ALU.add))
                dve.wait_ge(s_sz, g + 1)
                st.wait()
                v.tensor_tensor(y_n, y_n, sz, ALU.mult).then_inc(s_yn, 1)
                dve.wait_ge(s_o_ps, g + 1)
                res_g = resid[:, bass.ds(g * TG, TG), :]
                st(v.tensor_tensor(res_g, res_g, ps[:, 3:3 + TG, 0:C], ALU.add))
                st.wait()
                alone(dve)
                for t in range(TG):
                    st(v.bn_stats(stats[:, t, :], resid[:, bass.ds(g * TG + t, 1), :].rearrange("p a c -> p (a c)")))
                st.wait()
                alone(dve)
                for t in range(TG):
                    last = v.bn_aggr(mv[:, t, :], stats[:, t, :])
                last.then_inc(s_ln, 1)
                dve.wait_ge(s_rstd, 2 + 2 * g + 2)
                newton(0, TG)
                for t in range(TG):
                    last = v.tensor_scalar(x_g[:, t, :], resid[:, bass.ds(g * TG + t, 1), :].rearrange("p a c -> p (a c)"),
                                           mv[:, t, 0:1], rs[:, t:t + 1], ALU.subtract, ALU.mult)
                last.then_inc(s_xg, 1)
                dve.wait_ge(s_xg_t, g + 1)
                v.tensor_copy(x_t[:, :, bass.ds(g * GT, GT)], x_g_t).then_inc(s_group, 1)
                dve.wait_ge(s_group, g + 1)
                assert st.n == PER, st.n
            st = Steps(dve, v_step, base_setup + NG * PER)

            dve.wait_ge(s_r, NG)
            dve.wait_ge(s_nrm, 1)
            st(v.tensor_reduce(rt_1["n2"][:], rt_sq[:], AX.X, ALU.add))
            dve.wait_ge(s_ident, 2)
            st.wait()
            v.tensor_copy(iota_e[:], iota_i[:]).then_inc(s_nrm_r, 1)
            dve.wait_ge(s_nrm_r, 3)
            st(v.tensor_scalar(rt_1["m"][:], rt_1["n"][:], 1e-12, None, ALU.max))
            st(v.tensor_scalar(gain_r[:], gain[:], 1e-12, None, ALU.max))
            st.wait()
            st(v.reciprocal(rt_1["r"][:], rt_1["m"][:]))
            st(v.reciprocal(gain_1[:], gain_r[:]))
            st(v.tensor_scalar(rt_1["tp"][:], routed[:, :, E + DR], 0.02 / C, None, ALU.mult))
            st(v.tensor_scalar(gain_p[:], gain[:], 1.0, None, ALU.add))
            st(v.tensor_tensor(bias_e[:], energy_sb[:], fatigue_sb[:], ALU.subtract))
            st.wait()

            def by_tile(m):
                return m[:].unsqueeze(2).to_broadcast([P, TILES, E])

            def by_expert(m):
                return m[:].unsqueeze(1).to_broadcast([P, TILES, E])
            st(v.tensor_tensor(rt["a"][:], by_tile(rt_1["tp"]), by_expert(gain_p), ALU.mult))
            st(v.tensor_tensor(rt["b"][:], by_tile(rt_1["r"]), by_expert(gain_1), ALU.mult))
            st.wait()
            st(v.tensor_tensor(rt["a"][:], rt["a"][:], routed[:, :, 0:E], ALU.add))
            st(v.tensor_tensor(rt["b"][:], rt["b"][:], routed[:, :, E + DR + 1:RC], ALU.mult))
            st.wait()
            st.then(v.scalar_tensor_tensor(rt["a"][:], rt["b"][:], 0.02, rt["a"][:], ALU.mult, ALU.add))
            st.then(v.scalar_tensor_tensor(rt["logit"][:], by_expert(bias_e), 0.1, rt["a"][:], ALU.mult, ALU.add))
            for t in range(TILES):
                st(v.max(rt["top"][:, t, :], rt["logit"][:, t, :]))
            st.wait()
            for t in range(TILES):
                st(v.max_index(rt_i[:, t, :], rt["top"][:, t, :], rt["logit"][:, t, :]))
            v.tensor_tensor(rt_1["d"][:], rt["top"][:, :, 1], rt["top"][:, :, 0], ALU.subtract).then_inc(s_gd, 1)
            st.wait()
            st.then(v.tensor_copy(rt_f[:], rt_i[:]))
            st(v.tensor_tensor(rt["hot0"][:], by_expert(iota_e), rt_f[:, :, 0:1].to_broadcast([P, TILES, E]), ALU.is_equal))
            st(v.tensor_tensor(rt["hot1"][:], by_expert(iota_e), rt_f[:, :, 1:2].to_broadcast([P, TILES, E]), ALU.is_equal))
            dve.wait_ge(s_ge, 1)
            st.then(v.tensor_scalar(rt_1["s"][:], rt_1["e"][:], 1.0, None, ALU.add))
            st.then(v.reciprocal(rt_1["g0"][:], rt_1["s"][:]))
            st(v.tensor_tensor(rt_1["g1"][:], rt_1["g0"][:], rt_1["e"][:], ALU.mult))
            st.wait()
            st(v.tensor_tensor(rt["hot0"][:], rt["hot0"][:], by_tile(rt_1["g0"]), ALU.mult))
            st(v.tensor_tensor(rt["hot1"][:], rt["hot1"][:], by_tile(rt_1["g1"]), ALU.mult))
            st.wait()
            v.tensor_tensor(rt["gate"][:], rt["hot0"][:], rt["hot1"][:], ALU.add).then_inc(s_gate, 1)
            for part in range(4):
                dve.wait_ge(s_gb, part + 1)
                res_g = resid[:, TG * part:TG * part + TG, :]
                v.tensor_tensor(res_g, res_g, ps[:, 4:4 + TG, 0:C], ALU.add).then_inc(s_acc, 1)
            dve.wait_ge(s_acc, 4)

            def combine(e, half, nth):
                dve.wait_ge(s_raw[half], 96 * nth)
                mg1 = mg_sb[0:KC, 0, bass.ds(e, 1)]
                mg2 = mg_sb[:, 1, bass.ds(e, 1)]
                f1, s1, h1 = (m.rearrange("p a b -> p (a b)") for m in raw1[half])
                f2, s2, h2 = (m.rearrange("p a b -> p (a b)") for m in raw2[half])
                v.scalar_tensor_tensor(s1, s1, mg1, f1, ALU.mult, ALU.add).then_inc(s_wtmp, 1)
                v.scalar_tensor_tensor(s2, s2, mg2, f2, ALU.mult, ALU.add).then_inc(s_wtmp, 1)
                dve.wait_ge(s_wtmp, 2 * e + 2)
                v.tensor_tensor(w1[half].rearrange("p a b -> p (a b)"), s1, h1, ALU.add).then_inc(s_h1, 1)
                v.tensor_tensor(w2[half].rearrange("p a b -> p (a b)"), s2, h2, ALU.add).then_inc(s_w, 1)

            def add_expert(e):
                with dve.Fori(0, NG) as g:
                    G = e * NG + g
                    dve.wait_ge(s_o2, G + 1)
                    dve.wait_ge(s_added, G)
                    for t in range(TG):
                        i = g * TG + t
                        r = resid[:, bass.ds(i, 1), :].rearrange("p a c -> p (a c)")
                        gt = rt["gate"][:, bass.ds(i, 1), bass.ds(e, 1)].rearrange("p a c -> p (a c)")
                        last = v.scalar_tensor_tensor(r, ps[:, 4 + t, 0:C], gt, r, ALU.mult, ALU.add)
                    last.then_inc(s_added, 1)

            combine(0, 0, 1)
            with dve.Fori(0, E // 2 - 1) as pair:
                combine(2 * pair + 1, 1, pair + 1)
                add_expert(2 * pair)
                combine(2 * pair + 2, 0, pair + 2)
                add_expert(2 * pair + 1)
            combine(E - 1, 1, E // 2)
            add_expert(E - 2)
            add_expert(E - 1)

        @block.scalar
        def _(act):
            a = nc.scalar
            a.preload_act_table_set("natural_log_exp_and_others")
            act.wait_ge(s_sel_d, 1)
            a.activation(sel_e, sel_d, ACT.Exp).then_inc(s_sel_e, 1)
            a.activation(ln_in[:, :, 0:SUB], rows, ACT.Copy).then_inc(s_cp, 1)
            st = Steps(act, a_step)

            def rstd(t0, n, k):
                act.wait_ge(s_ln, k)
                st.then(a.activation(nt2[:, t0:t0 + n], mv[:, t0:t0 + n, 1], ACT.Ln, bias=eps_sb[:]))
                a.activation(rs[:, t0:t0 + n], nt2[:, t0:t0 + n], ACT.Exp, scale=-0.5).then_inc(s_rstd, 1)

            act.wait_ge(s_setup_v, 1)
            rstd(0, TILES, 1)
            rstd(0, TILES, 2)
            act.wait_ge(s_par, 16 * (PAR_LOADS))
            a.activation(neg_a[:], chan_sb[:, :, CH_ALOG:CH_ALOG + 2 * NS].rearrange("p b (d n) -> p b d n", n=NS), ACT.Exp).then_inc(s_nega, 1)
            base_setup = st.n
            PER = 8
            with act.Fori(0, NG) as g:
                st = Steps(act, a_step, base_setup + g * PER)
                act.wait_ge(s_xn_ps, g + 1)
                for k in range(KT):
                    a.activation(xn_t[:, k, :], ps[0:KC, 3 + k, :], ACT.Identity, scale=gb_in_sb[:, k, 0:1],
                                 bias=gb_in_sb[:, k, 1:2]).then_inc(s_xn_t, 1)
                act.wait_ge(s_z, g + 1)
                a.activation(sz, ps[:, 3:3 + TG, 0:DI], ACT.Silu).then_inc(s_sz, 1)
                for blk in range(DB):
                    act.wait_ge(s_conv, DB * g + blk + 1)
                    a.activation(u[:, blk, :], conv[:, blk, :], ACT.Silu).then_inc(s_u, 1)
                act.wait_ge(s_low_ps, g + 1)
                a.activation(low, ps[0:64, BB, :], ACT.Copy).then_inc(s_low, 1)
                a.preload_act_table_set("natural_log_exp_and_others")
                for d in range(2):
                    for blk in range(DB):
                        act.wait_ge(s_dt_ps, 2 * DB * g + DB * d + blk + 1)
                        bias = chan_sb[:, blk, CH_DTB + d:CH_DTB + d + 1]
                        bank = ps[:, DT_BANKS[d][blk], :]
                        st(a.activation(sp_abs[d][:, blk, :], bank, ACT.Abs, bias=bias))
                        a.activation(sp_pos[d][:, blk, :], bank, ACT.Relu, bias=bias).then_inc(s_pos, 1)
                    st.wait()
                    a.activation(sp_e[d], sp_abs[d], ACT.Exp, scale=-1.0).then_inc(s_e, 1)
                for d in range(2):
                    act.wait_ge(s_e, 2 * g + d + 1)
                    a.activation(sp_l[d], sp_e[d], ACT.Ln, bias=1.0).then_inc(s_l, 1)
                act.wait_ge(s_x, 2 * g + 2)

                def exps(k, q):
                    d, blk = divmod(k, DB)
                    G = g * NQ + q
                    act.wait_ge(s_scan, PER_QUAD * G + k + PER_QUAD + (-3, -5, -1)[blk])
                    out_b = decay[d][blk % 2].rearrange("p n (s t) -> p n s t", t=SEQ)
                    src = dt_sb[d][:, blk, :].rearrange("p (s t) -> p s t", t=SEQ)
                    lo, hi = (1, SEQ) if d == 0 else (0, SEQ - 1)
                    for n in range(QN):
                        scale = neg_a[:, blk, d, bass.ds(q * QN + n, 1)]
                        last = a.activation(out_b[:, n, :, lo:hi], src[:, :, lo:hi], ACT.Exp, scale=scale)
                    last.then_inc(s_decay, 1)

                def b_copy(stage, d):
                    act.wait_ge(s_in, DB * stage + DB)
                    for n in range(QN):
                        act.wait_ge(s_b_ps, 4 * stage + n + 1)
                        a.activation(b_bc[d][:, n, :], ps[:, BB, :], ACT.Copy, scale=merge_sb[:, d:d + 1]).then_inc(s_b, 1)

                def quad(q, last):
                    G = g * NQ + q
                    for k in range(4):
                        exps(k, q)
                    if not last:
                        b_copy(2 * G + 2, 0)
                    exps(4, q)
                    exps(5, q)
                    if not last:
                        b_copy(2 * G + 3, 1)
                b_copy(2 * g * NQ, 0)
                b_copy(2 * g * NQ + 1, 1)
                with act.Fori(0, NQ - 1) as q:
                    quad(q, False)
                quad(NQ - 1, True)
                rstd(0, TG, 2 + 2 * g + 1)
                act.wait_ge(s_yt_ps, g + 1)
                a.activation(y_t, ps[:, 3:3 + DB, :], ACT.Copy).then_inc(s_yt, 1)
                rstd(0, TG, 2 + 2 * g + 2)
                act.wait_ge(s_xg_ps, g + 1)
                a.activation(x_g_t, ps[0:KC, 0:KT, :], ACT.Copy).then_inc(s_xg_t, 1)
                act.wait_ge(s_r_ps, g + 1)
                a.activation(routed[:, bass.ds(g * TG, TG), :],
                             ps[:, 2, :].rearrange("p (t c) -> p t c", t=TG)[:, :, 0:RC], ACT.Copy).then_inc(s_r, 1)
                act.wait_ge(s_group, g + 1)
                assert st.n == PER, st.n
            act.wait_ge(s_r, NG)
            a.activation(rt_sq[:], routed[:, :, E:E + DR], ACT.Square).then_inc(s_nrm, 1)
            act.wait_ge(s_nrm_r, 1)
            a.activation(rt_1["n"][:], rt_1["n2"][:], ACT.Sqrt).then_inc(s_nrm_r, 1)
            a.activation(gain[:], gain_1[:], ACT.Sqrt).then_inc(s_nrm_r, 1)
            act.wait_ge(s_gd, 1)
            a.activation(rt_1["e"][:], rt_1["d"][:], ACT.Exp).then_inc(s_ge, 1)
            for part in range(4):
                act.wait_ge(s_gt_ps, part + 1)
                a.activation(gate_t[:, GT * part:GT * (part + 1)], ps[0:E, part, :], ACT.Copy).then_inc(s_gt, 1)
            with act.Fori(0, E) as e:
                with act.Fori(0, NG) as g:
                    G = e * NG + g
                    for j in range(HB):
                        n = HB * G + j
                        act.wait_ge(s_h_ps, n + 1)
                        if j == 0:
                            act.wait_ge(s_o2, G)
                            act.wait_ge(s_h, HB * G)
                        if j >= 2:
                            act.wait_ge(s_h, n - 1)
                        bias = b1_sb[:, bass.ds(e, 1), j:j + 1].rearrange("p a c -> p (a c)")
                        a.activation(h_pos[j % 2], ps[:, j % 4, :], ACT.Relu, bias=bias).then_inc(s_hr, 1)
                        act.wait_ge(s_hr, n + 1)
                        a.activation(h_sq[0][:, j, :], h_pos[j % 2], ACT.Square).then_inc(s_h, 1)

        @block.tensor
        def _(pe):
            t_ = nc.tensor
            mm = t_.matmul

            def transpose(o, src, parts, start=True):
                return mm(o, src, ident[0:parts, 0:parts], start=start, stop=True, is_transpose=True, skip_group_check=True)

            pe.wait_ge(s_ident, 1)
            pe.wait_ge(s_par, 16 * (PAR_LOADS))
            pe.wait_ge(s_esq, 1)
            mm(ps[:, 7, 0:E], ones[:], emb_sq[:], start=True, stop=True)
            for k in range(KT):
                last = mm(ps[0:KC, 5 + k, 0:E], w_probe[:, KC * k:KC * k + KC], emb_t_sb[:], start=True, stop=True)
            last.then_inc(s_rset, 1)
            pe.wait_ge(s_wr, 1)
            pe.sem_inc(s_sum, 3)
            with pe.Fori(0, NG) as g:
                pe.wait_ge(s_group, g)
                pe.wait_ge(s_r, g)
                pe.wait_ge(s_xn, g + 1)
                for t in range(TG):
                    for k in range(KT):
                        last = transpose(ps[0:KC, 3 + k, P * t:P * t + P], xn[:, t, KC * k:KC * k + KC], P)
                last.then_inc(s_xn_ps, 1)
                pe.wait_ge(s_xn_t, KT * (g + 1))
                for blk in range(DB):
                    for k in range(KT):
                        last = mm(ps[:, blk, :], w_in_sb[:, k, P * blk:P * blk + P], xn_t[:, k, :], start=k == 0, stop=k == KT - 1)
                    last.then_inc(s_xi, 1)
                for t in range(TG):
                    for k in range(KT):
                        last = mm(ps[:, 3 + t, 0:DI], xn_t[:, k, P * t:P * t + P], w_in_sb[:, k, DI:2 * DI], start=k == 0, stop=k == KT - 1)
                last.then_inc(s_z, 1)
                pe.wait_ge(s_u, DB * (g + 1))
                for blk in range(DB):
                    last = mm(ps[0:64, BB, :], w_low[:, blk, :], u[:, blk, :], start=blk == 0, stop=blk == DB - 1)
                last.then_inc(s_low_ps, 1)
                pe.wait_ge(s_sz, g + 1)
                for d in range(2):
                    for blk in range(DB):
                        last = mm(ps[0:96, 3 + d, :], w_bc[:, d, blk, :], u[:, blk, :], start=blk == 0, stop=blk == DB - 1)
                    last.then_inc(s_bc_ps, 1)
                pe.wait_ge(s_low, g + 1)
                for d in range(2):
                    for blk in range(DB):
                        last = mm(ps[:, DT_BANKS[d][blk], :], dt_w_sb[32 * d:32 * d + RANK, P * blk:P * blk + P],
                                  low[32 * d:32 * d + RANK, :], start=True, stop=True)
                        last.then_inc(s_dt_ps, 1)
                pe.wait_ge(s_ud, g + 1)
                pe.wait_ge(s_pos, 2 * DB * (g + 1))
                for t in range(TG):
                    for blk in range(DB):
                        c = t * DB + blk
                        transpose(y_ps[:, P * c:P * c + P], ud[:, blk, P * t:P * t + P], P, start=c % 4 == 0)

                pe.wait_ge(s_split, 2 * g + 2)

                def b_rows(q, d):
                    G = g * NQ + q
                    for n in range(QN):
                        i = 8 * G + 4 * d + n
                        pe.wait_ge(s_b, i)
                        mm(ps[:, BB, :], pick[:, bass.ds(q * QN + n, 1)].to_broadcast([96, P]), bc_split[d],
                           start=True, stop=True).then_inc(s_b_ps, 1)

                def c_rows(q, d):
                    G = g * NQ + q
                    pe.wait_ge(s_mul, DB * (2 * G + d))
                    for n in range(QN):
                        last = mm(ps[:, BCAST + n, :], pick[:, bass.ds(q * QN + n + NS, 1)].to_broadcast([96, P]), bc_split[d],
                                  start=True, stop=True)
                    last.then_inc(s_c_ps, 1)

                def add(i, blk):
                    pe.wait_ge(s_mul, i + 1)
                    for n in range(QN):
                        for t in range(TG):
                            c = t * DB + blk
                            last = transpose(y_ps[:, P * c:P * c + P], state[blk][:, n, P * t:P * t + P], P, start=False)
                    last.then_inc(s_sum, 1)

                def quad(q, first, final):
                    G = g * NQ + q
                    i = PER_QUAD * G
                    c_rows(q, 0)
                    if not first:
                        add(i - 1, 2)
                    add(i, 0)
                    if not final:
                        b_rows(q + 1, 0)
                    add(i + 1, 1)
                    c_rows(q, 1)
                    add(i + 2, 2)
                    add(i + 3, 0)
                    if not final:
                        b_rows(q + 1, 1)
                    add(i + 4, 1)
                b_rows(0, 0)
                b_rows(0, 1)
                quad(0, True, False)
                with pe.Fori(1, NQ - 1) as q:
                    quad(q, False, False)
                quad(NQ - 1, False, True)
                add(PER_QUAD * NQ * (g + 1) - 1, 2)
                pe.wait_ge(s_yn, g + 1)
                for t in range(TG):
                    for blk in range(DB):
                        last = transpose(ps[:, 3 + blk, P * t:P * t + P], y_n[:, t, P * blk:P * blk + P], P)
                last.then_inc(s_yt_ps, 1)
                pe.wait_ge(s_yt, g + 1)
                for t in range(TG):
                    for blk in range(DB):
                        last = mm(ps[:, 3 + t, 0:C], y_t[:, blk, P * t:P * t + P], w_out_sb[:, blk, :], start=blk == 0, stop=blk == DB - 1)
                last.then_inc(s_o_ps, 1)
                pe.wait_ge(s_xg, g + 1)
                for t in range(TG):
                    for k in range(KT):
                        last = transpose(ps[0:KC, k, P * t:P * t + P], x_g[:, t, KC * k:KC * k + KC], P)
                last.then_inc(s_xg_ps, 1)
                pe.wait_ge(s_xg_t, g + 1)
                for t in range(TG):
                    for k in range(KT):
                        last = mm(ps[:, 2, P * t:P * t + RC], x_g_t[:, k, P * t:P * t + P], w_route_sb[:, k, :], start=k == 0, stop=k == KT - 1)
                last.then_inc(s_r_ps, 1)
            pe.wait_ge(s_gate, 1)
            for part in range(4):
                for t in range(TG):
                    last = transpose(ps[0:E, part, P * t:P * t + P], rt["gate"][:, TG * part + t, :], P)
                last.then_inc(s_gt_ps, 1)
            for part in range(4):
                pe.wait_ge(s_gt, part + 1)
                if part:
                    pe.wait_ge(s_acc, part)
                for t in range(TG):
                    i = TG * part + t
                    last = mm(ps[:, 4 + t, 0:C], gate_t[:, P * i:P * i + P], b2_sb[:], start=True, stop=True)
                last.then_inc(s_gb, 1)
            pe.wait_ge(s_acc, 4)
            with pe.Fori(0, E // 2) as pair:
                for half in range(2):
                    e = 2 * pair + half
                    pe.wait_ge(s_w, e + 1)
                    alone(pe)
                    with pe.Fori(0, NG) as g:
                        G = e * NG + g
                        for j in range(HB):
                            n = HB * G + j
                            if j >= 4:
                                pe.wait_ge(s_hr, n - 3)
                            else:
                                pe.wait_ge(s_hr, HB * G)
                            for k in range(KT):
                                last = mm(ps[:, j % 4, :], w1[half][:, k, P * j:P * j + P], x_t[:, k, bass.ds(g * GT, GT)],
                                          start=k == 0, stop=k == KT - 1)
                            last.then_inc(s_h_ps, 1)
                        pe.wait_ge(s_added, G)
                        pe.wait_ge(s_h, HB * (G + 1))
                        for t in range(TG):
                            for j in range(HB):
                                last = mm(ps[:, 4 + t, 0:C], h_sq[0][:, j, P * t:P * t + P], w2[half][:, j, :],
                                          start=j == 0, stop=j == HB - 1)
                        last.then_inc(s_o2, 1)


def _positions():
    import numpy as np
    depth = C // 2
    depths = (np.arange(depth, dtype=np.float32) / np.float32(depth))[None, :]
    rates = (np.float32(1.0) / np.power(np.float32(10000.0), depths)).astype(np.float32)
    rad = np.arange(SEQ, dtype=np.float32)[:, None] * rates
    table = np.concatenate([np.sin(rad), np.cos(rad)], axis=-1).astype(np.float32)
    return np.ascontiguousarray(table.reshape(SEQ // P, P, C).transpose(1, 0, 2))


def kernel(**inputs):
    import numpy as np
    import concourse.bacc as bacc
    from concourse.bass_utils import run_bass_kernel_spmd

    a = {k.replace("L0_", ""): np.asarray(v) for k, v in inputs.items()}

    def per_channel(m, blocks):
        return m.reshape((blocks, m.shape[0] // blocks) + m.shape[1:]).swapaxes(0, 1)

    def per_expert(m, blocks):
        return m.reshape(E, blocks, m.shape[1] // blocks, m.shape[2]).transpose(0, 2, 1, 3)

    chan = np.concatenate([a["attn_conv_w"], a["attn_conv_b"][:, None], a["attn_dt_b"].T,
                           a["attn_A_log"].transpose(1, 0, 2).reshape(DI, 2 * NS), a["attn_D_skip"].T], axis=1)
    arrays = {
        "tok": a["x"].reshape(TILES, P).T,
        "emb": a["tok_emb_table"],
        "spos": np.stack([a["tok_spos0"], a["tok_spos1"]]).reshape(1, -1),
        "pos": _positions(),
        "chan": per_channel(chan, DB),
        "w_in": per_channel(a["attn_W_in"], KT),
        "gb_in": per_channel(np.stack([a["attn_gamma_in"], a["attn_beta_in"]], axis=1), KT),
        "xproj": a["attn_x_proj_w"].reshape(2, DB, P, RANK + 2 * NS).transpose(2, 0, 1, 3),
        "dt_w": a["attn_dt_w"],
        "gb_out": np.concatenate([a["attn_gamma_out"], a["attn_beta_out"]]).reshape(1, -1),
        "w_out": per_channel(a["attn_W_out"], DB),
        "merge": a["attn_merge_w"].reshape(1, 2),
        "w_route": per_channel(np.concatenate([a["ffn_router_w"].T, a["ffn_probe_w"].T], axis=1), KT),
        "emb_t": np.concatenate([a["ffn_router_emb"].T, a["ffn_probe_w"]], axis=1),
        "energy": a["ffn_energy"].reshape(1, E),
        "fatigue": a["ffn_fatigue"].reshape(1, E),
        "gates12": np.concatenate([a["ffn_m_gate1"], a["ffn_m_gate2"]]).reshape(1, 2 * E),
        "b1": a["ffn_b1"].reshape(E, HB, P).transpose(2, 0, 1),
        "b2": a["ffn_b2"],
        "wf1": per_expert(a["ffn_w_fast1"], KT),
        "ws1": per_expert(a["ffn_w_slow1"], KT),
        "hf1": per_expert(a["ffn_h_fast1"], KT),
        "wf2": per_expert(a["ffn_w_fast2"], HB),
        "ws2": per_expert(a["ffn_w_slow2"], HB),
        "hf2": per_expert(a["ffn_h_fast2"], HB),
    }
    arrays = {k: np.ascontiguousarray(m) for k, m in arrays.items()}
    nc = bacc.Bacc("TRN2", target_bir_lowering=False, num_devices=1)
    aps = {k: nc.dram_tensor(k, m.shape, mybir.dt.from_np(m.dtype), kind="ExternalInput").ap() for k, m in arrays.items()}
    out = nc.dram_tensor("out", (TOK, C), FP32, kind="ExternalOutput").ap()
    build(nc, out=out, **aps)
    r = run_bass_kernel_spmd(nc, [arrays], core_ids=[0])
    return r.results[0]["out"].reshape(BATCH, SEQ, C)
```

```python
import concourse.bass as bass
from concourse import mybir
from contextlib import ExitStack

FP32 = mybir.dt.float32
BF16 = mybir.dt.bfloat16
I32 = mybir.dt.int32
U32 = mybir.dt.uint32
ALU = mybir.AluOpType
ACT = mybir.ActivationFunctionType
AX = mybir.AxisListType

P = 128
BATCH, SEQ = 8, 256
TOK = BATCH * SEQ
TILES = TOK // P
SUB = 64
NPOS = 3
C = 192
KT, KC = 2, C // 2
DI = 384
DB = DI // P
NS = 16
RANK = 12
GT = 512
NG = TOK // GT
TG = GT // P
SG = GT // SEQ
NQ, QN = 4, 4
E, H = 8, 768
HB = H // P
HT = TILES // 2
SP = 3
DR = 24
RC = E + DR + 1 + E
EPS = 1e-5
CH_CONV, CH_CB, CH_DTB, CH_ALOG, CH_D = 0, 3, 4, 6, 38
CH = 40
SHIFT = P.bit_length() - 1
PER_QUAD = 2 * DB
TOP = 2
SLOTS = (TOP * TOK - E) // P + E
BATCHES = (0, 2, 8, 16, 24, 32, SLOTS)
HH = H // 2
GATE_W = 2 * TG * DI


class Steps:

    def __init__(self, eng, sem, base=0):
        self.eng, self.sem, self.base, self.n = eng, sem, base, 0

    def __call__(self, ins):
        ins.then_inc(self.sem, 1)
        self.n += 1

    def wait(self):
        self.eng.wait_ge(self.sem, self.base + self.n)

    def then(self, ins):
        self(ins)
        self.wait()


def build(nc, tok, emb, spos, pos, chan, w_in, gb_in, xproj, dt_w, gb_out, w_out, merge, w_route, emb_t,
          energy, fatigue, gates12, b1, b2, wf1, ws1, hf1, wf2, ws2, hf2, gates_dram, b_rows, x_rows, y_rows, out):
    ctx = ExitStack()
    with ctx:
        def sb(name, shape, dt=FP32):
            return ctx.enter_context(nc.sbuf_tensor(name, shape, dt))

        def sem(name):
            return ctx.enter_context(nc.semaphore(name))

        tok_sb = sb("tok_sb", [P, TILES], I32)
        ident = sb("ident", [P, P])
        pick = sb("pick", [96, 32], BF16)
        chan_sb = sb("chan_sb", [P, DB, CH])
        neg_a = sb("neg_a", [P, DB, 2, NS])
        d_merged = sb("d_merged", [P, DB])
        skip = sb("skip", [P, DB, P])
        gb_in_sb = sb("gb_in_sb", [KC, KT, 2])
        merge_sb = sb("merge_sb", [P, 2])
        w_route_sb = sb("w_route_sb", [KC, KT, RC])
        emb_t_sb = sb("emb_t_sb", [DR, E])
        energy_sb = sb("energy_sb", [P, E])
        fatigue_sb = sb("fatigue_sb", [P, E])
        mg_sb = sb("mg_sb", [P, 2, E])
        b2_sb = sb("b2_sb", [E, C])
        eps_sb = sb("eps_sb", [P, 1])
        ones = sb("ones", [P, P])
        iota_e = sb("iota_e", [P, E])
        iota_i = sb("iota_i", [P, E], I32)
        iota_p = sb("iota_p", [P, P])
        iota_pi = sb("iota_pi", [P, P], I32)
        before = sb("before", [P, P])
        row_ii = sb("row_ii", [P, TOP, TILES], I32)
        row_lo_i = sb("row_lo_i", [P, TOP, TILES], I32)
        row_lo = sb("row_lo", [P, TOP, TILES])
        row_id = sb("row_id", [P, TOP, TILES])
        row_hi = sb("row_hi", [P, TOP, TILES])
        spare = sb("spare", [P, SLOTS])
        spare_i = sb("spare_i", [P, SLOTS], I32)

        ln_in = sb("ln_in", [P, TILES, C])
        ln_flat = ln_in[:].rearrange("p a b -> p (a b)")
        resid = sb("resid", [P, TILES, C])
        stats = sb("stats", [P, TILES, 6])
        mv = sb("mv", [P, TILES, 2])
        rs = sb("rs", [P, TILES])
        mv2 = sb("mv2", [P, TILES, 2])
        rs2 = sb("rs2", [P, TILES])
        nt1 = sb("nt1", [P, TILES])
        nt2 = sb("nt2", [P, TILES])
        gain = sb("gain", [P, E])
        gain_r = sb("gain_r", [P, E])
        gain_p = sb("gain_p", [P, E])
        gain_1 = sb("gain_1", [P, E])
        bias_e = sb("bias_e", [P, E])
        emb_sq = sb("emb_sq", [DR, E])

        ARENA = 41984
        arena = sb("arena", [P, ARENA])
        used = [0]

        def cut(shape, dt=FP32, parts=P):
            n = 1
            for s in shape:
                n *= s
            words = n if dt != BF16 else n // 2
            assert used[0] + words <= ARENA, used[0]
            v = arena[0:parts, used[0]:used[0] + words]
            used[0] += words
            if dt != FP32:
                v = v.bitcast(dt)
            if len(shape) == 2:
                v = v.rearrange("p (a b) -> p a b", b=shape[1])
            if len(shape) == 3:
                v = v.rearrange("p (a b c) -> p a b c", b=shape[1], c=shape[2])
            if len(shape) == 4:
                v = v.rearrange("p (a b c d) -> p a b c d", b=shape[1], c=shape[2], d=shape[3])
            return v

        u_all = [cut([DB, GT]) for _ in range(NG)]
        y_all = [m.rearrange("p a b -> p (a b)").rearrange("p (t d) -> p t d", d=DI) for m in u_all]
        temps = used[0]
        dt_all = [[cut([DB, GT]) for _ in range(2)] for _ in range(NG)]
        c_all = cut([NG, GT], BF16, parts=96)
        fronts = used[0]
        b_bc = [cut([QN, GT]) for _ in range(2)]
        decay = [[cut([QN, GT]) for _ in range(2)] for _ in range(2)]
        state = [cut([QN, GT]) for _ in range(DB)]
        prod = [cut([QN, GT]) for _ in range(2)]
        dtu = [ln_flat[:, DB * GT * d:DB * GT * (d + 1)].rearrange("p (b t) -> p b t", b=DB) for d in range(2)]
        used[0] = temps
        conv = [cut([DB, GT]) for _ in range(2)]
        sz = [cut([TG, DI]) for _ in range(2)]
        gate_in = [cut([2, TG, DI]) for _ in range(2)]
        used[0] = fronts
        w_in_sb = cut([KT, 2 * DI], parts=KC)
        pos_sb = cut([2, C])
        spos_sb = cut([2, NPOS, SUB])
        w_probe = cut([C], parts=DR)
        w_lb = cut([DB, 96])
        w_c = cut([DB, 96])
        dt_w_sb = cut([DI], parts=64)
        gb_out_sb = cut([2, DI])
        after_params = used[0]
        rows = cut([TILES, SUB])
        sel_d = cut([TILES, 2, NPOS])
        sel_e = cut([TILES, 2, NPOS])
        sel_w = cut([TILES, 2, NPOS])
        sel_m = cut([TILES, 2])
        sel_s = cut([TILES, 2])
        sel_r = cut([TILES, 2])
        mix = [cut([HT, SUB]) for _ in range(2)]
        used[0] = after_params
        lb = [cut([GT], parts=96) for _ in range(2)]
        c_rest = cut([GT], parts=96)
        c_hi = cut([GT], BF16, parts=96)
        c_mid = cut([GT], BF16, parts=96)
        sp_pos, sp_e, sp_w = zip(*[[cut([DB, GT]) for _ in range(3)] for _ in range(SP)])
        used[0] -= 3 * DB * GT
        xn = [cut([TG, C]) for _ in range(2)]
        xn_t = [cut([KT, GT], parts=KC) for _ in range(2)]

        used[0] = 0
        slot_rows = cut([SLOTS, C])
        slot_flat = slot_rows.rearrange("p a b -> p (a b)")
        HOT_B, HOT_A = TOP * TILES * P // 2, TOP * TILES * SLOTS
        hot_b = slot_flat[:, 0:HOT_B].bitcast(BF16).rearrange("p (a b) -> p a b", b=P)
        hot_a = slot_flat[:, HOT_B:HOT_B + HOT_A].bitcast(BF16).rearrange("p (a h b) -> p a h b", b=SLOTS, h=2)
        is_slot = slot_flat[:, HOT_B + HOT_A:HOT_B + 2 * HOT_A].rearrange("p (a b) -> p a b", b=SLOTS)
        w1_at = used[0]
        w1 = cut([E, KT, H], parts=KC + 1)
        w2_at = used[0]
        w2 = cut([E, HB, C])
        raw1 = [cut([KT, H], parts=KC) for _ in range(3)]
        raw2 = [cut([HB, C]) for _ in range(3)]
        slot_x_t = [cut([KT, P], parts=KC + 1) for _ in range(2)]
        x_cur = [cut([C]) for _ in range(2)]
        routed = cut([TILES, RC])
        w_out_sb = cut([DB, C])
        rt = {n: cut([TILES, E]) for n in ("a", "b", "logit", "top", "hot0", "hot1", "gate", "f")}
        rt_i = cut([TILES, E], U32)
        rt_sq = cut([TILES, DR])
        tables = used[0]
        rt_1 = {n: sb("rt1_" + n, [P, TILES]) for n in ("n2", "n", "m", "r", "tp", "d", "e", "s", "g0", "g1")}
        w2_flat = w2.rearrange("p a b c -> p (a b c)")

        def y_back(g):
            return w2_flat[:, TG * TOP * C * g:TG * TOP * C * (g + 1)].rearrange("p (t c) -> p t c", t=TG)
        LATE = E // 2
        used[0] = w1_at + LATE * KT * H
        gate_back = [cut([2, TG, DI]) for _ in range(2)]
        assert used[0] <= w2_at
        used[0] = w2_at + LATE * HB * C
        y_t = [cut([DB, GT]) for _ in range(2)]
        x_g = [cut([TG, C]) for _ in range(2)]
        assert used[0] <= w2_at + E * HB * C
        x_g_t = [ln_flat[0:KC, KT * GT * i:KT * GT * (i + 1)].rearrange("p (k t) -> p k t", k=KT) for i in range(2)]
        h_pos = [ln_flat[:, H * i:H * i + H] for i in range(2)]
        h_t = [ln_flat[:, H * (2 + i):H * (3 + i)].rearrange("p (a b) -> p a b", b=P) for i in range(2)]
        gate_t = ln_flat[0:E, 0:TOK]
        by_et = [ln_flat[:, TOK + E * TILES * i:TOK + E * TILES * (i + 1)] for i in range(8)]
        tot, run_tot, offs, not_first = (m.rearrange("p (e t) -> p e t", e=E) for m in by_et[0:4])
        full, hots, *picked = (m.rearrange("p (t e) -> p t e", e=E) for m in by_et[4:8])
        used[0] = tables
        where_f, slot_f, place_f = (cut([TOP, TILES]) for _ in range(3))
        where_i, slot_i, place_i = (cut([TOP, TILES], I32) for _ in range(3))
        past = cut([SLOTS, E], parts=1)
        past_n = cut([SLOTS], parts=1)
        slot_expert = cut([SLOTS], I32, parts=1)
        cnt_i, cnt_s = (cut([E], I32) for _ in range(2))
        n_slots, end_slot, base_row = (cut([E]) for _ in range(3))
        held = cut([SLOTS])
        empty = cut([SLOTS])
        empty_s = cut([SLOTS])
        src_2 = cut([SLOTS], I32)
        src_row = cut([SLOTS], I32)
        dst_row = cut([SLOTS], I32)

        ps = ctx.enter_context(nc.psum_tensor("ps", [P, 8, 512], FP32))
        Y, BCAST = 0, 3
        y_ps = ps[:, Y:Y + DB, :].rearrange("p a b -> p (a b)")

        s_tok = sem("tokens_loaded")
        s_front = sem("front_loaded")
        s_par = sem("params_loaded")
        s_rows = [sem("rows_gathered_0"), sem("rows_gathered_1")]
        s_ln_in = sem("layer_norm_variance_ready")
        s_rstd_in = sem("layer_norm_rstd_ready")
        s_ident = sem("ident_ready")
        s_setup_v = sem("setup_vector")
        v_step = sem("vector_step")
        a_step = sem("scalar_step")
        p_step = sem("pool_step")
        s_sel_d = sem("select_logits_ready")
        s_sel_e = sem("select_exp_ready")
        s_sel_w = sem("select_weights_ready")
        s_cp = sem("row_copied")
        s_mix1 = sem("second_mix_ready")
        s_ln = sem("variance_ready")
        s_rstd = sem("rstd_ready")
        s_lnin = sem("ln_in_ready")
        s_res = sem("resid_ready")
        s_nega = sem("decay_rate_exp_ready")
        s_xn = sem("xn_ready")
        s_xn_ps = sem("xn_transposed")
        s_xn_t = sem("xn_t_ready")
        s_xi = sem("xi_ready")
        s_z = sem("z_ready")
        s_sz = sem("sz_ready")
        s_conv = sem("conv_ready")
        s_u = sem("u_ready")
        s_split = sem("bc_split_ready")
        s_dt_ps = sem("dt_product")
        s_pos = sem("softplus_pos_ready")
        s_e = sem("softplus_exp_ready")
        s_c = sem("softplus_corr_ready")
        s_rc = sem("softplus_pos_corrected")
        s_l = sem("softplus_log_ready")
        s_lb_ps = sem("dt_and_b_product")
        s_lb = sem("dt_and_b_rows_ready")
        s_cc_ps = sem("c_product")
        s_gate_in = sem("gate_terms_ready")
        s_gate_st = [sem("gate_terms_stored_0"), sem("gate_terms_stored_1")]
        s_gate_ld = [sem("gate_terms_loaded_0"), sem("gate_terms_loaded_1")]
        s_b_st = [sem("b_rows_stored_0"), sem("b_rows_stored_1")]
        s_b_ld = [sem("b_forward_loaded"), sem("b_backward_loaded")]
        s_dt = sem("dt_ready")
        s_skip = sem("skip_diagonals_ready")
        s_w_out = sem("w_out_loaded")
        s_yv = sem("y_left_banks")
        s_added = sem("layer_output_added")
        s_ln2 = sem("expert_norm_variance_ready")
        s_rstd2 = sem("expert_norm_rstd_ready")
        s_rstd_y = sem("y_norm_rstd_ready")
        s_ln_y = sem("y_norm_variance_ready")
        s_x = sem("dtu_ready")
        s_c_ps = sem("c_broadcast_ready")
        s_decay = sem("decay_ready")
        s_in = sem("scan_input_ready")
        s_scan = sem("scan_done")
        s_mul = sem("c_multiplied")
        s_sum = sem("y_summed")
        s_yn = sem("y_normed")
        s_yt_ps = sem("y_transposed")
        s_yt = sem("y_t_ready")
        s_o_ps = sem("out_product")
        s_xg = sem("x_g_ready")
        s_xg_ps = sem("x_g_transposed")
        s_xg_t = sem("x_g_t_ready")
        s_r_ps = sem("router_product")
        s_r = sem("router_sums_kept")
        s_nrm = sem("norms_summed")
        s_nrm_r = sem("norms_rooted")
        s_gd = sem("gate_difference_ready")
        s_ge = sem("gate_exp_ready")
        s_gate = sem("gates_ready")
        s_gt_ps = sem("gates_transposed")
        s_gt = sem("gates_t_ready")
        s_gb = sem("gated_b2_product")
        s_acc = sem("accumulator_started")
        s_raw1 = sem("raw_first_weights_loaded")
        s_raw2 = sem("raw_second_weights_loaded")
        s_w1 = sem("first_weights_ready")
        s_w2 = sem("second_weights_ready")
        s_bias = sem("bias_row_loaded")
        s_xs = [sem("expert_inputs_stored_0"), sem("expert_inputs_stored_1")]
        s_hots = sem("hots_ready")
        s_cnt = sem("counts_product")
        s_place = sem("places_ready")
        s_held = sem("held_product")
        s_src = sem("source_rows_ready")
        s_dst = sem("slot_tables_ready")
        s_gather = sem("slot_gather_done")
        s_slot_in = sem("slots_gathered")
        s_one = sem("bias_ones_ready")
        s_xc = sem("slot_input_copied")
        s_xt_ps = sem("slot_input_transposed")
        s_xt = sem("slot_input_t_ready")
        s_h_ps = sem("hidden_product")
        s_hr = sem("hidden_relu")
        s_ht_ps = sem("hidden_transposed")
        s_h = sem("hidden_ready")
        s_o2 = sem("expert_product")
        s_y = sem("slot_output_ready")
        s_scatter = sem("slot_scatter_done")
        s_back = [sem(f"outputs_back_{i}") for i in range(4)]
        s_final = sem("group_final")
        s_esq = sem("embedding_squared")
        s_rset = sem("router_setup_product")
        s_wr = sem("router_weights_ready")
        s_store = sem("stored")
        s_passed = sem("waits_passed")
        FRONT_LOADS, PAR_LOADS = 2, 24
        DT_BANK = 2
        MUL0, SUM0 = DB, 2

        def alone(eng):
            eng.sem_inc(s_passed, 1)

        block = ctx.enter_context(nc.Block())

        @block.sync
        def _(sp):
            sp.dma_start(tok_sb[:], tok).then_inc(s_tok, 16)
            sp.dma_start(spos_sb.rearrange("p a b c -> p (a b c)"), spos.to_broadcast([P, 2 * NPOS * SUB])).then_inc(s_front, 16)
            sp.dma_start(pos_sb, pos).then_inc(s_front, 16)
            sp.wait_ge(s_setup_v, 1)
            loads = [(chan_sb[:], chan), (w_in_sb, w_in), (gb_in_sb[:], gb_in),
                     (dt_w_sb[0:RANK, :], dt_w[0]), (dt_w_sb[32:32 + RANK, :], dt_w[1]),
                     (merge_sb[:], merge.to_broadcast([P, 2])),
                     (gb_out_sb.rearrange("p a b -> p (a b)"), gb_out.to_broadcast([P, 2 * DI]))]
            for d in range(2):
                loads.append((w_lb[:, :, 32 * d:32 * d + RANK], xproj[:, d, :, 0:RANK]))
                loads.append((w_lb[:, :, 64 + NS * d:64 + NS * (d + 1)], xproj[:, d, :, RANK:RANK + NS]))
                for r in range(3):
                    loads.append((w_c[:, :, 32 * r + NS * d:32 * r + NS * (d + 1)], xproj[:, d, :, RANK + NS:RANK + 2 * NS]))
            loads += [(w_route_sb[:, :, 0:E + DR], w_route), (emb_t_sb[:], emb_t[0:DR, 0:E]), (w_probe, emb_t[0:DR, E:E + C]),
                      (energy_sb[:], energy.to_broadcast([P, E])), (fatigue_sb[:], fatigue.to_broadcast([P, E])),
                      (mg_sb[:].rearrange("p a b -> p (a b)"), gates12.to_broadcast([P, 2 * E])),
                      (b2_sb[:], b2)]
            assert len(loads) == PAR_LOADS, len(loads)
            for dst, src in loads:
                sp.dma_start(dst, src).then_inc(s_par, 16)
            for g in range(NG):
                sp.wait_ge(s_gate_in, g + 1)
                sp.dma_start(gates_dram[g], gate_in[g % 2].rearrange("p a b c -> p (a b c)")).then_inc(s_gate_st[g % 2], 16)
            for g in range(NG):
                sp.wait_ge(s_lb, g + 1)
                for d in range(2):
                    sp.dma_start(b_rows[d, NS * g:NS * (g + 1), :], lb[g % 2][64 + NS * d:64 + NS * (d + 1), :]).then_inc(s_b_st[g % 2], 16)
            for i in range(2):
                sp.wait_ge(s_b_st[i], 32 * NG // 2)

            def load_b(G, d):
                sp.dma_start(b_bc[d].rearrange("p n t -> p (n t)"),
                             b_rows[d, bass.ds(QN * G, QN), :].rearrange("(o n) t -> o (n t)", o=1).to_broadcast([P, QN * GT])).then_inc(s_b_ld[d], 16)
            sp.wait_ge(s_dt_ps, NG * 2 * DB)
            sp.wait_ge(s_dt, 2 * NG)
            sp.wait_ge(s_rset, 1)
            load_b(0, 0)
            load_b(0, 1)
            with sp.Fori(1, NG * NQ) as G:
                for d in range(2):
                    sp.wait_ge(s_in, PER_QUAD * G + DB * d - DB)
                    load_b(G, d)
            sp.wait_ge(s_sum, SUM0 + NG * NQ * PER_QUAD)
            def load_first(e):
                for k, src in enumerate((wf1, ws1, hf1)):
                    sp.dma_start(raw1[k], src[bass.ds(e, 1), :, :, :].rearrange("e p a b -> (e p) a b")).then_inc(s_raw1, 16)

            def load_second(e):
                for k, src in enumerate((wf2, ws2, hf2)):
                    sp.dma_start(raw2[k], src[bass.ds(e, 1), :, :, :].rearrange("e p a b -> (e p) a b")).then_inc(s_raw2, 16)
            sp.dma_start(w1[KC:KC + 1, 0:LATE, 1, :], b1[:, 0:LATE, :]).then_inc(s_bias, 16)
            load_first(0)
            load_second(0)
            with sp.Fori(1, E) as e:
                sp.wait_ge(s_w1, e)
                load_first(e)
                sp.wait_ge(s_w2, e)
                load_second(e)
            sp.wait_ge(s_o2, SLOTS)
            sp.wait_ge(s_scatter, 16 * SLOTS)
            for g in range(NG):
                sp.dma_start(y_back(g), y_rows[TOP * GT * g:TOP * GT * (g + 1), :].rearrange("(t p k) c -> p t (k c)", p=P, k=TOP)).then_inc(s_back[g], 16)
            for g in range(NG):
                sp.wait_ge(s_final, g + 1)
                sp.dma_start(out[GT * g:GT * (g + 1), :].rearrange("(t p) c -> p t c", p=P), resid[:, TG * g:TG * (g + 1), :]).then_inc(s_store, 16)
            sp.wait_ge(s_store, 16 * NG)

        @block.gpsimd
        def _(pool):
            g_ = nc.gpsimd
            st = Steps(pool, p_step)
            pool.wait_ge(s_tok, 16)
            for t in range(TILES):
                g_.indirect_dma_start(out=rows[:, t, :], out_offset=None, in_=emb,
                                      in_offset=bass.IndirectOffsetOnAxis(ap=tok_sb[:, t:t + 1].bitcast(U32), axis=0)).then_inc(s_rows[t // HT], 16)
            st(g_.memset(ident[:], 0.0))
            st(g_.memset(pick[:], 0.0))
            st.wait()
            g_.affine_select(out=ident[:], in_=ident[:], compare_op=ALU.not_equal, fill=1.0, base=0,
                             pattern=[[-1, P]], channel_multiplier=1).then_inc(s_ident, 1)
            for r in range(3):
                st.then(g_.affine_select(out=pick[:], in_=pick[:], compare_op=ALU.not_equal, fill=1.0, base=-32 * r,
                                         pattern=[[-1, 32]], channel_multiplier=1))
            st(g_.memset(before[:], 1.0))
            st(g_.iota(iota_i[:], pattern=[[1, E]], base=0, channel_multiplier=0))
            st(g_.iota(iota_pi[:], pattern=[[1, P]], base=0, channel_multiplier=0))
            st(g_.iota(row_ii[:], pattern=[[1, TOP], [TOP * P, TILES]], base=1, channel_multiplier=TOP))
            st(g_.iota(spare_i[:], pattern=[[P, SLOTS]], base=TOP * TOK + 1, channel_multiplier=1))
            st.wait()
            g_.affine_select(out=before[:], in_=before[:], compare_op=ALU.is_ge, fill=0.0, base=-1,
                             pattern=[[1, P]], channel_multiplier=-1).then_inc(s_ident, 1)
            pool.wait_ge(s_sel_w, 2)
            pool.wait_ge(s_front, 16 * FRONT_LOADS)
            half = slice(HT, TILES)
            dst = ln_in[:, half, 2 * SUB:3 * SUB]
            for k in range(NPOS):
                o = dst if k == 0 else mix[1]
                st.then(g_.tensor_tensor(o, spos_sb[:, 1:2, k, :].to_broadcast([P, HT, SUB]),
                                         sel_w[:, half, 1, k:k + 1].to_broadcast([P, HT, SUB]), ALU.mult))
                if k:
                    ins = g_.tensor_tensor(dst, dst, mix[1], ALU.add)
                    if k == NPOS - 1:
                        ins.then_inc(s_mix1, 1)
                    else:
                        st.then(ins)
            for h in range(2):
                half = slice(HT * h, HT * (h + 1))
                pool.wait_ge(s_lnin, h + 1)
                g_.tensor_tensor(resid[:, half, :], resid[:, half, :], ln_in[:, half, :], ALU.add).then_inc(s_res, 1)
            pool.wait_ge(s_par, 16 * PAR_LOADS)
            for g in range(NG):
                pool.wait_ge(s_sz, TG * (g + 1))
                if g >= 2:
                    pool.wait_ge(s_gate_st[g % 2], 16)
                for i in range(2):
                    last = g_.tensor_tensor(gate_in[g % 2][:, i], sz[g % 2], gb_out_sb[:, i:i + 1, :].to_broadcast([P, TG, DI]), ALU.mult)
                last.then_inc(s_gate_in, 1)
            for n in range(2 * NG):
                pool.wait_ge(s_c, n + 1)
                g_.tensor_tensor(sp_pos[n % SP], sp_pos[n % SP], sp_w[n % SP], ALU.subtract).then_inc(s_rc, 1)
            for g in range(NG):
                with pool.Fori(NQ * g, NQ * (g + 1)) as G:
                    for k in range(PER_QUAD):
                        d, blk = divmod(k, DB)
                        if blk == 0:
                            pool.wait_ge(s_b_ld[d], 16 * G + 16)
                            pool.wait_ge(s_x, 2 * g + d + 1)
                        pool.wait_ge(s_mul, PER_QUAD * G + k + 1)
                        g_.tensor_tensor(state[blk], dtu[d][:, blk:blk + 1, :].to_broadcast([P, QN, GT]),
                                         b_bc[d], ALU.mult).then_inc(s_in, 1)

            def combine(e):
                for raw, w, parts, row, loaded, made in ((raw1, w1, KC, 0, s_raw1, s_w1), (raw2, w2, P, 1, s_raw2, s_w2)):
                    f, s, h = (m.rearrange("p a b -> p (a b)") for m in raw)
                    n = w.shape[2] * w.shape[3]
                    flat = w.rearrange("p e a b -> p (e a b)")[0:parts]
                    pool.wait_ge(loaded, 48 * (e + 1))
                    st.then(g_.tensor_tensor(s, s, mg_sb[0:parts, row, e:e + 1].to_broadcast([parts, n]), ALU.mult))
                    st.then(g_.tensor_tensor(s, s, f, ALU.add))
                    g_.tensor_tensor(flat[:, n * e:n * (e + 1)], s, h, ALU.add).then_inc(made, 1)

            def gather(first, end):
                for s in range(first, end):
                    g_.indirect_dma_start(out=slot_rows[:, s, :], out_offset=None, in_=x_rows,
                                          in_offset=bass.IndirectOffsetOnAxis(ap=src_row[:, s:s + 1].bitcast(U32), axis=0)).then_inc(s_gather, 16)

            for e in range(LATE):
                combine(e)
            pool.wait_ge(s_src, 1)
            for i in range(2):
                pool.wait_ge(s_xs[i], 16 * NG // 2)
            for b, (first, end) in enumerate(zip(BATCHES, BATCHES[1:])):
                gather(first, end)
                pool.wait_ge(s_gather, 16 * end)
                pool.sem_inc(s_slot_in, end - first)
                if b >= 1 and LATE + b - 1 < E:
                    combine(LATE + b - 1)
            pool.wait_ge(s_dst, 1)
            for s in range(SLOTS):
                pool.wait_ge(s_y, s + 1)
                g_.indirect_dma_start(out=y_rows, out_offset=bass.IndirectOffsetOnAxis(ap=dst_row[:, s:s + 1].bitcast(U32), axis=0),
                                      in_=slot_rows[:, s, :], in_offset=None).then_inc(s_scatter, 16)
            pool.wait_ge(s_scatter, 16 * SLOTS)

        @block.vector
        def _(dve):
            v = nc.vector
            st = Steps(dve, v_step)
            v.memset(w_lb, 0.0)
            v.memset(w_route_sb[:, :, E + DR:E + DR + 1], 1.0)
            v.memset(eps_sb[:], EPS)
            v.memset(ones[:], 1.0).then_inc(s_setup_v, 1)
            def moments(src, t0, n, m, done):
                for t in range(n):
                    st(v.bn_stats(stats[:, t0 + t, :], src(t)))
                st.wait()
                for t in range(n):
                    last = v.bn_aggr(m[:, t0 + t, :], stats[:, t0 + t, :])
                last.then_inc(done, 1)

            def newton(t0, n, m, root):
                var, r, a, b = m[:, t0:t0 + n, 1], root[:, t0:t0 + n], nt1[:, t0:t0 + n], nt2[:, t0:t0 + n]
                st.then(v.tensor_tensor(a, r, r, ALU.mult))
                st.then(v.scalar_tensor_tensor(b, var, EPS, a, ALU.add, ALU.mult))
                st.then(v.tensor_scalar(a, b, -0.5, 1.5, ALU.mult, ALU.add))
                st.then(v.tensor_tensor(r, r, a, ALU.mult))

            def select(h):
                half = slice(HT * h, HT * (h + 1))
                dve.wait_ge(s_rows[h], 16 * HT)
                six = rows[:, half, 0:2 * NPOS].rearrange("p t (i k) -> p t i k", k=NPOS)
                st.then(v.tensor_reduce(sel_m[:, half], six, AX.X, ALU.max))
                v.tensor_tensor(sel_d[:, half], six, sel_m[:, half].unsqueeze(3).to_broadcast([P, HT, 2, NPOS]), ALU.subtract).then_inc(s_sel_d, 1)
                dve.wait_ge(s_sel_e, h + 1)
                st.then(v.tensor_reduce(sel_s[:, half], sel_e[:, half], AX.X, ALU.add))
                st.then(v.reciprocal(sel_r[:, half], sel_s[:, half]))
                v.tensor_tensor(sel_w[:, half], sel_e[:, half], sel_r[:, half].unsqueeze(3).to_broadcast([P, HT, 2, NPOS]), ALU.mult).then_inc(s_sel_w, 1)
                dve.wait_ge(s_sel_w, h + 1)
                dve.wait_ge(s_front, 16 * FRONT_LOADS)

            def mix_in(h, i):
                half = slice(HT * h, HT * (h + 1))
                dst = ln_in[:, half, SUB * (i + 1):SUB * (i + 2)]
                for k in range(NPOS):
                    o = dst if k == 0 else mix[0]
                    st.then(v.tensor_tensor(o, spos_sb[:, i:i + 1, k, :].to_broadcast([P, HT, SUB]),
                                            sel_w[:, half, i, k:k + 1].to_broadcast([P, HT, SUB]), ALU.mult))
                    if k:
                        st.then(v.tensor_tensor(dst, dst, mix[0], ALU.add))

            def embed(h):
                half = slice(HT * h, HT * (h + 1))
                dve.wait_ge(s_cp, h + 1)
                st.then(v.scalar_tensor_tensor(
                    resid[:, half, :].rearrange("p (b t) c -> p b (t c)", t=2), ln_in[:, half, :].rearrange("p (b t) c -> p b (t c)", t=2),
                    float(C) ** 0.5, pos_sb.rearrange("p t c -> p (t c)").unsqueeze(1).to_broadcast([P, BATCH // 2, 2 * C]),
                    ALU.mult, ALU.add))
                moments(lambda t: resid[:, HT * h + t, :], HT * h, HT, mv, s_ln)

            def norm_twice(h):
                half = slice(HT * h, HT * (h + 1))
                dve.wait_ge(s_rstd, h + 1)
                newton(HT * h, HT, mv, rs)
                st.then(v.tensor_tensor(nt1[:, half], rs[:, half], rs[:, half], ALU.mult))
                v.tensor_tensor(mv2[:, half, 1], mv[:, half, 1], nt1[:, half], ALU.mult).then_inc(s_ln_in, 1)
                for t in range(HT * h, HT * (h + 1)):
                    last = v.tensor_scalar(ln_in[:, t, :], resid[:, t, :], mv[:, t, 0:1], rs[:, t:t + 1], ALU.subtract, ALU.mult)
                last.then_inc(s_lnin, 1)
                dve.wait_ge(s_lnin, h + 1)
                dve.wait_ge(s_rstd_in, h + 1)
                newton(HT * h, HT, mv2, rs2)

            def norm_in(g):
                if g >= 2:
                    dve.wait_ge(s_xn_ps, g - 1)
                for t in range(TG):
                    i = g * TG + t
                    last = v.tensor_scalar(xn[g % 2][:, t, :], ln_in[:, i, :], rs2[:, i:i + 1], None, ALU.mult)
                last.then_inc(s_xn, 1)

            def constants():
                dve.wait_ge(s_nega, 1)
                st(v.tensor_scalar(neg_a[:], neg_a[:], -1.0, None, ALU.mult))
                st.then(v.tensor_scalar(d_merged[:], chan_sb[:, :, CH_D], merge_sb[:, 0:1], None, ALU.mult))
                st(v.scalar_tensor_tensor(d_merged[:], chan_sb[:, :, CH_D + 1], merge_sb[:, 1:2], d_merged[:], ALU.mult, ALU.add))
                v.tensor_tensor(emb_sq[:], emb_t_sb[:], emb_t_sb[:], ALU.mult).then_inc(s_esq, 1)
                dve.wait_ge(s_ident, 2)
                st(v.tensor_copy(iota_e[:], iota_i[:]))
                st(v.tensor_copy(iota_p[:], iota_pi[:]))
                st(v.tensor_copy(row_id[:], row_ii[:]))
                st(v.tensor_copy(spare[:], spare_i[:]))
                st.then(v.tensor_scalar(row_lo_i[:], row_ii[:], 63, None, ALU.bitwise_and))
                st.then(v.tensor_copy(row_lo[:], row_lo_i[:]))
                st(v.tensor_tensor(row_hi[:], row_id[:], row_lo[:], ALU.subtract))
                for blk in range(DB):
                    last = v.tensor_scalar(skip[:, blk, :], ident[:], d_merged[:, blk:blk + 1], None, ALU.mult)
                last.then_inc(s_skip, 1)

            select(0)
            mix_in(0, 0)
            mix_in(0, 1)
            embed(0)
            norm_twice(0)

            norm_in(0)
            norm_in(1)
            select(1)
            mix_in(1, 0)
            dve.wait_ge(s_mix1, 1)
            embed(1)
            dve.wait_ge(s_par, 16 * PAR_LOADS)
            def convolve(g):
                for blk in range(DB):
                    dve.wait_ge(s_xi, DB * g + blk + 1)
                    if g >= 2:
                        dve.wait_ge(s_u, DB * (g - 2) + blk + 1)
                    cv = conv[g % 2][:, blk, :].rearrange("p (s t) -> p s t", t=SEQ)
                    bank = ps[:, 2 + blk, :]
                    xi = bank.rearrange("p (s t) -> p s t", t=SEQ)
                    st.then(v.tensor_scalar(conv[g % 2][:, blk, :], bank, chan_sb[:, blk, 1:2], chan_sb[:, blk, CH_CB:CH_CB + 1],
                                            ALU.mult, ALU.add))
                    st.then(v.scalar_tensor_tensor(cv[:, :, 1:SEQ], xi[:, :, 0:SEQ - 1], chan_sb[:, blk, 0:1],
                                                   cv[:, :, 1:SEQ], ALU.mult, ALU.add))
                    v.scalar_tensor_tensor(cv[:, :, 0:SEQ - 1], xi[:, :, 1:SEQ], chan_sb[:, blk, 2:3],
                                           cv[:, :, 0:SEQ - 1], ALU.mult, ALU.add).then_inc(s_conv, 1)

            convolve(0)
            norm_twice(1)
            norm_in(2)
            convolve(1)
            norm_in(3)
            constants()
            convolve(2)
            convolve(3)

            def split_c(g):
                dve.wait_ge(s_cc_ps, g + 1)
                bank = ps[0:96, 1, :]
                st(v.tensor_copy(c_all[0:32, g, :], bank[0:32, :]))
                st.then(v.tensor_copy(c_hi, bank))
                st.then(v.tensor_tensor(c_rest, bank, c_hi, ALU.subtract))
                st(v.tensor_copy(c_all[32:64, g, :], c_rest[32:64, :]))
                st.then(v.tensor_copy(c_mid[64:96, :], c_rest[64:96, :]))
                v.tensor_tensor(c_all[64:96, g, :], c_rest[64:96, :], c_mid[64:96, :], ALU.subtract).then_inc(s_split, 1)

            def correction(n):
                w, e = sp_w[n % SP], sp_e[n % SP]
                dve.wait_ge(s_e, n + 1)
                st.then(v.tensor_scalar(w, e, 1.0, None, ALU.add))
                v.scalar_tensor_tensor(w, w, -1.0, e, ALU.add, ALU.subtract).then_inc(s_c, 1)

            def dt_sum(n):
                dt = dt_all[n // 2][n % 2]
                dve.wait_ge(s_l, n + 1)
                dve.wait_ge(s_rc, n + 1)
                v.tensor_tensor(dt, sp_pos[n % SP], dt, ALU.add).then_inc(s_dt, 1)

            for n in range(2 * NG):
                if n % 2 == 0:
                    if n:
                        dve.wait_ge(s_split, n // 2)
                    split_c(n // 2)
                correction(n)
                if n:
                    dt_sum(n - 1)
            dt_sum(2 * NG - 1)

            def times_u(g, d):
                v.scalar_tensor_tensor(dtu[d], dt_all[g][d], merge_sb[:, d:d + 1], u_all[g], ALU.mult, ALU.mult).then_inc(s_x, 1)

            dve.wait_ge(s_rset, 1)
            st(v.tensor_copy(gain_1[:], ps[:, 7, 0:E]))
            st.wait()
            v.tensor_copy(w_route_sb[:, :, E + DR + 1:RC], ps[0:KC, 7, E:(1 + KT) * E].rearrange("p (k e) -> p k e", k=KT)).then_inc(s_wr, 1)
            dve.wait_ge(s_res, 2)
            dve.wait_ge(s_xn_ps, NG)
            dve.wait_ge(s_dt, 2 * NG)
            times_u(0, 0)
            times_u(0, 1)
            for i in range(2):
                dve.wait_ge(s_b_st[i], 32 * NG // 2)
            for d in range(2):
                for b in range(2):
                    st(v.memset(decay[d][b].rearrange("p n (s t) -> p n s t", t=SEQ)[:, :, :, 0 if d == 0 else SEQ - 1], 0.0))
            st.wait()
            dve.sem_inc(s_mul, MUL0)
            dve.sem_inc(s_scan, PER_QUAD)

            def scan(k, G):
                d, blk = divmod(k, DB)
                i = PER_QUAD * G + k
                dve.wait_ge(s_decay, i + 1)
                dve.wait_ge(s_in, i + 1)
                a, x = (m.rearrange("p n t -> p (n t)") for m in (decay[d][blk % 2], state[blk]))
                if d:
                    a, x = a[:, ::-1], x[:, ::-1]
                v.tensor_tensor_scan(x, a, x, 0.0, ALU.mult, ALU.add).then_inc(s_scan, 1)

            def times_c(k, G):
                d, blk = divmod(k, DB)
                i = PER_QUAD * G + k
                dve.wait_ge(s_scan, i + 1 + PER_QUAD)
                if blk == 0:
                    dve.wait_ge(s_c_ps, 2 * G + d + 1)
                dve.wait_ge(s_sum, i - 1 + SUM0)
                v.tensor_tensor(prod[k % 2], state[blk], ps[:, BCAST:BCAST + QN, :], ALU.mult).then_inc(s_mul, 1)

            def quad(G, following=None):
                scan(0, G)
                for k in range(1, PER_QUAD):
                    scan(k, G)
                    if following is not None and k == DB + 1:
                        dve.wait_ge(s_in, PER_QUAD * G + DB)
                        times_u(following, 0)
                    if following is not None and k == PER_QUAD - 1:
                        dve.wait_ge(s_in, PER_QUAD * G + PER_QUAD)
                        times_u(following, 1)
                    times_c(k - 1, G)
                times_c(PER_QUAD - 1, G)

            for g in range(NG):
                if g + 1 < NG:
                    with dve.Fori(NQ * g, NQ * g + NQ - 1) as G:
                        quad(G)
                    quad(NQ * g + NQ - 1, following=g + 1)
                else:
                    with dve.Fori(NQ * g, NQ * (g + 1)) as G:
                        quad(G)

            alone(dve)
            def moments_y(g):
                dve.wait_ge(s_yv, g + 1)
                moments(lambda t: y_all[g][:, t, :], TG * g, TG, mv, s_ln_y)

            def gate_y(g):
                dve.wait_ge(s_gate_ld[g % 2], 16 * (g // 2 + 1))
                for t in range(TG):
                    i = TG * g + t
                    st(v.scalar_tensor_tensor(y_all[g][:, t, :], y_all[g][:, t, :], mv[:, i, 0:1], gate_back[g % 2][:, 0, t, :],
                                              ALU.subtract, ALU.mult))
                st.wait()
                for t in range(TG):
                    i = TG * g + t
                    last = v.scalar_tensor_tensor(y_all[g][:, t, :], y_all[g][:, t, :], rs[:, i:i + 1], gate_back[g % 2][:, 1, t, :],
                                                  ALU.mult, ALU.add)
                last.then_inc(s_yn, 1)

            def add_layer(g):
                dve.wait_ge(s_o_ps, g + 1)
                part = resid[:, TG * g:TG * (g + 1), :]
                v.tensor_tensor(part.rearrange("p (a b) c -> p a (b c)", b=2), part.rearrange("p (a b) c -> p a (b c)", b=2),
                                ps[:, 3:5, 0:2 * C], ALU.add).then_inc(s_added, 1)
                dve.wait_ge(s_added, g + 1)
                moments(lambda t: resid[:, TG * g + t, :], TG * g, TG, mv2, s_ln2)

            def norm_x(g):
                dve.wait_ge(s_rstd2, g + 1)
                newton(TG * g, TG, mv2, rs2)
                if g >= 2:
                    dve.wait_ge(s_xg_ps, g - 1)
                    dve.wait_ge(s_xs[g % 2], 16)
                for t in range(TG):
                    i = TG * g + t
                    last = v.tensor_scalar(x_g[g % 2][:, t, :], resid[:, i, :], mv2[:, i, 0:1], rs2[:, i:i + 1], ALU.subtract, ALU.mult)
                last.then_inc(s_xg, 1)
            for h in range(2):
                moments_y(2 * h)
                moments_y(2 * h + 1)
                dve.wait_ge(s_rstd_y, h + 1)
                newton(HT * h, HT, mv, rs)
                if h == 0:
                    gate_y(0)
            for g in range(NG):
                if g + 1 < NG:
                    gate_y(g + 1)
                add_layer(g)
                norm_x(g)
            for i in range(2):
                dve.wait_ge(s_xs[i], 16 * NG // 2)

            dve.wait_ge(s_r, NG)
            dve.wait_ge(s_nrm, 1)
            st(v.tensor_reduce(rt_1["n2"][:], rt_sq, AX.X, ALU.add))
            st.wait()
            dve.sem_inc(s_nrm_r, 1)
            dve.wait_ge(s_nrm_r, 3)
            st(v.tensor_scalar(rt_1["m"][:], rt_1["n"][:], 1e-12, None, ALU.max))
            st(v.tensor_scalar(gain_r[:], gain[:], 1e-12, None, ALU.max))
            st.wait()
            st(v.reciprocal(rt_1["r"][:], rt_1["m"][:]))
            st(v.reciprocal(gain_1[:], gain_r[:]))
            st(v.tensor_scalar(rt_1["tp"][:], routed[:, :, E + DR], 0.02 / C, None, ALU.mult))
            st(v.tensor_scalar(gain_p[:], gain[:], 1.0, None, ALU.add))
            st(v.tensor_tensor(bias_e[:], energy_sb[:], fatigue_sb[:], ALU.subtract))
            st.wait()

            def by_tile(m):
                return m[:].unsqueeze(2).to_broadcast([P, TILES, E])

            def by_expert(m):
                return m[:].unsqueeze(1).to_broadcast([P, TILES, E])
            st(v.tensor_tensor(rt["a"], by_tile(rt_1["tp"]), by_expert(gain_p), ALU.mult))
            st(v.tensor_tensor(rt["b"], by_tile(rt_1["r"]), by_expert(gain_1), ALU.mult))
            st.wait()
            st(v.tensor_tensor(rt["a"], rt["a"], routed[:, :, 0:E], ALU.add))
            st(v.tensor_tensor(rt["b"], rt["b"], routed[:, :, E + DR + 1:RC], ALU.mult))
            st.wait()
            st.then(v.scalar_tensor_tensor(rt["a"], rt["b"], 0.02, rt["a"], ALU.mult, ALU.add))
            st.then(v.scalar_tensor_tensor(rt["logit"], by_expert(bias_e), 0.1, rt["a"], ALU.mult, ALU.add))
            for t in range(TILES):
                st(v.max(rt["top"][:, t, :], rt["logit"][:, t, :]))
            st.wait()
            for t in range(TILES):
                st(v.max_index(rt_i[:, t, :], rt["top"][:, t, :], rt["logit"][:, t, :]))
            v.tensor_tensor(rt_1["d"][:], rt["top"][:, :, 1], rt["top"][:, :, 0], ALU.subtract).then_inc(s_gd, 1)
            st.wait()
            st.then(v.tensor_copy(rt["f"], rt_i))
            st(v.tensor_tensor(rt["hot0"], by_expert(iota_e), rt["f"][:, :, 0:1].to_broadcast([P, TILES, E]), ALU.is_equal))
            st(v.tensor_tensor(rt["hot1"], by_expert(iota_e), rt["f"][:, :, 1:2].to_broadcast([P, TILES, E]), ALU.is_equal))
            st.wait()
            v.tensor_tensor(hots, rt["hot0"], rt["hot1"], ALU.add).then_inc(s_hots, 1)
            dve.wait_ge(s_ge, 1)
            st.then(v.tensor_scalar(rt_1["s"][:], rt_1["e"][:], 1.0, None, ALU.add))
            st.then(v.reciprocal(rt_1["g0"][:], rt_1["s"][:]))
            st.then(v.tensor_tensor(rt_1["g1"][:], rt_1["g0"][:], rt_1["e"][:], ALU.mult))
            st(v.tensor_tensor(rt["a"], rt["hot0"], by_tile(rt_1["g0"]), ALU.mult))
            st.then(v.tensor_tensor(rt["b"], rt["hot1"], by_tile(rt_1["g1"]), ALU.mult))
            v.tensor_tensor(rt["gate"], rt["a"], rt["b"], ALU.add).then_inc(s_gate, 1)
            st.then(v.memset(not_first, 1.0))
            st(v.memset(not_first[:, :, 0], 0.0))
            dve.wait_ge(s_cnt, 1)
            st.then(v.tensor_copy(tot, ps[:, 1, 0:TILES * E].rearrange("p (t e) -> p e t", e=E)))
            flat = [m.rearrange("p a b -> p (a b)") for m in (run_tot, not_first, tot)]
            st.then(v.tensor_tensor_scan(flat[0], flat[1], flat[2], 0.0, ALU.mult, ALU.add))
            st.then(v.tensor_scalar(cnt_i, run_tot[:, :, TILES - 1], float(P - 1), None, ALU.add))
            st.then(v.tensor_scalar(cnt_s, cnt_i, SHIFT, None, ALU.logical_shift_right))
            st.then(v.tensor_copy(n_slots, cnt_s))
            st.then(v.tensor_tensor_scan(end_slot, ones[:, 0:E], n_slots, 0.0, ALU.mult, ALU.add))
            st(v.tensor_tensor(past, iota_p[0:1, 0:SLOTS].unsqueeze(2).to_broadcast([1, SLOTS, E]),
                               end_slot[0:1, :].unsqueeze(1).to_broadcast([1, SLOTS, E]), ALU.is_ge))
            st.then(v.tensor_tensor(base_row, end_slot, n_slots, ALU.subtract))
            st(v.tensor_scalar(base_row, base_row, float(P), None, ALU.mult))
            st.then(v.tensor_tensor(offs, run_tot, tot, ALU.subtract))
            st.then(v.tensor_tensor(offs, offs, base_row.unsqueeze(2).to_broadcast([P, E, TILES]), ALU.add))
            st.then(v.tensor_tensor(full, ps[:, 0, 0:TILES * E].rearrange("p (t e) -> p t e", e=E),
                                    offs.rearrange("p e t -> p t e"), ALU.add))
            for k in range(TOP):
                st(v.tensor_tensor(picked[k], full, rt[f"hot{k}"], ALU.mult))
            st.wait()
            for k in range(TOP):
                st(v.tensor_reduce(where_f[:, k, :], picked[k], AX.X, ALU.add))
            st.then(v.tensor_reduce(past_n, past, AX.X, ALU.add))
            st(v.tensor_scalar(slot_expert, past_n, float(E - 1), None, ALU.min))
            st.then(v.tensor_copy(where_i, where_f))
            st(v.tensor_scalar(slot_i, where_i, SHIFT, None, ALU.logical_shift_right))
            st.then(v.tensor_scalar(place_i, where_i, P - 1, None, ALU.bitwise_and))
            st(v.tensor_copy(slot_f, slot_i))
            st.then(v.tensor_copy(place_f, place_i))

            def each(m, n):
                return m.rearrange("p k t -> p (k t)").unsqueeze(2).to_broadcast([P, TOP * TILES, n])
            st.then(v.tensor_tensor(is_slot, iota_p[:, 0:SLOTS].unsqueeze(1).to_broadcast([P, TOP * TILES, SLOTS]), each(slot_f, SLOTS), ALU.is_equal))
            for h, part in enumerate((row_hi, row_lo)):
                st(v.tensor_tensor(hot_a[:, :, h, :], is_slot, each(part[:], SLOTS), ALU.mult))
            v.tensor_tensor(hot_b, iota_p[:].unsqueeze(1).to_broadcast([P, TOP * TILES, P]), each(place_f, P), ALU.is_equal).then_inc(s_place, 1)
            st.wait()
            dve.sem_inc(s_place, 1)
            dve.wait_ge(s_held, 1)
            st.then(v.tensor_copy(empty_s, ps[:, 2, 0:SLOTS]))
            st.then(v.tensor_tensor(held, ps[:, 2, SLOTS:2 * SLOTS], empty_s, ALU.add))
            st(v.tensor_scalar(src_2, held, -1.0, 0.0, ALU.add, ALU.max))
            st.then(v.tensor_scalar(empty, held, 0.0, None, ALU.is_equal))
            v.tensor_scalar(src_row, src_2, 1, None, ALU.logical_shift_right).then_inc(s_src, 1)
            st.then(v.tensor_tensor(empty_s, empty, spare[:], ALU.mult))
            v.scalar_tensor_tensor(dst_row, held, -1.0, empty_s, ALU.add, ALU.add).then_inc(s_dst, 1)
            for i in range(2):
                last = v.memset(slot_x_t[i][KC:KC + 1, KT - 1, :], 1.0)
            last.then_inc(s_one, 1)
            for part in range(4):
                dve.wait_ge(s_gb, part + 1)
                res_g = resid[:, TG * part:TG * part + TG, :]
                v.tensor_tensor(res_g, res_g, ps[:, 4:4 + TG, 0:C], ALU.add).then_inc(s_acc, 1)

            def relu(s, half):
                dve.wait_ge(s_h_ps, s + 1)
                dve.wait_ge(s_ht_ps, s + 1)
                v.tensor_scalar(h_pos[half].rearrange("p (a b) -> p a b", a=2), ps[:, 0:2, 0:HH], 0.0, None, ALU.max).then_inc(s_hr, 1)

            def keep(s):
                dve.wait_ge(s_o2, s + 1)
                row = slot_rows[:, bass.ds(s, 1), :].rearrange("p a c -> p (a c)") if not isinstance(s, int) else slot_rows[:, s, :]
                v.tensor_copy(row, ps[:, 3, 0:C]).then_inc(s_y, 1)
            relu(0, 0)
            with dve.Fori(0, (SLOTS - 1) // 2) as pair:
                for i in range(2):
                    relu(2 * pair + 1 + i, 1 - i)
                    keep(2 * pair + i)
            keep(SLOTS - 1)
            for g in range(NG):
                dve.wait_ge(s_back[g], 16)
                if g == 0:
                    dve.wait_ge(s_acc, 4)
                for k in range(TOP):
                    for t in range(TG):
                        i = g * TG + t
                        last = v.scalar_tensor_tensor(resid[:, i, :], y_back(g)[:, t, C * k:C * k + C], rt_1[f"g{k}"][:, i:i + 1],
                                                      resid[:, i, :], ALU.mult, ALU.add)
                        if k == 0:
                            st(last)
                    if k == 0:
                        st.wait()
                last.then_inc(s_final, 1)

        @block.scalar
        def _(act):
            a = nc.scalar
            a.preload_act_table_set("natural_log_exp_and_others")
            st = Steps(act, a_step)

            def rstd(t0, n, m, root, ready, k, done):
                act.wait_ge(ready, k)
                st.then(a.activation(nt2[:, t0:t0 + n], m[:, t0:t0 + n, 1], ACT.Ln, bias=eps_sb[:]))
                a.activation(root[:, t0:t0 + n], nt2[:, t0:t0 + n], ACT.Exp, scale=-0.5).then_inc(done, 1)

            act.wait_ge(s_setup_v, 1)

            def select_exp(h):
                half = slice(HT * h, HT * (h + 1))
                act.wait_ge(s_sel_d, h + 1)
                a.activation(sel_e[:, half], sel_d[:, half], ACT.Exp).then_inc(s_sel_e, 1)
                a.activation(ln_in[:, half, 0:SUB], rows[:, half], ACT.Copy).then_inc(s_cp, 1)

            def norm_roots(h):
                rstd(HT * h, HT, mv, rs, s_ln, h + 1, s_rstd)
                rstd(HT * h, HT, mv2, rs2, s_ln_in, h + 1, s_rstd_in)
            select_exp(0)
            norm_roots(0)
            act.wait_ge(s_par, 16 * (PAR_LOADS))
            a.activation(neg_a[:], chan_sb[:, :, CH_ALOG:CH_ALOG + 2 * NS].rearrange("p b (d n) -> p b d n", n=NS), ACT.Exp).then_inc(s_nega, 1)

            def keep_xn_t(g):
                act.wait_ge(s_xn_ps, g + 1)
                if g >= 2:
                    act.wait_ge(s_z, TG * (g - 1))
                for k in range(KT):
                    a.activation(xn_t[g % 2][:, k, :], ps[0:KC, k, :], ACT.Identity, scale=gb_in_sb[:, k, 0:1],
                                 bias=gb_in_sb[:, k, 1:2]).then_inc(s_xn_t, 1)

            select_exp(1)
            keep_xn_t(0)
            keep_xn_t(1)
            norm_roots(1)
            for g in range(NG):
                if 0 < g < NG - 1:
                    keep_xn_t(g + 1)
                for blk in range(DB):
                    act.wait_ge(s_conv, DB * g + blk + 1)
                    a.activation(u_all[g][:, blk, :], conv[g % 2][:, blk, :], ACT.Silu).then_inc(s_u, 1)
                if g >= 2:
                    act.wait_ge(s_gate_in, g - 1)
                for t in range(TG):
                    n = TG * g + t
                    act.wait_ge(s_z, n + 1)
                    a.activation(sz[g % 2][:, t, :], ps[:, 5 + n % 3, 0:DI], ACT.Silu).then_inc(s_sz, 1)

            def keep_lb(g):
                act.wait_ge(s_lb_ps, g + 1)
                if g >= 2:
                    act.wait_ge(s_b_st[g % 2], 32)
                a.activation(lb[g % 2], ps[0:96, 0, :], ACT.Copy).then_inc(s_lb, 1)

            a.preload_act_table_set("natural_log_exp_and_others")
            keep_lb(0)
            for g in range(NG):
                for d in range(2):
                    n = 2 * g + d
                    if n >= SP:
                        act.wait_ge(s_dt, n - SP + 1)
                    if n == 0:
                        act.wait_ge(s_u, NG * DB)
                    if n == 2:
                        act.wait_ge(s_gate_in, NG)
                    if n == 4:
                        for i in range(2):
                            act.wait_ge(s_gate_st[i], 16 * NG // 2)
                    dt = dt_all[g][d]
                    for blk in range(DB):
                        act.wait_ge(s_dt_ps, DB * n + blk + 1)
                        bias = chan_sb[:, blk, CH_DTB + d:CH_DTB + d + 1]
                        bank = ps[:, DT_BANK + DB * d + blk, :]
                        st(a.activation(dt[:, blk, :], bank, ACT.Abs, bias=bias))
                        a.activation(sp_pos[n % SP][:, blk, :], bank, ACT.Relu, bias=bias).then_inc(s_pos, 1)
                    st.wait()
                    a.activation(sp_e[n % SP], dt, ACT.Exp, scale=-1.0).then_inc(s_e, 1)
                    if d == 1 and g + 1 < NG:
                        keep_lb(g + 1)
                    act.wait_ge(s_e, n + 1)
                    a.activation(dt, sp_e[n % SP], ACT.Ln, bias=1.0).then_inc(s_l, 1)

            def exps(k, g, G):
                d, blk = divmod(k, DB)
                act.wait_ge(s_scan, PER_QUAD * G + k + PER_QUAD + (-3, -5, -1)[blk])
                out_b = decay[d][blk % 2].rearrange("p n (s t) -> p n s t", t=SEQ)
                src = dt_all[g][d][:, blk, :].rearrange("p (s t) -> p s t", t=SEQ)
                lo, hi = (1, SEQ) if d == 0 else (0, SEQ - 1)
                for n in range(QN):
                    q = G - NQ * g
                    scale = neg_a[:, blk, d, bass.ds(q * QN + n, 1)]
                    last = a.activation(out_b[:, n, :, lo:hi], src[:, :, lo:hi], ACT.Exp, scale=scale)
                last.then_inc(s_decay, 1)

            def keep_y(g):
                act.wait_ge(s_sum, SUM0 + NQ * PER_QUAD * (g + 1))
                a.activation(y_all[g].rearrange("p t d -> p (t d)"), y_ps, ACT.Copy).then_inc(s_yv, 1)

            act.wait_ge(s_dt, 2 * NG)
            for g in range(NG):
                for k in range(PER_QUAD):
                    exps(k, g, NQ * g)
                    if g and k == DB:
                        keep_y(g - 1)
                with act.Fori(NQ * g + 1, NQ * (g + 1)) as G:
                    for k in range(PER_QUAD):
                        exps(k, g, G)

            def load_gate(g):
                act.dma_start(gate_back[g % 2].rearrange("p a b c -> p (a b c)"), gates_dram[g]).then_inc(s_gate_ld[g % 2], 16)

            act.wait_ge(s_sum, SUM0 + NG * NQ * PER_QUAD)
            act.dma_start(w_out_sb, w_out).then_inc(s_w_out, 16)
            load_gate(0)
            load_gate(1)
            keep_y(NG - 1)
            for h in range(2):
                rstd(HT * h, HT, mv, rs, s_ln_y, NG // 2 * (h + 1), s_rstd_y)
            for g in range(NG + 1):
                if g:
                    rstd(TG * (g - 1), TG, mv2, rs2, s_ln2, g, s_rstd2)
                if g == NG:
                    act.wait_ge(s_wr, 1)
                    a.activation(gain[:], gain_1[:], ACT.Sqrt).then_inc(s_nrm_r, 1)
                if g < NG:
                    act.wait_ge(s_yt_ps, g + 1)
                    if g >= 2:
                        act.wait_ge(s_o_ps, g - 1)
                    a.activation(y_t[g % 2], ps[:, 0:DB, :], ACT.Copy).then_inc(s_yt, 1)
                    if g + 2 < NG:
                        act.wait_ge(s_yn, g + 1)
                        load_gate(g + 2)
                if g:
                    act.wait_ge(s_xg, g)
                    act.dma_start(x_rows[GT * (g - 1):GT * g, :].rearrange("(t p) c -> p t c", p=P), x_g[(g - 1) % 2]).then_inc(s_xs[(g - 1) % 2], 16)
                    act.wait_ge(s_xg_ps, g)
                    if g >= 3:
                        act.wait_ge(s_r_ps, g - 2)
                    a.activation(x_g_t[(g - 1) % 2], ps[0:KC, 5:5 + KT, :], ACT.Copy).then_inc(s_xg_t, 1)
                    act.wait_ge(s_r_ps, g)
                    a.activation(routed[:, TG * (g - 1):TG * g, :],
                                 ps[:, 7, :].rearrange("p (t c) -> p t c", t=TG)[:, :, 0:RC], ACT.Copy).then_inc(s_r, 1)
            act.dma_start(w1[KC:KC + 1, LATE:E, 1, :], b1[:, LATE:E, :]).then_inc(s_bias, 16)
            act.wait_ge(s_r, NG)
            a.activation(rt_sq, routed[:, :, E:E + DR], ACT.Square).then_inc(s_nrm, 1)
            act.wait_ge(s_nrm_r, 2)
            a.activation(rt_1["n"][:], rt_1["n2"][:], ACT.Sqrt).then_inc(s_nrm_r, 1)
            act.wait_ge(s_gd, 1)
            a.activation(rt_1["e"][:], rt_1["d"][:], ACT.Exp).then_inc(s_ge, 1)
            for part in range(4):
                act.wait_ge(s_gt_ps, part + 1)
                a.activation(gate_t[:, GT * part:GT * (part + 1)], ps[0:E, 3 + part, :], ACT.Copy).then_inc(s_gt, 1)

            def copy_x(s, half):
                act.wait_ge(s_slot_in, s + 1)
                if not isinstance(s, int) or s >= 2:
                    act.wait_ge(s_xt_ps, s - 1)
                a.activation(x_cur[half], slot_rows[:, bass.ds(s, 1), :].rearrange("p a c -> p (a c)"), ACT.Copy).then_inc(s_xc, 1)

            def keep_x_t(s, half):
                act.wait_ge(s_xt_ps, s + 1)
                if not isinstance(s, int) or s >= 2:
                    act.wait_ge(s_h_ps, s - 1)
                a.activation(slot_x_t[half][0:KC], ps[0:KC, 2, 0:KT * P].rearrange("p (k t) -> p k t", t=P), ACT.Copy).then_inc(s_xt, 1)

            def square(s, half):
                act.wait_ge(s_ht_ps, s + 3)
                if not isinstance(s, int) or s >= 2:
                    act.wait_ge(s_o2, s - 1)
                a.activation(h_t[half].rearrange("p (a b) c -> p a (b c)", a=2), ps[:, 4:6, 0:HH], ACT.Square).then_inc(s_h, 1)
            copy_x(0, 0)
            copy_x(1, 1)
            keep_x_t(0, 0)
            copy_x(2, 0)
            keep_x_t(1, 1)
            square(0, 0)
            with act.Fori(0, (SLOTS - 3) // 2) as pair:
                for i in range(2):
                    s = 2 * pair + 1 + i
                    copy_x(s + 2, 1 - i)
                    keep_x_t(s + 1, i)
                    square(s, 1 - i)
            keep_x_t(SLOTS - 1, 0)
            square(SLOTS - 2, 1)
            square(SLOTS - 1, 0)

        @block.tensor
        def _(pe):
            t_ = nc.tensor
            mm = t_.matmul

            def transpose(o, src, parts, start=True):
                return mm(o, src, ident[0:parts, 0:parts], start=start, stop=True, is_transpose=True, skip_group_check=True)

            pe.wait_ge(s_ident, 1)
            pe.wait_ge(s_par, 16 * (PAR_LOADS))
            def norm_transposes(g):
                pe.wait_ge(s_xn, g + 1)
                for t in range(TG):
                    for k in range(KT):
                        last = transpose(ps[0:KC, k, P * t:P * t + P], xn[g % 2][:, t, KC * k:KC * k + KC], P)
                last.then_inc(s_xn_ps, 1)

            norm_transposes(0)
            for g in range(NG):
                x = xn_t[g % 2]
                pe.wait_ge(s_xn_t, KT * (g + 1))
                for blk in range(DB):
                    if g:
                        pe.wait_ge(s_conv, DB * (g - 1) + blk + 1)
                    for k in range(KT):
                        last = mm(ps[:, 2 + blk, :], w_in_sb[:, k, P * blk:P * blk + P], x[:, k, :], start=k == 0, stop=k == KT - 1)
                    last.then_inc(s_xi, 1)
                if g + 1 < NG:
                    norm_transposes(g + 1)
                for t in range(TG):
                    n = TG * g + t
                    if n >= 3:
                        pe.wait_ge(s_sz, n - 2)
                    for k in range(KT):
                        last = mm(ps[:, 5 + n % 3, 0:DI], x[:, k, P * t:P * t + P], w_in_sb[:, k, DI:2 * DI], start=k == 0, stop=k == KT - 1)
                    last.then_inc(s_z, 1)

            def projections(g):
                pe.wait_ge(s_u, DB * (g + 1))
                if g:
                    pe.wait_ge(s_lb, g)
                for blk in range(DB):
                    last = mm(ps[0:96, 0, :], w_lb[:, blk, :], u_all[g][:, blk, :], start=blk == 0, stop=blk == DB - 1)
                last.then_inc(s_lb_ps, 1)
                if g:
                    pe.wait_ge(s_split, g)
                for blk in range(DB):
                    last = mm(ps[0:96, 1, :], w_c[:, blk, :], u_all[g][:, blk, :], start=blk == 0, stop=blk == DB - 1)
                last.then_inc(s_cc_ps, 1)

            projections(0)
            pe.wait_ge(s_conv, NG * DB)
            pe.wait_ge(s_sz, NG * TG)
            for g in range(NG):
                pe.wait_ge(s_lb, g + 1)
                for d in range(2):
                    for blk in range(DB):
                        if g:
                            pe.wait_ge(s_pos, DB * (2 * (g - 1) + d) + blk + 1)
                        mm(ps[:, DT_BANK + DB * d + blk, :], dt_w_sb[32 * d:32 * d + RANK, P * blk:P * blk + P],
                           lb[g % 2][32 * d:32 * d + RANK, :], start=True, stop=True).then_inc(s_dt_ps, 1)
                if g + 1 < NG:
                    projections(g + 1)

            def c_rows(g, G, d):
                pe.wait_ge(s_mul, DB * (2 * G + d) + MUL0)
                for n in range(QN):
                    j = (G - NQ * g) * QN + n + NS * d
                    last = mm(ps[:, BCAST + n, :], pick[:, bass.ds(j, 1)].to_broadcast([96, P]), c_all[:, g, :], start=True, stop=True)
                last.then_inc(s_c_ps, 1)

            def add(k, G, opens=False):
                blk = k % DB
                pe.wait_ge(s_mul, PER_QUAD * G + k + 1 + MUL0)
                for n in range(QN):
                    for t in range(TG):
                        c = t * DB + blk
                        first = opens and n == 0 and (t == 0 or c // 4 != (c - DB) // 4)
                        last = transpose(y_ps[:, P * c:P * c + P], prod[k % 2][:, n, P * t:P * t + P], P, start=first)
                last.then_inc(s_sum, 1)

            def skip_term(g, tiles):
                for t in tiles:
                    for blk in range(DB):
                        c = t * DB + blk
                        mm(y_ps[:, P * c:P * c + P], u_all[g][:, blk, P * t:P * t + P], skip[:, blk, :], start=False, stop=True,
                           skip_group_check=True)

            def quad(g, G, first=False, tiles=()):
                c_rows(g, G, 0)
                if not (first and g == 0):
                    add(PER_QUAD - 1, G - 1)
                if first and g:
                    pe.wait_ge(s_yv, g)
                add(0, G, opens=first)
                add(1, G)
                c_rows(g, G, 1)
                add(2, G)
                add(3, G)
                skip_term(g, tiles)
                add(4, G)

            pe.wait_ge(s_lb, NG)
            pe.wait_ge(s_split, NG)
            pe.wait_ge(s_pos, 2 * NG * DB)
            pe.wait_ge(s_skip, 1)
            pe.wait_ge(s_esq, 1)
            mm(ps[:, 7, 0:E], ones[0:DR, :], emb_sq[:], start=True, stop=True)
            for k in range(KT):
                last = mm(ps[0:KC, 7, (1 + k) * E:(2 + k) * E], w_probe[:, KC * k:KC * k + KC], emb_t_sb[:], start=True, stop=True)
            last.then_inc(s_rset, 1)
            pe.sem_inc(s_sum, SUM0)
            for g in range(NG):
                quad(g, NQ * g, first=True, tiles=(0, 1))
                with pe.Fori(NQ * g + 1, NQ * g + NQ - 1) as G:
                    quad(g, G)
                quad(g, NQ * g + NQ - 1, tiles=(2, 3))
            add(PER_QUAD - 1, NG * NQ - 1)

            pe.wait_ge(s_yv, NG)
            pe.wait_ge(s_w_out, 16)
            pe.wait_ge(s_wr, 1)
            for g in range(NG + 1):
                if g < NG:
                    pe.wait_ge(s_yn, g + 1)
                    if g:
                        pe.wait_ge(s_yt, g)
                    for t in range(TG):
                        for blk in range(DB):
                            last = transpose(ps[:, blk, P * t:P * t + P], y_all[g][:, t, P * blk:P * blk + P], P)
                    last.then_inc(s_yt_ps, 1)
                    pe.wait_ge(s_yt, g + 1)
                    if g:
                        pe.wait_ge(s_added, g)
                    for t in range(TG):
                        for blk in range(DB):
                            last = mm(ps[:, 3 + t // 2, C * (t % 2):C * (t % 2) + C], y_t[g % 2][:, blk, P * t:P * t + P], w_out_sb[:, blk, :],
                                      start=blk == 0, stop=blk == DB - 1)
                    last.then_inc(s_o_ps, 1)
                if g:
                    pe.wait_ge(s_xg, g)
                    if g >= 2:
                        pe.wait_ge(s_xg_t, g - 1)
                    for t in range(TG):
                        for k in range(KT):
                            last = transpose(ps[0:KC, 5 + k, P * t:P * t + P], x_g[(g - 1) % 2][:, t, KC * k:KC * k + KC], P)
                    last.then_inc(s_xg_ps, 1)
                    pe.wait_ge(s_xg_t, g)
                    if g >= 2:
                        pe.wait_ge(s_r, g - 1)
                    for t in range(TG):
                        for k in range(KT):
                            last = mm(ps[:, 7, P * t:P * t + RC], x_g_t[(g - 1) % 2][:, k, P * t:P * t + P], w_route_sb[:, k, :],
                                      start=k == 0, stop=k == KT - 1)
                    last.then_inc(s_r_ps, 1)
            pe.wait_ge(s_hots, 1)
            hot_cols = hots.rearrange("p t e -> p (t e)")
            mm(ps[:, 0, 0:TILES * E], before[:], hot_cols, start=True, stop=True)
            mm(ps[:, 1, 0:TILES * E], ones[:], hot_cols, start=True, stop=True).then_inc(s_cnt, 1)
            pe.wait_ge(s_gate, 1)
            for part in range(4):
                for t in range(TG):
                    last = transpose(ps[0:E, 3 + part, P * t:P * t + P], rt["gate"][:, TG * part + t, :], P)
                last.then_inc(s_gt_ps, 1)
            pe.wait_ge(s_place, 2)
            for i in range(TOP * TILES):
                last = mm(ps[:, 2, 0:2 * SLOTS], hot_b[:, i, :], hot_a[:, i, :, :].rearrange("p h b -> p (h b)"), start=i == 0, stop=i == TOP * TILES - 1)
            last.then_inc(s_held, 1)
            pe.wait_ge(s_gt, 4)
            for part in range(4):
                if part:
                    pe.wait_ge(s_acc, part)
                for t in range(TG):
                    i = TG * part + t
                    last = mm(ps[:, 4 + t, 0:C], gate_t[:, P * i:P * i + P], b2_sb[:], start=True, stop=True)
                last.then_inc(s_gb, 1)
            pe.wait_ge(s_acc, 4)
            w1_flat = w1.rearrange("p e a b -> p (e a b)")
            w2_all = w2.rearrange("p e a b -> p (e a b)")

            def expert_of(s):
                return t_.value_load(slot_expert[0:1, bass.ds(s, 1)], min_val=0, max_val=E - 1)

            def x_transposes(s, half):
                pe.wait_ge(s_xc, s + 1)
                for k in range(KT):
                    last = transpose(ps[0:KC, 2, P * k:P * k + P], x_cur[half][:, KC * k:KC * k + KC], P)
                last.then_inc(s_xt_ps, 1)

            def first_product(s, half, e):
                pe.wait_ge(s_w1, e + 1)
                pe.wait_ge(s_xt, s + 1)
                if not isinstance(s, int) or s:
                    pe.wait_ge(s_hr, s)
                for h in range(2):
                    for k in range(KT):
                        last = mm(ps[:, h, 0:HH], slot_x_t[half][0:KC + k, k, :],
                                  w1_flat[0:KC + k, bass.ds(e * (KT * H) + (k * H + h * HH), HH)], start=k == 0, stop=k == KT - 1)
                last.then_inc(s_h_ps, 1)

            def second_product(s, half, e):
                pe.wait_ge(s_w2, e + 1)
                pe.wait_ge(s_h, s + 1)
                if not isinstance(s, int) or s:
                    pe.wait_ge(s_y, s)
                for j in range(HB):
                    last = mm(ps[:, 3, 0:C], h_t[half][:, j, :], w2_all[:, bass.ds(e * (HB * C) + j * C, C)], start=j == 0, stop=j == HB - 1)
                last.then_inc(s_o2, 1)

            def h_transposes(s, half):
                pe.wait_ge(s_hr, s + 1)
                if not isinstance(s, int) or s:
                    pe.wait_ge(s_h, s)
                for j in range(HB):
                    last = transpose(ps[:, 4 + j // 3, P * (j % 3):P * (j % 3) + P], h_pos[half][:, P * j:P * j + P], P)
                last.then_inc(s_ht_ps, 1)
            pe.wait_ge(s_dst, 1)
            pe.wait_ge(s_one, 1)
            pe.wait_ge(s_bias, 32)
            pe.sem_inc(s_ht_ps, 2)
            x_transposes(0, 0)
            first_product(0, 0, expert_of(0))
            x_transposes(1, 1)
            h_transposes(0, 0)

            def slot(s, half):
                first_product(s, half, expert_of(s))
                if not (isinstance(s, int) and s == SLOTS - 1):
                    x_transposes(s + 1, 1 - half)
                second_product(s - 1, 1 - half, expert_of(s - 1))
                h_transposes(s, half)
            with pe.Fori(0, (SLOTS - 3) // 2) as pair:
                for i in range(2):
                    slot(2 * pair + 1 + i, 1 - i)
            slot(SLOTS - 2, 1)
            slot(SLOTS - 1, 0)
            second_product(SLOTS - 1, 0, expert_of(SLOTS - 1))


def _positions():
    import numpy as np
    depth = C // 2
    depths = (np.arange(depth, dtype=np.float32) / np.float32(depth))[None, :]
    rates = (np.float32(1.0) / np.power(np.float32(10000.0), depths)).astype(np.float32)
    rad = np.arange(SEQ, dtype=np.float32)[:, None] * rates
    table = np.concatenate([np.sin(rad), np.cos(rad)], axis=-1).astype(np.float32)
    return np.ascontiguousarray(table.reshape(SEQ // P, P, C).transpose(1, 0, 2))


def kernel(**inputs):
    import numpy as np
    import concourse.bacc as bacc
    from concourse.bass_utils import run_bass_kernel_spmd

    a = {k.replace("L0_", ""): np.asarray(v) for k, v in inputs.items()}

    def per_channel(m, blocks):
        return m.reshape((blocks, m.shape[0] // blocks) + m.shape[1:]).swapaxes(0, 1)

    def per_expert(m, blocks):
        return m.reshape(E, blocks, m.shape[1] // blocks, m.shape[2]).transpose(0, 2, 1, 3)

    chan = np.concatenate([a["attn_conv_w"], a["attn_conv_b"][:, None], a["attn_dt_b"].T,
                           a["attn_A_log"].transpose(1, 0, 2).reshape(DI, 2 * NS), a["attn_D_skip"].T], axis=1)
    arrays = {
        "tok": a["x"].reshape(TILES, P).T,
        "emb": a["tok_emb_table"],
        "spos": np.stack([a["tok_spos0"], a["tok_spos1"]]).reshape(1, -1),
        "pos": _positions(),
        "chan": per_channel(chan, DB),
        "w_in": per_channel(a["attn_W_in"], KT),
        "gb_in": per_channel(np.stack([a["attn_gamma_in"], a["attn_beta_in"]], axis=1), KT),
        "xproj": a["attn_x_proj_w"].reshape(2, DB, P, RANK + 2 * NS).transpose(2, 0, 1, 3),
        "dt_w": a["attn_dt_w"],
        "gb_out": np.concatenate([a["attn_gamma_out"], a["attn_beta_out"]]).reshape(1, -1),
        "w_out": per_channel(a["attn_W_out"], DB),
        "merge": a["attn_merge_w"].reshape(1, 2),
        "w_route": per_channel(np.concatenate([a["ffn_router_w"].T, a["ffn_probe_w"].T], axis=1), KT),
        "emb_t": np.concatenate([a["ffn_router_emb"].T, a["ffn_probe_w"]], axis=1),
        "energy": a["ffn_energy"].reshape(1, E),
        "fatigue": a["ffn_fatigue"].reshape(1, E),
        "gates12": np.concatenate([a["ffn_m_gate1"], a["ffn_m_gate2"]]).reshape(1, 2 * E),
        "b1": a["ffn_b1"].reshape(1, E, H),
        "b2": a["ffn_b2"],
        "wf1": per_expert(a["ffn_w_fast1"], KT),
        "ws1": per_expert(a["ffn_w_slow1"], KT),
        "hf1": per_expert(a["ffn_h_fast1"], KT),
        "wf2": per_expert(a["ffn_w_fast2"], HB),
        "ws2": per_expert(a["ffn_w_slow2"], HB),
        "hf2": per_expert(a["ffn_h_fast2"], HB),
    }
    arrays = {k: np.ascontiguousarray(m) for k, m in arrays.items()}
    nc = bacc.Bacc("TRN2", target_bir_lowering=False, num_devices=1)
    aps = {k: nc.dram_tensor(k, m.shape, mybir.dt.from_np(m.dtype), kind="ExternalInput").ap() for k, m in arrays.items()}
    out = nc.dram_tensor("out", (TOK, C), FP32, kind="ExternalOutput").ap()
    gates_dram = nc.dram_tensor("gates_dram", (NG, P, GATE_W), FP32, kind="Internal").ap()
    b_rows = nc.dram_tensor("b_rows", (2, NG * NS, GT), FP32, kind="Internal").ap()
    x_rows = nc.dram_tensor("x_rows", (TOK, C), FP32, kind="Internal").ap()
    y_rows = nc.dram_tensor("y_rows", (TOP * TOK + SLOTS * P, C), FP32, kind="Internal").ap()
    build(nc, gates_dram=gates_dram, b_rows=b_rows, x_rows=x_rows, y_rows=y_rows, out=out, **aps)
    r = run_bass_kernel_spmd(nc, [arrays], core_ids=[0])
    return r.results[0]["out"].reshape(BATCH, SEQ, C)
```

```python
import concourse.bass as bass
from concourse import mybir
from contextlib import ExitStack

FP32 = mybir.dt.float32
BF16 = mybir.dt.bfloat16
I32 = mybir.dt.int32
U32 = mybir.dt.uint32
ALU = mybir.AluOpType
ACT = mybir.ActivationFunctionType
AX = mybir.AxisListType

P = 128
BATCH, SEQ = 8, 256
TOK = BATCH * SEQ
TILES = TOK // P
SUB = 64
NPOS = 3
C = 192
KT, KC = 2, C // 2
DI = 384
DB = DI // P
NS = 16
RANK = 12
GT = 512
NG = TOK // GT
TG = GT // P
SG = GT // SEQ
NQ, QN = 4, 4
E, H = 8, 768
HB = H // P
HT = TILES // 2
STATES, DECAYS = 4, 3
SP = 3
DR = 24
RC = E + DR + 1 + E
EPS = 1e-5
CH_CONV, CH_CB, CH_DTB, CH_ALOG, CH_D = 0, 3, 4, 6, 38
CH = 40
SHIFT = P.bit_length() - 1
PER_QUAD = 2 * DB
TOP = 2
SLOTS = (TOP * TOK - E) // P + E
BATCHES = (0, 2, 8, 16, 24, 32, SLOTS)
HH = H // 2
GATE_W = 2 * TG * DI


class Steps:

    def __init__(self, eng, sem, base=0):
        self.eng, self.sem, self.base, self.n = eng, sem, base, 0

    def __call__(self, ins):
        ins.then_inc(self.sem, 1)
        self.n += 1

    def wait(self):
        self.eng.wait_ge(self.sem, self.base + self.n)

    def then(self, ins):
        self(ins)
        self.wait()


def build(nc, tok, emb, spos, pos, chan, w_in, gb_in, xproj, dt_w, gb_out, w_out, merge, w_route, emb_t,
          energy, fatigue, gates12, b1, b2, wf1, ws1, hf1, wf2, ws2, hf2, gates_dram, b_rows, x_rows, y_rows, out):
    ctx = ExitStack()
    with ctx:
        def sb(name, shape, dt=FP32):
            return ctx.enter_context(nc.sbuf_tensor(name, shape, dt))

        def sem(name):
            return ctx.enter_context(nc.semaphore(name))

        tok_sb = sb("tok_sb", [P, TILES], I32)
        ident = sb("ident", [P, P])
        pick = sb("pick", [96, 32], BF16)
        chan_sb = sb("chan_sb", [P, DB, CH])
        neg_a = sb("neg_a", [P, DB, 2, NS])
        d_merged = sb("d_merged", [P, DB])
        skip = sb("skip", [P, DB, P])
        gb_in_sb = sb("gb_in_sb", [KC, KT, 2])
        merge_sb = sb("merge_sb", [P, 2])
        row_scale = sb("row_scale", [96, 1])
        w_route_sb = sb("w_route_sb", [KC, KT, RC])
        emb_t_sb = sb("emb_t_sb", [DR, E])
        energy_sb = sb("energy_sb", [P, E])
        fatigue_sb = sb("fatigue_sb", [P, E])
        mg_sb = sb("mg_sb", [P, 2, E])
        b2_sb = sb("b2_sb", [E, C])
        eps_sb = sb("eps_sb", [P, 1])
        zeros = sb("zeros", [P, QN, SG])
        ones = sb("ones", [P, P])
        iota_e = sb("iota_e", [P, E])
        iota_i = sb("iota_i", [P, E], I32)
        iota_p = sb("iota_p", [P, P])
        iota_pi = sb("iota_pi", [P, P], I32)
        before = sb("before", [P, P])
        row_ii = sb("row_ii", [P, TOP, TILES], I32)
        row_lo_i = sb("row_lo_i", [P, TOP, TILES], I32)
        row_lo = sb("row_lo", [P, TOP, TILES])
        row_id = sb("row_id", [P, TOP, TILES])
        row_hi = sb("row_hi", [P, TOP, TILES])
        spare = sb("spare", [P, SLOTS])
        spare_i = sb("spare_i", [P, SLOTS], I32)

        ln_in = sb("ln_in", [P, TILES, C])
        ln_flat = ln_in[:].rearrange("p a b -> p (a b)")
        resid = sb("resid", [P, TILES, C])
        stats = sb("stats", [P, TILES, 6])
        mv = sb("mv", [P, TILES, 2])
        rs = sb("rs", [P, TILES])
        mv2 = sb("mv2", [P, TILES, 2])
        rs2 = sb("rs2", [P, TILES])
        nt1 = sb("nt1", [P, TILES])
        nt2 = sb("nt2", [P, TILES])
        gain = sb("gain", [P, E])
        gain_r = sb("gain_r", [P, E])
        gain_p = sb("gain_p", [P, E])
        gain_1 = sb("gain_1", [P, E])
        bias_e = sb("bias_e", [P, E])
        emb_sq = sb("emb_sq", [DR, E])
        y_sum = sb("y_sum", [P, TILES])
        y_neg = sb("y_neg", [P, TILES])
        y_sq = sb("y_sq", [P, TILES])

        ARENA = 41984
        arena = sb("arena", [P, ARENA])
        used = [0]

        def cut(shape, dt=FP32, parts=P):
            n = 1
            for s in shape:
                n *= s
            words = n if dt != BF16 else n // 2
            assert used[0] + words <= ARENA, used[0]
            v = arena[0:parts, used[0]:used[0] + words]
            used[0] += words
            if dt != FP32:
                v = v.bitcast(dt)
            if len(shape) == 2:
                v = v.rearrange("p (a b) -> p a b", b=shape[1])
            if len(shape) == 3:
                v = v.rearrange("p (a b c) -> p a b c", b=shape[1], c=shape[2])
            if len(shape) == 4:
                v = v.rearrange("p (a b c d) -> p a b c d", b=shape[1], c=shape[2], d=shape[3])
            return v

        u_all = [cut([DB, GT]) for _ in range(NG)]
        y_all = [m.rearrange("p a b -> p (a b)").rearrange("p (t d) -> p t d", d=DI) for m in u_all]
        temps = used[0]
        dt_all = [[cut([DB, GT]) for _ in range(2)] for _ in range(NG)]
        c_all = cut([NG, GT], BF16, parts=96)
        fronts = used[0]
        b_bc = [cut([QN, GT]) for _ in range(2)]
        decay = [cut([QN, GT]) for _ in range(DECAYS)]
        state = [cut([QN, GT]) for _ in range(STATES)]
        prod = [cut([QN, GT]) for _ in range(2)]
        dtu = [ln_flat[:, DB * GT * d:DB * GT * (d + 1)].rearrange("p (b t) -> p b t", b=DB) for d in range(2)]
        used[0] = temps
        conv = [cut([DB, GT]) for _ in range(2)]
        sz = [cut([TG, DI]) for _ in range(2)]
        gate_in = [cut([2, TG, DI]) for _ in range(2)]
        used[0] = fronts
        w_in_sb = cut([KT, 2 * DI], parts=KC)
        pos_sb = cut([2, C])
        spos_sb = cut([2, NPOS, SUB])
        w_probe = cut([C], parts=DR)
        w_x = cut([DB, P])
        dt_w_sb = cut([DI], parts=64)
        gb_out_sb = cut([2, DI])
        after_params = used[0]
        rows = cut([TILES, SUB])
        sel_d = cut([TILES, 2, NPOS])
        sel_e = cut([TILES, 2, NPOS])
        sel_w = cut([TILES, 2, NPOS])
        sel_m = cut([TILES, 2])
        sel_s = cut([TILES, 2])
        sel_r = cut([TILES, 2])
        mix = [cut([HT, SUB]) for _ in range(2)]
        used[0] = after_params
        lb = [cut([GT], parts=96) for _ in range(2)]
        c_rest = cut([GT])[96:P]
        c_parts = [[cut([GT], BF16)[96:P] for _ in range(3)] for _ in range(2)]
        sp_pos, sp_e, sp_w = zip(*[[cut([DB, GT]) for _ in range(3)] for _ in range(SP)])
        used[0] -= 3 * DB * GT
        xn = [cut([TG, C]) for _ in range(2)]
        xn_t = [cut([KT, GT], parts=KC) for _ in range(2)]

        used[0] = 0
        slot_rows = cut([SLOTS, C])
        slot_flat = slot_rows.rearrange("p a b -> p (a b)")
        HOT_B, HOT_A = TOP * TILES * P // 2, TOP * TILES * SLOTS
        PART = TOP * TILES // 4
        hot_b = slot_flat[:, 0:HOT_B].bitcast(BF16).rearrange("p (a b) -> p a b", b=P)
        hot_a = slot_flat[:, HOT_B:HOT_B + HOT_A].bitcast(BF16).rearrange("p (a h b) -> p a h b", b=SLOTS, h=2)
        is_slot = slot_flat[:, HOT_B + HOT_A:HOT_B + 2 * HOT_A].rearrange("p (a b) -> p a b", b=SLOTS)
        w1_at = used[0]
        w1 = cut([E, KT, H], parts=KC + 1)
        w2_at = used[0]
        w2 = cut([E, HB, C])
        raw1 = [cut([KT, H], parts=KC) for _ in range(3)]
        raw2 = [cut([HB, C]) for _ in range(3)]
        slot_x_t = [cut([KT, P], parts=KC + 1) for _ in range(2)]
        x_cur = [cut([C]) for _ in range(2)]
        routed = cut([TILES, RC])
        w_out_sb = cut([DB, C])
        rt = {n: cut([TILES, E]) for n in ("a", "b", "logit", "top", "hot0", "hot1", "gate", "f")}
        rt_i = cut([TILES, E], U32)
        rt_sq = cut([TILES, DR])
        tables = used[0]
        rt_1 = {n: sb("rt1_" + n, [P, TILES]) for n in ("n2", "n", "m", "r", "tp", "d", "e", "s", "g0", "g1")}
        w2_flat = w2.rearrange("p a b c -> p (a b c)")

        def y_back(g):
            return w2_flat[:, TG * TOP * C * g:TG * TOP * C * (g + 1)].rearrange("p (t c) -> p t c", t=TG)
        LATE = E // 2
        used[0] = w1_at + LATE * KT * H
        gate_even, gate_odd = (cut([2, TG, DI]) for _ in range(2))
        assert used[0] <= w2_at
        used[0] = temps
        gate_back = [cut([2, TG, DI]), gate_odd, gate_even, gate_odd]
        used[0] = w2_at + LATE * HB * C
        y_t = [cut([DB, GT]) for _ in range(2)]
        x_g = [cut([TG, C]) for _ in range(2)]
        assert used[0] <= w2_at + E * HB * C
        x_g_t = [ln_flat[0:KC, KT * GT * i:KT * GT * (i + 1)].rearrange("p (k t) -> p k t", k=KT) for i in range(2)]
        h_pos = [ln_flat[:, H * i:H * i + H] for i in range(2)]
        h_t = [ln_flat[:, H * (2 + i):H * (3 + i)].rearrange("p (a b) -> p a b", b=P) for i in range(2)]
        gate_t = ln_flat[0:E, 0:TOK]
        by_et = [ln_flat[:, TOK + E * TILES * i:TOK + E * TILES * (i + 1)] for i in range(8)]
        tot, run_tot, offs, not_first = (m.rearrange("p (e t) -> p e t", e=E) for m in by_et[0:4])
        full, hots, *picked = (m.rearrange("p (t e) -> p t e", e=E) for m in by_et[4:8])
        used[0] = tables
        B2_BANKS, B2_AT = (3, 4, 5, 6, 7, 0, 1, 2), P
        where_f, slot_f, place_f = (cut([TOP, TILES]) for _ in range(3))
        where_i, slot_i, place_i = (cut([TOP, TILES], I32) for _ in range(3))
        past = cut([SLOTS, E], parts=1)
        past_n = cut([SLOTS], parts=1)
        slot_expert = cut([SLOTS], I32, parts=1)
        cnt_i, cnt_s = (cut([E], I32) for _ in range(2))
        n_slots, end_slot, base_row = (cut([E]) for _ in range(3))
        held = cut([SLOTS])
        empty = cut([SLOTS])
        empty_s = cut([SLOTS])
        src_2 = cut([SLOTS], I32)
        src_row = cut([SLOTS], I32)
        dst_row = cut([SLOTS], I32)

        ps = ctx.enter_context(nc.psum_tensor("ps", [P, 8, 512], FP32))
        Y, BCAST = 0, 3
        y_ps = ps[:, Y:Y + DB, :].rearrange("p a b -> p (a b)")

        s_tok = sem("tokens_loaded")
        s_front = sem("front_loaded")
        s_par = sem("params_loaded")
        s_rows = [sem("rows_gathered_0"), sem("rows_gathered_1")]
        s_ln_in = sem("layer_norm_variance_ready")
        s_rstd_in = sem("layer_norm_rstd_ready")
        s_ident = sem("ident_ready")
        s_setup_v = sem("setup_vector")
        v_step = sem("vector_step")
        a_step = sem("scalar_step")
        p_step = sem("pool_step")
        s_sel_d = sem("select_logits_ready")
        s_sel_e = sem("select_exp_ready")
        s_sel_w = sem("select_weights_ready")
        s_cp = sem("row_copied")
        s_mix1 = sem("second_mix_ready")
        s_ln = sem("variance_ready")
        s_rstd = sem("rstd_ready")
        s_lnin = sem("ln_in_ready")
        s_res = sem("resid_ready")
        s_nega = sem("decay_rate_exp_ready")
        s_xn = sem("xn_ready")
        s_xn_ps = sem("xn_transposed")
        s_xn_t = sem("xn_t_ready")
        s_xi = sem("xi_ready")
        s_z = sem("z_ready")
        s_sz = sem("sz_ready")
        s_conv = sem("conv_ready")
        s_u = sem("u_ready")
        s_split = sem("bc_split_ready")
        s_dt_ps = sem("dt_product")
        s_pos = sem("softplus_pos_ready")
        s_e = sem("softplus_exp_ready")
        s_c = sem("softplus_corr_ready")
        s_rc = sem("softplus_pos_corrected")
        s_l = sem("softplus_log_ready")
        s_lb_ps = sem("dt_and_b_product")
        s_lb = sem("dt_and_b_rows_ready")
        s_stack = [sem("c_parts_stacked_0"), sem("c_parts_stacked_1")]
        s_gate_in = sem("gate_terms_ready")
        s_gate_st = [sem("gate_terms_stored_0"), sem("gate_terms_stored_1")]
        s_gate_ld = [sem(f"gate_terms_loaded_{i}") for i in range(4)]
        s_b_st = [sem("b_rows_stored_0"), sem("b_rows_stored_1")]
        s_b_ld = [sem("b_forward_loaded"), sem("b_backward_loaded")]
        s_dt = sem("dt_ready")
        s_skip = sem("skip_diagonals_ready")
        s_w_out = sem("w_out_loaded")
        s_yv = sem("y_left_banks")
        s_added = sem("layer_output_added")
        s_ln2 = sem("expert_norm_variance_ready")
        s_rstd2 = sem("expert_norm_rstd_ready")
        s_rstd_y = sem("y_norm_rstd_ready")
        s_ln_y = sem("y_norm_variance_ready")
        s_x = sem("dtu_ready")
        s_c_ps = sem("c_broadcast_ready")
        s_decay = sem("decay_ready")
        s_in = sem("scan_input_ready")
        s_scan = sem("scan_done")
        s_mul = sem("c_multiplied")
        s_sum = sem("y_summed")
        s_yn = sem("y_normed")
        s_yt_ps = sem("y_transposed")
        s_yt = sem("y_t_ready")
        s_o_ps = sem("out_product")
        s_xg = sem("x_g_ready")
        s_xg_ps = sem("x_g_transposed")
        s_xg_t = sem("x_g_t_ready")
        s_r_ps = sem("router_product")
        s_r = sem("router_sums_kept")
        s_nrm = sem("norms_summed")
        s_nrm_r = sem("norms_rooted")
        s_gd = sem("gate_difference_ready")
        s_ge = sem("gate_exp_ready")
        s_gate = sem("gates_ready")
        s_gt_ps = sem("gates_transposed")
        s_gt = sem("gates_t_ready")
        s_counted = sem("counts_read")
        s_acc = sem("accumulator_started")
        s_raw1 = sem("raw_first_weights_loaded")
        s_raw2 = sem("raw_second_weights_loaded")
        s_w1 = sem("first_weights_ready")
        s_w2 = sem("second_weights_ready")
        s_scaled = sem("second_outputs_scaled")
        s_bias = sem("bias_row_loaded")
        s_xs = [sem("expert_inputs_stored_0"), sem("expert_inputs_stored_1")]
        s_hots = sem("hots_ready")
        s_cnt = sem("counts_product")
        s_place = sem("places_ready")
        s_held = sem("held_product")
        s_src = sem("source_rows_ready")
        s_dst = sem("slot_tables_ready")
        s_gather = sem("slot_gather_done")
        s_slot_in = sem("slots_gathered")
        s_one = sem("bias_ones_ready")
        s_xc = sem("slot_input_copied")
        s_xt_ps = sem("slot_input_transposed")
        s_xt = sem("slot_input_t_ready")
        s_h_ps = sem("hidden_product")
        s_hr = sem("hidden_relu")
        s_ht_ps = sem("hidden_transposed")
        s_h = sem("hidden_ready")
        s_o2 = sem("expert_product")
        s_y = sem("slot_output_ready")
        s_scatter = sem("slot_scatter_done")
        s_back = [sem(f"outputs_back_{i}") for i in range(4)]
        s_final = sem("group_final")
        s_esq = sem("embedding_squared")
        s_rset = sem("router_setup_product")
        s_wr = sem("router_weights_ready")
        s_store = sem("stored")
        s_passed = sem("waits_passed")
        FRONT_LOADS, PAR_LOADS = 2, 22
        DT_BANK = 2
        MUL0, SUM0 = STATES, 2

        def alone(eng):
            eng.sem_inc(s_passed, 1)

        block = ctx.enter_context(nc.Block())

        @block.sync
        def _(sp):
            sp.dma_start(tok_sb[:], tok).then_inc(s_tok, 16)
            sp.dma_start(spos_sb.rearrange("p a b c -> p (a b c)"), spos.to_broadcast([P, 2 * NPOS * SUB])).then_inc(s_front, 16)
            sp.dma_start(pos_sb, pos).then_inc(s_front, 16)
            sp.wait_ge(s_setup_v, 1)
            loads = [(chan_sb[:], chan), (w_in_sb, w_in), (gb_in_sb[:], gb_in),
                     (dt_w_sb[0:RANK, :], dt_w[0]), (dt_w_sb[32:32 + RANK, :], dt_w[1]),
                     (merge_sb[:], merge.to_broadcast([P, 2])),
                     (gb_out_sb.rearrange("p a b -> p (a b)"), gb_out.to_broadcast([P, 2 * DI]))]
            for d in range(2):
                loads.append((row_scale[64 + NS * d:64 + NS * (d + 1), :], merge[:, d:d + 1].to_broadcast([NS, 1])))
                for at, first, n in ((32 * d, 0, RANK), (64 + NS * d, RANK, NS), (96 + NS * d, RANK + NS, NS)):
                    loads.append((w_x[:, :, at:at + n], xproj[:, d, :, first:first + n]))
            loads += [(w_route_sb[:, :, 0:E + DR], w_route), (emb_t_sb[:], emb_t[0:DR, 0:E]), (w_probe, emb_t[0:DR, E:E + C]),
                      (energy_sb[:], energy.to_broadcast([P, E])), (fatigue_sb[:], fatigue.to_broadcast([P, E])),
                      (mg_sb[:].rearrange("p a b -> p (a b)"), gates12.to_broadcast([P, 2 * E])),
                      (b2_sb[:], b2)]
            assert len(loads) == PAR_LOADS, len(loads)
            for dst, src in loads:
                sp.dma_start(dst, src).then_inc(s_par, 16)
            for g in range(NG):
                sp.wait_ge(s_gate_in, g + 1)
                sp.dma_start(gates_dram[g], gate_in[g % 2].rearrange("p a b c -> p (a b c)")).then_inc(s_gate_st[g % 2], 16)
            for g in range(NG):
                sp.wait_ge(s_lb, g + 1)
                for d in range(2):
                    sp.dma_start(b_rows[d, NS * g:NS * (g + 1), :], lb[g % 2][64 + NS * d:64 + NS * (d + 1), :]).then_inc(s_b_st[g % 2], 16)
                sp.wait_ge(s_split, g + 1)
                for r in range(3):
                    sp.dma_start(c_all[32 * r:32 * (r + 1), g, :], c_parts[g % 2][r]).then_inc(s_stack[g % 2], 16)
            for i in range(2):
                sp.wait_ge(s_b_st[i], 32 * NG // 2)
                sp.wait_ge(s_stack[i], 48 * NG // 2)

            def load_b(G, d):
                sp.dma_start(b_bc[d].rearrange("p n t -> p (n t)"),
                             b_rows[d, bass.ds(QN * G, QN), :].rearrange("(o n) t -> o (n t)", o=1).to_broadcast([P, QN * GT])).then_inc(s_b_ld[d], 16)
            sp.wait_ge(s_dt_ps, NG * 2 * DB)
            load_b(0, 0)
            sp.wait_ge(s_rset, 1)
            load_b(0, 1)

            def load_quads(first, end):
                with sp.Fori(first, end) as G:
                    for d in range(2):
                        sp.wait_ge(s_in, PER_QUAD * G + DB * d - DB)
                        load_b(G, d)
            load_quads(1, 2 * NQ)
            sp.wait_ge(s_scan, PER_QUAD * (NQ + 1))
            sp.dma_start(gate_back[0].rearrange("p a b c -> p (a b c)"), gates_dram[0]).then_inc(s_gate_ld[0], 16)
            load_quads(2 * NQ, NG * NQ)
            sp.wait_ge(s_sum, SUM0 + NG * NQ * PER_QUAD)
            def load_first(e):
                for k, src in enumerate((wf1, ws1, hf1)):
                    sp.dma_start(raw1[k], src[bass.ds(e, 1), :, :, :].rearrange("e p a b -> (e p) a b")).then_inc(s_raw1, 16)

            def load_second(e):
                for k, src in enumerate((wf2, ws2, hf2)):
                    sp.dma_start(raw2[k], src[bass.ds(e, 1), :, :, :].rearrange("e p a b -> (e p) a b")).then_inc(s_raw2, 16)
            load_first(0)
            load_second(0)
            with sp.Fori(1, E) as e:
                sp.wait_ge(s_w1, e)
                load_first(e)
                sp.wait_ge(s_w2, e)
                load_second(e)
            sp.wait_ge(s_o2, SLOTS + 1)
            sp.wait_ge(s_scatter, 16 * SLOTS)
            for g in range(NG):
                sp.dma_start(y_back(g), y_rows[TOP * GT * g:TOP * GT * (g + 1), :].rearrange("(t p k) c -> p t (k c)", p=P, k=TOP)).then_inc(s_back[g], 16)
            for g in range(NG):
                sp.wait_ge(s_final, g + 1)
                sp.dma_start(out[GT * g:GT * (g + 1), :].rearrange("(t p) c -> p t c", p=P), resid[:, TG * g:TG * (g + 1), :]).then_inc(s_store, 16)
            sp.wait_ge(s_store, 16 * NG)

        @block.gpsimd
        def _(pool):
            g_ = nc.gpsimd
            st = Steps(pool, p_step)
            pool.wait_ge(s_tok, 16)
            for t in range(TILES):
                g_.indirect_dma_start(out=rows[:, t, :], out_offset=None, in_=emb,
                                      in_offset=bass.IndirectOffsetOnAxis(ap=tok_sb[:, t:t + 1].bitcast(U32), axis=0)).then_inc(s_rows[t // HT], 16)
            st(g_.memset(ident[:], 0.0))
            st(g_.memset(pick[:], 0.0))
            st.wait()
            g_.affine_select(out=ident[:], in_=ident[:], compare_op=ALU.not_equal, fill=1.0, base=0,
                             pattern=[[-1, P]], channel_multiplier=1).then_inc(s_ident, 1)
            for r in range(3):
                st.then(g_.affine_select(out=pick[:], in_=pick[:], compare_op=ALU.not_equal, fill=1.0, base=-32 * r,
                                         pattern=[[-1, 32]], channel_multiplier=1))
            st(g_.memset(before[:], 1.0))
            st(g_.iota(iota_i[:], pattern=[[1, E]], base=0, channel_multiplier=0))
            st(g_.iota(iota_pi[:], pattern=[[1, P]], base=0, channel_multiplier=0))
            st(g_.iota(row_ii[:], pattern=[[1, TOP], [TOP * P, TILES]], base=1, channel_multiplier=TOP))
            st(g_.iota(spare_i[:], pattern=[[P, SLOTS]], base=TOP * TOK + 1, channel_multiplier=1))
            st.wait()
            g_.affine_select(out=before[:], in_=before[:], compare_op=ALU.is_ge, fill=0.0, base=-1,
                             pattern=[[1, P]], channel_multiplier=-1).then_inc(s_ident, 1)
            pool.wait_ge(s_sel_w, 2)
            pool.wait_ge(s_front, 16 * FRONT_LOADS)
            half = slice(HT, TILES)
            dst = ln_in[:, half, 2 * SUB:3 * SUB]
            for k in range(NPOS):
                o = dst if k == 0 else mix[1]
                st.then(g_.tensor_tensor(o, spos_sb[:, 1:2, k, :].to_broadcast([P, HT, SUB]),
                                         sel_w[:, half, 1, k:k + 1].to_broadcast([P, HT, SUB]), ALU.mult))
                if k:
                    ins = g_.tensor_tensor(dst, dst, mix[1], ALU.add)
                    if k == NPOS - 1:
                        ins.then_inc(s_mix1, 1)
                    else:
                        st.then(ins)
            for h in range(2):
                half = slice(HT * h, HT * (h + 1))
                pool.wait_ge(s_lnin, h + 1)
                g_.tensor_tensor(resid[:, half, :], resid[:, half, :], ln_in[:, half, :], ALU.add).then_inc(s_res, 1)
            pool.wait_ge(s_par, 16 * PAR_LOADS)
            for g in range(NG):
                pool.wait_ge(s_sz, TG * (g + 1))
                if g >= 2:
                    pool.wait_ge(s_gate_st[g % 2], 16)
                for i in range(2):
                    last = g_.tensor_tensor(gate_in[g % 2][:, i], sz[g % 2], gb_out_sb[:, i:i + 1, :].to_broadcast([P, TG, DI]), ALU.mult)
                last.then_inc(s_gate_in, 1)
            for n in range(2 * NG):
                pool.wait_ge(s_c, n + 1)
                g_.tensor_tensor(sp_pos[n % SP], sp_pos[n % SP], sp_w[n % SP], ALU.subtract).then_inc(s_rc, 1)
            pool.wait_ge(s_dt, 2 * NG)
            with pool.Fori(0, NG) as g:
                for q in range(NQ):
                    for k in range(PER_QUAD):
                        i = PER_QUAD * q + k
                        d, blk = divmod(k, DB)
                        if blk == 0:
                            pool.wait_ge(s_b_ld[d], g * (16 * NQ) + 16 * (q + 1))
                            pool.wait_ge(s_x, 2 * g + d + 1)
                        pool.wait_ge(s_mul, g * (NQ * PER_QUAD) + i + 1)
                        g_.tensor_tensor(state[i % STATES], dtu[d][:, blk:blk + 1, :].to_broadcast([P, QN, GT]),
                                         b_bc[d], ALU.mult).then_inc(s_in, 1)

            def combine(e):
                for raw, w, parts, row, loaded, made in ((raw1, w1, KC, 0, s_raw1, s_w1), (raw2, w2, P, 1, s_raw2, s_w2)):
                    f, s, h = (m.rearrange("p a b -> p (a b)") for m in raw)
                    n = w.shape[2] * w.shape[3]
                    flat = w.rearrange("p e a b -> p (e a b)")[0:parts]
                    pool.wait_ge(loaded, 48 * (e + 1))
                    st.then(g_.tensor_tensor(s, s, mg_sb[0:parts, row, e:e + 1].to_broadcast([parts, n]), ALU.mult))
                    st.then(g_.tensor_tensor(s, s, f, ALU.add))
                    g_.tensor_tensor(flat[:, n * e:n * (e + 1)], s, h, ALU.add).then_inc(made, 1)

            def gather(first, end):
                for s in range(first, end):
                    g_.indirect_dma_start(out=slot_rows[:, s, :], out_offset=None, in_=x_rows,
                                          in_offset=bass.IndirectOffsetOnAxis(ap=src_row[:, s:s + 1].bitcast(U32), axis=0)).then_inc(s_gather, 16)

            pool.wait_ge(s_yn, 1)
            for e in range(LATE):
                combine(e)
            pool.wait_ge(s_src, 1)
            for i in range(2):
                pool.wait_ge(s_xs[i], 16 * NG // 2)
            for b, (first, end) in enumerate(zip(BATCHES, BATCHES[1:])):
                gather(first, end)
                pool.wait_ge(s_gather, 16 * end)
                pool.sem_inc(s_slot_in, end - first)
                if b >= 1 and LATE + b - 1 < E:
                    combine(LATE + b - 1)
            pool.wait_ge(s_dst, 1)
            for s in range(SLOTS):
                pool.wait_ge(s_y, s + 2)
                g_.indirect_dma_start(out=y_rows, out_offset=bass.IndirectOffsetOnAxis(ap=dst_row[:, s:s + 1].bitcast(U32), axis=0),
                                      in_=slot_rows[:, s, :], in_offset=None).then_inc(s_scatter, 16)
            pool.wait_ge(s_scatter, 16 * SLOTS)

        @block.vector
        def _(dve):
            v = nc.vector
            st = Steps(dve, v_step)
            v.memset(w_x, 0.0)
            v.memset(row_scale[:], 1.0)
            v.memset(w_route_sb[:, :, E + DR:E + DR + 1], 1.0)
            v.memset(eps_sb[:], EPS)
            v.memset(zeros[:], 0.0)
            v.memset(ones[:], 1.0).then_inc(s_setup_v, 1)
            def moments(src, t0, n, m, done):
                for t in range(n):
                    st(v.bn_stats(stats[:, t0 + t, :], src(t)))
                st.wait()
                for t in range(n):
                    last = v.bn_aggr(m[:, t0 + t, :], stats[:, t0 + t, :])
                last.then_inc(done, 1)

            def newton(t0, n, m, root):
                var, r, a, b = m[:, t0:t0 + n, 1], root[:, t0:t0 + n], nt1[:, t0:t0 + n], nt2[:, t0:t0 + n]
                st.then(v.tensor_tensor(a, r, r, ALU.mult))
                st.then(v.scalar_tensor_tensor(b, var, EPS, a, ALU.add, ALU.mult))
                st.then(v.tensor_scalar(a, b, -0.5, 1.5, ALU.mult, ALU.add))
                st.then(v.tensor_tensor(r, r, a, ALU.mult))

            def select(h):
                half = slice(HT * h, HT * (h + 1))
                dve.wait_ge(s_rows[h], 16 * HT)
                six = rows[:, half, 0:2 * NPOS].rearrange("p t (i k) -> p t i k", k=NPOS)
                st.then(v.tensor_reduce(sel_m[:, half], six, AX.X, ALU.max))
                v.tensor_tensor(sel_d[:, half], six, sel_m[:, half].unsqueeze(3).to_broadcast([P, HT, 2, NPOS]), ALU.subtract).then_inc(s_sel_d, 1)
                dve.wait_ge(s_sel_e, h + 1)
                st.then(v.tensor_reduce(sel_s[:, half], sel_e[:, half], AX.X, ALU.add))
                st.then(v.reciprocal(sel_r[:, half], sel_s[:, half]))
                v.tensor_tensor(sel_w[:, half], sel_e[:, half], sel_r[:, half].unsqueeze(3).to_broadcast([P, HT, 2, NPOS]), ALU.mult).then_inc(s_sel_w, 1)
                dve.wait_ge(s_sel_w, h + 1)
                dve.wait_ge(s_front, 16 * FRONT_LOADS)

            def mix_in(h, i):
                half = slice(HT * h, HT * (h + 1))
                dst = ln_in[:, half, SUB * (i + 1):SUB * (i + 2)]
                for k in range(NPOS):
                    o = dst if k == 0 else mix[0]
                    st.then(v.tensor_tensor(o, spos_sb[:, i:i + 1, k, :].to_broadcast([P, HT, SUB]),
                                            sel_w[:, half, i, k:k + 1].to_broadcast([P, HT, SUB]), ALU.mult))
                    if k:
                        st.then(v.tensor_tensor(dst, dst, mix[0], ALU.add))

            def embed(h):
                half = slice(HT * h, HT * (h + 1))
                dve.wait_ge(s_cp, h + 1)
                st.then(v.scalar_tensor_tensor(
                    resid[:, half, :].rearrange("p (b t) c -> p b (t c)", t=2), ln_in[:, half, :].rearrange("p (b t) c -> p b (t c)", t=2),
                    float(C) ** 0.5, pos_sb.rearrange("p t c -> p (t c)").unsqueeze(1).to_broadcast([P, BATCH // 2, 2 * C]),
                    ALU.mult, ALU.add))
                moments(lambda t: resid[:, HT * h + t, :], HT * h, HT, mv, s_ln)

            def norm_twice(h):
                half = slice(HT * h, HT * (h + 1))
                dve.wait_ge(s_rstd, h + 1)
                newton(HT * h, HT, mv, rs)
                st.then(v.tensor_tensor(nt1[:, half], rs[:, half], rs[:, half], ALU.mult))
                v.tensor_tensor(mv2[:, half, 1], mv[:, half, 1], nt1[:, half], ALU.mult).then_inc(s_ln_in, 1)
                for t in range(HT * h, HT * (h + 1)):
                    last = v.tensor_scalar(ln_in[:, t, :], resid[:, t, :], mv[:, t, 0:1], rs[:, t:t + 1], ALU.subtract, ALU.mult)
                last.then_inc(s_lnin, 1)
                dve.wait_ge(s_lnin, h + 1)
                dve.wait_ge(s_rstd_in, h + 1)
                newton(HT * h, HT, mv2, rs2)

            def norm_in(g):
                if g >= 2:
                    dve.wait_ge(s_xn_ps, g - 1)
                for t in range(TG):
                    i = g * TG + t
                    last = v.tensor_scalar(xn[g % 2][:, t, :], ln_in[:, i, :], rs2[:, i:i + 1], None, ALU.mult)
                last.then_inc(s_xn, 1)

            def constants():
                dve.wait_ge(s_nega, 1)
                st(v.tensor_scalar(neg_a[:], neg_a[:], -1.0, None, ALU.mult))
                st.then(v.tensor_scalar(d_merged[:], chan_sb[:, :, CH_D], merge_sb[:, 0:1], None, ALU.mult))
                st(v.scalar_tensor_tensor(d_merged[:], chan_sb[:, :, CH_D + 1], merge_sb[:, 1:2], d_merged[:], ALU.mult, ALU.add))
                v.tensor_tensor(emb_sq[:], emb_t_sb[:], emb_t_sb[:], ALU.mult).then_inc(s_esq, 1)
                dve.wait_ge(s_ident, 2)
                st(v.tensor_copy(iota_e[:], iota_i[:]))
                st(v.tensor_copy(iota_p[:], iota_pi[:]))
                st(v.tensor_copy(row_id[:], row_ii[:]))
                st(v.tensor_copy(spare[:], spare_i[:]))
                st.then(v.tensor_scalar(row_lo_i[:], row_ii[:], 63, None, ALU.bitwise_and))
                st.then(v.tensor_copy(row_lo[:], row_lo_i[:]))
                st(v.tensor_tensor(row_hi[:], row_id[:], row_lo[:], ALU.subtract))
                for blk in range(DB):
                    last = v.tensor_scalar(skip[:, blk, :], ident[:], d_merged[:, blk:blk + 1], None, ALU.mult)
                last.then_inc(s_skip, 1)

            select(0)
            mix_in(0, 0)
            mix_in(0, 1)
            embed(0)
            norm_twice(0)

            norm_in(0)
            norm_in(1)
            select(1)
            mix_in(1, 0)
            dve.wait_ge(s_mix1, 1)
            embed(1)
            dve.wait_ge(s_par, 16 * PAR_LOADS)
            def convolve(g):
                for blk in range(DB):
                    dve.wait_ge(s_xi, DB * g + blk + 1)
                    if g >= 2:
                        dve.wait_ge(s_u, DB * (g - 2) + blk + 1)
                    cv = conv[g % 2][:, blk, :].rearrange("p (s t) -> p s t", t=SEQ)
                    bank = ps[:, 2 + blk, :]
                    xi = bank.rearrange("p (s t) -> p s t", t=SEQ)
                    st.then(v.tensor_scalar(conv[g % 2][:, blk, :], bank, chan_sb[:, blk, 1:2], chan_sb[:, blk, CH_CB:CH_CB + 1],
                                            ALU.mult, ALU.add))
                    st.then(v.scalar_tensor_tensor(cv[:, :, 1:SEQ], xi[:, :, 0:SEQ - 1], chan_sb[:, blk, 0:1],
                                                   cv[:, :, 1:SEQ], ALU.mult, ALU.add))
                    v.scalar_tensor_tensor(cv[:, :, 0:SEQ - 1], xi[:, :, 1:SEQ], chan_sb[:, blk, 2:3],
                                           cv[:, :, 0:SEQ - 1], ALU.mult, ALU.add).then_inc(s_conv, 1)

            norm_twice(1)
            convolve(0)
            norm_in(2)
            convolve(1)
            norm_in(3)
            constants()
            convolve(2)
            convolve(3)

            def split_c(g):
                hi, mid, lo = c_parts[g % 2]
                bank = ps[96:P, 0, :]
                dve.wait_ge(s_lb_ps, g + 1)
                if g >= 2:
                    dve.wait_ge(s_stack[g % 2], 48)
                st.then(v.tensor_copy(hi, bank))
                st.then(v.tensor_tensor(c_rest, bank, hi, ALU.subtract))
                st.then(v.tensor_copy(mid, c_rest))
                v.tensor_tensor(lo, c_rest, mid, ALU.subtract).then_inc(s_split, 1)

            def correction(n):
                w, e = sp_w[n % SP], sp_e[n % SP]
                dve.wait_ge(s_e, n + 1)
                st.then(v.tensor_scalar(w, e, 1.0, None, ALU.add))
                v.scalar_tensor_tensor(w, w, -1.0, e, ALU.add, ALU.subtract).then_inc(s_c, 1)

            def dt_sum(n):
                dt = dt_all[n // 2][n % 2]
                dve.wait_ge(s_l, n + 1)
                dve.wait_ge(s_rc, n + 1)
                v.tensor_tensor(dt, sp_pos[n % SP], dt, ALU.add).then_inc(s_dt, 1)

            def times_u(g, d):
                words = DB * GT
                dt = arena[:, bass.ds(g * (2 * words) + (temps + d * words), words)]
                u = arena[:, bass.ds(g * words, words)]
                v.tensor_tensor(dtu[d].rearrange("p b t -> p (b t)"), dt, u, ALU.mult).then_inc(s_x, 1)

            for n in range(2 * NG):
                if n % 2 == 0:
                    if n:
                        dve.wait_ge(s_split, n // 2)
                    split_c(n // 2)
                correction(n)
                if n:
                    dt_sum(n - 1)
                if n == 4:
                    dve.wait_ge(s_res, 2)
                    dve.wait_ge(s_xn_ps, NG)
                    dve.wait_ge(s_dt, n)
                    times_u(0, 0)
                    times_u(0, 1)
            dve.sem_inc(s_mul, MUL0)
            dve.sem_inc(s_scan, PER_QUAD)
            dt_sum(2 * NG - 1)

            dve.wait_ge(s_dt, 2 * NG)
            for i in range(2):
                dve.wait_ge(s_b_st[i], 32 * NG // 2)
                dve.wait_ge(s_stack[i], 48 * NG // 2)

            def scan(i, g):
                n = g * (NQ * PER_QUAD) + i
                dve.wait_ge(s_decay, n + 1)
                dve.wait_ge(s_in, n + 1)
                a, x = (m.rearrange("p n t -> p (n t)") for m in (decay[i % DECAYS], state[i % STATES]))
                if i % PER_QUAD >= DB:
                    a, x = a[:, ::-1], x[:, ::-1]
                v.tensor_tensor_scan(x, a, x, 0.0, ALU.mult, ALU.add).then_inc(s_scan, 1)

            def times_c(i, g):
                n = g * (NQ * PER_QUAD) + i
                dve.wait_ge(s_scan, n + 1 + PER_QUAD)
                if i % DB == 0:
                    dve.wait_ge(s_c_ps, g * (2 * NQ) + i // DB + 1)
                dve.wait_ge(s_sum, n - 1 + SUM0)
                v.tensor_tensor(prod[i % 2], state[i % STATES], ps[:, BCAST:BCAST + QN, :], ALU.mult).then_inc(s_mul, 1)

            def scan_group(g, following=None):
                scan(0, g)
                for i in range(1, NQ * PER_QUAD):
                    scan(i, g)
                    if following is not None and i == NQ * PER_QUAD - 2:
                        dve.wait_ge(s_in, g * (NQ * PER_QUAD) + i - 1)
                        times_u(following, 0)
                    if following is not None and i == NQ * PER_QUAD - 1:
                        dve.wait_ge(s_in, g * (NQ * PER_QUAD) + i + 1)
                        times_u(following, 1)
                    times_c(i - 1, g)
                times_c(NQ * PER_QUAD - 1, g)

            with dve.Fori(0, NG - 1) as g:
                scan_group(g, following=g + 1)
            scan_group(NG - 1)

            alone(dve)
            def gate_y(g):
                dve.wait_ge(s_gate_ld[g], 16)
                for t in range(TG):
                    i = TG * g + t
                    st(v.scalar_tensor_tensor(y_all[g][:, t, :], y_all[g][:, t, :], mv[:, i, 0:1], gate_back[g][:, 0, t, :],
                                              ALU.subtract, ALU.mult))
                st.wait()
                for t in range(TG):
                    i = TG * g + t
                    last = v.scalar_tensor_tensor(y_all[g][:, t, :], y_all[g][:, t, :], rs[:, i:i + 1], gate_back[g][:, 1, t, :],
                                                  ALU.mult, ALU.add)
                last.then_inc(s_yn, 1)

            def add_layer(g):
                dve.wait_ge(s_o_ps, g + 1)
                part = resid[:, TG * g:TG * (g + 1), :]
                v.tensor_tensor(part.rearrange("p (a b) c -> p a (b c)", b=2), part.rearrange("p (a b) c -> p a (b c)", b=2),
                                ps[:, 3:5, 0:2 * C], ALU.add).then_inc(s_added, 1)
                dve.wait_ge(s_added, g + 1)
                moments(lambda t: resid[:, TG * g + t, :], TG * g, TG, mv2, s_ln2)

            def norm_x(g):
                dve.wait_ge(s_rstd2, g + 1)
                newton(TG * g, TG, mv2, rs2)
                if g >= 2:
                    dve.wait_ge(s_xg_ps, g - 1)
                    dve.wait_ge(s_xs[g % 2], 16)
                for t in range(TG):
                    i = TG * g + t
                    last = v.tensor_scalar(x_g[g % 2][:, t, :], resid[:, i, :], mv2[:, i, 0:1], rs2[:, i:i + 1], ALU.subtract, ALU.mult)
                last.then_inc(s_xg, 1)
            dve.wait_ge(s_rset, 1)
            st(v.tensor_copy(gain_1[:], ps[:, 7, 0:E]))
            st.wait()
            v.tensor_copy(w_route_sb[:, :, E + DR + 1:RC], ps[0:KC, 7, E:(1 + KT) * E].rearrange("p (k e) -> p k e", k=KT)).then_inc(s_wr, 1)
            dve.wait_ge(s_rstd_y, 1)
            newton(0, TG * (NG - 1), mv, rs)
            gate_y(0)
            dve.wait_ge(s_yv, NG)
            moments(lambda t: y_all[NG - 1][:, t, :], TG * (NG - 1), TG, mv, s_ln_y)
            for g in range(NG):
                if g + 1 == NG - 1:
                    dve.wait_ge(s_rstd_y, 2)
                    newton(TG * (NG - 1), TG, mv, rs)
                if g + 1 < NG:
                    gate_y(g + 1)
                add_layer(g)
                norm_x(g)
            for i in range(2):
                dve.wait_ge(s_xs[i], 16 * NG // 2)

            dve.wait_ge(s_r, NG)
            dve.wait_ge(s_nrm, 1)
            st(v.tensor_reduce(rt_1["n2"][:], rt_sq, AX.X, ALU.add))
            st.wait()
            dve.sem_inc(s_nrm_r, 1)
            dve.wait_ge(s_nrm_r, 3)
            st(v.tensor_scalar(rt_1["m"][:], rt_1["n"][:], 1e-12, None, ALU.max))
            st(v.tensor_scalar(gain_r[:], gain[:], 1e-12, None, ALU.max))
            st.wait()
            st(v.reciprocal(rt_1["r"][:], rt_1["m"][:]))
            st(v.reciprocal(gain_1[:], gain_r[:]))
            st(v.tensor_scalar(rt_1["tp"][:], routed[:, :, E + DR], 0.02 / C, None, ALU.mult))
            st(v.tensor_scalar(gain_p[:], gain[:], 1.0, None, ALU.add))
            st(v.tensor_tensor(bias_e[:], energy_sb[:], fatigue_sb[:], ALU.subtract))
            st.wait()

            def by_tile(m):
                return m[:].unsqueeze(2).to_broadcast([P, TILES, E])

            def by_expert(m):
                return m[:].unsqueeze(1).to_broadcast([P, TILES, E])
            st(v.tensor_tensor(rt["a"], by_tile(rt_1["tp"]), by_expert(gain_p), ALU.mult))
            st(v.tensor_tensor(rt["b"], by_tile(rt_1["r"]), by_expert(gain_1), ALU.mult))
            st.wait()
            st(v.tensor_tensor(rt["a"], rt["a"], routed[:, :, 0:E], ALU.add))
            st(v.tensor_tensor(rt["b"], rt["b"], routed[:, :, E + DR + 1:RC], ALU.mult))
            st.wait()
            st.then(v.scalar_tensor_tensor(rt["a"], rt["b"], 0.02, rt["a"], ALU.mult, ALU.add))
            st.then(v.scalar_tensor_tensor(rt["logit"], by_expert(bias_e), 0.1, rt["a"], ALU.mult, ALU.add))
            for t in range(TILES):
                st(v.max(rt["top"][:, t, :], rt["logit"][:, t, :]))
            st.wait()
            for t in range(TILES):
                st(v.max_index(rt_i[:, t, :], rt["top"][:, t, :], rt["logit"][:, t, :]))
            v.tensor_tensor(rt_1["d"][:], rt["top"][:, :, 1], rt["top"][:, :, 0], ALU.subtract).then_inc(s_gd, 1)
            st.wait()
            st.then(v.tensor_copy(rt["f"], rt_i))
            st(v.tensor_tensor(rt["hot0"], by_expert(iota_e), rt["f"][:, :, 0:1].to_broadcast([P, TILES, E]), ALU.is_equal))
            st(v.tensor_tensor(rt["hot1"], by_expert(iota_e), rt["f"][:, :, 1:2].to_broadcast([P, TILES, E]), ALU.is_equal))
            st.wait()
            v.tensor_tensor(hots, rt["hot0"], rt["hot1"], ALU.add).then_inc(s_hots, 1)
            dve.wait_ge(s_ge, 1)
            st.then(v.tensor_scalar(rt_1["s"][:], rt_1["e"][:], 1.0, None, ALU.add))
            st.then(v.reciprocal(rt_1["g0"][:], rt_1["s"][:]))
            st.then(v.tensor_tensor(rt_1["g1"][:], rt_1["g0"][:], rt_1["e"][:], ALU.mult))
            st(v.tensor_tensor(rt["a"], rt["hot0"], by_tile(rt_1["g0"]), ALU.mult))
            st.then(v.tensor_tensor(rt["b"], rt["hot1"], by_tile(rt_1["g1"]), ALU.mult))
            v.tensor_tensor(rt["gate"], rt["a"], rt["b"], ALU.add).then_inc(s_gate, 1)
            st.then(v.memset(not_first, 1.0))
            st(v.memset(not_first[:, :, 0], 0.0))
            dve.wait_ge(s_cnt, 1)
            st.then(v.tensor_copy(tot, ps[:, 1, 0:TILES * E].rearrange("p (t e) -> p e t", e=E)))
            flat = [m.rearrange("p a b -> p (a b)") for m in (run_tot, not_first, tot)]
            st.then(v.tensor_tensor_scan(flat[0], flat[1], flat[2], 0.0, ALU.mult, ALU.add))
            st.then(v.tensor_scalar(cnt_i, run_tot[:, :, TILES - 1], float(P - 1), None, ALU.add))
            st.then(v.tensor_scalar(cnt_s, cnt_i, SHIFT, None, ALU.logical_shift_right))
            st.then(v.tensor_copy(n_slots, cnt_s))
            st.then(v.tensor_tensor_scan(end_slot, ones[:, 0:E], n_slots, 0.0, ALU.mult, ALU.add))
            st(v.tensor_tensor(past, iota_p[0:1, 0:SLOTS].unsqueeze(2).to_broadcast([1, SLOTS, E]),
                               end_slot[0:1, :].unsqueeze(1).to_broadcast([1, SLOTS, E]), ALU.is_ge))
            st.then(v.tensor_tensor(base_row, end_slot, n_slots, ALU.subtract))
            st(v.tensor_scalar(base_row, base_row, float(P), None, ALU.mult))
            st.then(v.tensor_tensor(offs, run_tot, tot, ALU.subtract))
            st.then(v.tensor_tensor(offs, offs, base_row.unsqueeze(2).to_broadcast([P, E, TILES]), ALU.add))
            st.then(v.tensor_tensor(full, ps[:, 0, 0:TILES * E].rearrange("p (t e) -> p t e", e=E),
                                    offs.rearrange("p e t -> p t e"), ALU.add))
            dve.sem_inc(s_counted, 1)
            for k in range(TOP):
                st(v.tensor_tensor(picked[k], full, rt[f"hot{k}"], ALU.mult))
            st.wait()
            for k in range(TOP):
                st(v.tensor_reduce(where_f[:, k, :], picked[k], AX.X, ALU.add))
            st.then(v.tensor_reduce(past_n, past, AX.X, ALU.add))
            st(v.tensor_scalar(slot_expert, past_n, float(E - 1), None, ALU.min))
            st.then(v.tensor_copy(where_i, where_f))
            st(v.tensor_scalar(slot_i, where_i, SHIFT, None, ALU.logical_shift_right))
            st.then(v.tensor_scalar(place_i, where_i, P - 1, None, ALU.bitwise_and))
            st(v.tensor_copy(slot_f, slot_i))
            st.then(v.tensor_copy(place_f, place_i))

            def each(m, n):
                return m.rearrange("p k t -> p (k t)").unsqueeze(2).to_broadcast([P, TOP * TILES, n])
            st.then(v.tensor_tensor(is_slot, iota_p[:, 0:SLOTS].unsqueeze(1).to_broadcast([P, TOP * TILES, SLOTS]), each(slot_f, SLOTS), ALU.is_equal))
            for h, part in enumerate((row_hi, row_lo)):
                st(v.tensor_tensor(hot_a[:, :, h, :], is_slot, each(part[:], SLOTS), ALU.mult))
            st.wait()
            for part in range(4):
                turn = slice(PART * part, PART * (part + 1))
                v.tensor_tensor(hot_b[:, turn, :], iota_p[:].unsqueeze(1).to_broadcast([P, PART, P]), each(place_f, P)[:, turn, :],
                                ALU.is_equal).then_inc(s_place, 1)
            dve.wait_ge(s_held, 1)
            st.then(v.tensor_copy(empty_s, ps[:, 2, 0:SLOTS]))
            st.then(v.tensor_tensor(held, ps[:, 2, SLOTS:2 * SLOTS], empty_s, ALU.add))
            st(v.tensor_scalar(src_2, held, -1.0, 0.0, ALU.add, ALU.max))
            st.then(v.tensor_scalar(empty, held, 0.0, None, ALU.is_equal))
            v.tensor_scalar(src_row, src_2, 1, None, ALU.logical_shift_right).then_inc(s_src, 1)
            st.then(v.tensor_tensor(empty_s, empty, spare[:], ALU.mult))
            v.scalar_tensor_tensor(dst_row, held, -1.0, empty_s, ALU.add, ALU.add).then_inc(s_dst, 1)
            for i in range(2):
                last = v.memset(slot_x_t[i][KC:KC + 1, KT - 1, :], 1.0)
            last.then_inc(s_one, 1)
            for first, bank, n in ((5, 0, 3), (0, 3, 5)):
                part = resid[:, 2 * first:2 * (first + n), :].rearrange("p (a b) c -> p a (b c)", b=2)
                last = v.tensor_tensor(part, part, ps[:, bank:bank + n, B2_AT:B2_AT + 2 * C], ALU.add)
            last.then_inc(s_acc, 1)

            def relu(s, half):
                dve.wait_ge(s_h_ps, s + 1)
                dve.wait_ge(s_ht_ps, s + 1)
                v.tensor_scalar(h_pos[half].rearrange("p (a b) -> p a b", a=2), ps[:, 0:2, 0:HH], 0.0, None, ALU.max).then_inc(s_hr, 1)

            def keep(s):
                dve.wait_ge(s_o2, s + 2)
                row = slot_rows[:, bass.ds(s, 1), :].rearrange("p a c -> p (a c)") if not isinstance(s, int) else slot_rows[:, s, :]
                v.tensor_copy(row, ps[:, 3, 0:C]).then_inc(s_y, 1)
            dve.sem_inc(s_y, 1)
            relu(0, 0)
            with dve.Fori(0, (SLOTS - 1) // 2) as pair:
                for i in range(2):
                    relu(2 * pair + 1 + i, 1 - i)
                    keep(2 * pair + i)
            keep(SLOTS - 1)
            for g in range(NG):
                dve.wait_ge(s_back[g], 16)
                if g == 0:
                    dve.wait_ge(s_acc, 1)
                if g:
                    tiles = slice(TG * g, TG * (g + 1))
                    for t in range(TG):
                        i = g * TG + t
                        st(v.scalar_tensor_tensor(resid[:, i, :], y_back(g)[:, t, 0:C], rt_1["g0"][:, i:i + 1], resid[:, i, :], ALU.mult, ALU.add))
                    dve.wait_ge(s_scaled, g)
                    st.wait()
                    v.tensor_tensor(resid[:, tiles, :], resid[:, tiles, :], y_back(g)[:, :, C:2 * C], ALU.add).then_inc(s_final, 1)
                    continue
                for k in range(TOP):
                    for t in range(TG):
                        i = g * TG + t
                        last = v.scalar_tensor_tensor(resid[:, i, :], y_back(g)[:, t, C * k:C * k + C], rt_1[f"g{k}"][:, i:i + 1],
                                                      resid[:, i, :], ALU.mult, ALU.add)
                        if k == 0:
                            st(last)
                    if k == 0:
                        st.wait()
                last.then_inc(s_final, 1)

        @block.scalar
        def _(act):
            a = nc.scalar
            a.preload_act_table_set("natural_log_exp_and_others")
            st = Steps(act, a_step)

            def rstd(t0, n, m, root, ready, k, done):
                act.wait_ge(ready, k)
                st.then(a.activation(nt2[:, t0:t0 + n], m[:, t0:t0 + n, 1], ACT.Ln, bias=eps_sb[:]))
                a.activation(root[:, t0:t0 + n], nt2[:, t0:t0 + n], ACT.Exp, scale=-0.5).then_inc(done, 1)

            act.wait_ge(s_setup_v, 1)

            def select_exp(h):
                half = slice(HT * h, HT * (h + 1))
                act.wait_ge(s_sel_d, h + 1)
                a.activation(sel_e[:, half], sel_d[:, half], ACT.Exp).then_inc(s_sel_e, 1)
                a.activation(ln_in[:, half, 0:SUB], rows[:, half], ACT.Copy).then_inc(s_cp, 1)

            def norm_roots(h):
                rstd(HT * h, HT, mv, rs, s_ln, h + 1, s_rstd)
                rstd(HT * h, HT, mv2, rs2, s_ln_in, h + 1, s_rstd_in)
            select_exp(0)
            norm_roots(0)
            act.wait_ge(s_par, 16 * (PAR_LOADS))
            a.activation(neg_a[:], chan_sb[:, :, CH_ALOG:CH_ALOG + 2 * NS].rearrange("p b (d n) -> p b d n", n=NS), ACT.Exp).then_inc(s_nega, 1)

            def keep_xn_t(g):
                act.wait_ge(s_xn_ps, g + 1)
                if g >= 2:
                    act.wait_ge(s_z, TG * (g - 1))
                for k in range(KT):
                    a.activation(xn_t[g % 2][:, k, :], ps[0:KC, k, :], ACT.Identity, scale=gb_in_sb[:, k, 0:1],
                                 bias=gb_in_sb[:, k, 1:2]).then_inc(s_xn_t, 1)

            select_exp(1)
            keep_xn_t(0)
            keep_xn_t(1)
            norm_roots(1)
            for g in range(NG):
                if 0 < g < NG - 1:
                    keep_xn_t(g + 1)
                if g >= 2:
                    act.wait_ge(s_gate_in, g - 1)
                for t in range(TG):
                    n = TG * g + t
                    act.wait_ge(s_z, n + 1)
                    a.activation(sz[g % 2][:, t, :], ps[:, 5 + n % 3, 0:DI], ACT.Silu).then_inc(s_sz, 1)
                for blk in range(DB):
                    act.wait_ge(s_conv, DB * g + blk + 1)
                    a.activation(u_all[g][:, blk, :], conv[g % 2][:, blk, :], ACT.Silu).then_inc(s_u, 1)

            def keep_lb(g):
                act.wait_ge(s_lb_ps, g + 1)
                if g >= 2:
                    act.wait_ge(s_b_st[g % 2], 32)
                a.activation(lb[g % 2], ps[0:96, 0, :], ACT.Copy, scale=row_scale[:]).then_inc(s_lb, 1)

            a.preload_act_table_set("natural_log_exp_and_others")
            keep_lb(0)
            for g in range(NG):
                for d in range(2):
                    n = 2 * g + d
                    if n >= SP:
                        act.wait_ge(s_dt, n - SP + 1)
                    if n == 0:
                        act.wait_ge(s_u, NG * DB)
                    if n == 2:
                        act.wait_ge(s_gate_in, NG)
                    if n == 4:
                        for i in range(2):
                            act.wait_ge(s_gate_st[i], 16 * NG // 2)
                    dt = dt_all[g][d]
                    for blk in range(DB):
                        act.wait_ge(s_dt_ps, DB * n + blk + 1)
                        bias = chan_sb[:, blk, CH_DTB + d:CH_DTB + d + 1]
                        bank = ps[:, DT_BANK + DB * d + blk, :]
                        st(a.activation(dt[:, blk, :], bank, ACT.Abs, bias=bias))
                        a.activation(sp_pos[n % SP][:, blk, :], bank, ACT.Relu, bias=bias).then_inc(s_pos, 1)
                    st.wait()
                    a.activation(sp_e[n % SP], dt, ACT.Exp, scale=-1.0).then_inc(s_e, 1)
                    if d == 1 and g + 1 < NG:
                        keep_lb(g + 1)
                    act.wait_ge(s_e, n + 1)
                    a.activation(dt, sp_e[n % SP], ACT.Ln, bias=1.0).then_inc(s_l, 1)

            def exps(k, g, G):
                d, blk = divmod(k, DB)
                act.wait_ge(s_scan, PER_QUAD * G + k + 1 - DECAYS + PER_QUAD)
                out_b = decay[k % DECAYS].rearrange("p n (s t) -> p n s t", t=SEQ)
                src = dt_all[g][d][:, blk, :].rearrange("p (s t) -> p s t", t=SEQ)
                lo, hi = (1, SEQ) if d == 0 else (0, SEQ - 1)
                for n in range(QN):
                    q = G - NQ * g
                    scale = neg_a[:, blk, d, bass.ds(q * QN + n, 1)]
                    a.activation(out_b[:, n, :, lo:hi], src[:, :, lo:hi], ACT.Exp, scale=scale)
                a.activation(out_b[:, :, :, 0 if d == 0 else SEQ - 1], zeros[:], ACT.Copy).then_inc(s_decay, 1)

            def keep_y(g):
                act.wait_ge(s_sum, SUM0 + NQ * PER_QUAD * (g + 1))
                for t in range(TG):
                    last = a.activation(y_all[g][:, t, :], y_ps[:, DI * t:DI * (t + 1)], ACT.Copy, accum_out=y_sum[:, TG * g + t:TG * g + t + 1])
                last.then_inc(s_yv, 1)

            def moments_y(g):
                tiles = slice(TG * g, TG * (g + 1))
                act.wait_ge(s_yv, g + 1)
                st(a.activation(mv[:, tiles, 0], y_sum[:, tiles], ACT.Copy, scale=1.0 / DI))
                st.then(a.activation(y_neg[:, tiles], y_sum[:, tiles], ACT.Copy, scale=-1.0 / DI))
                for t in range(TG):
                    i = TG * g + t
                    st(a.activation(ps[:, 7, P:P + DI], y_all[g][:, t, :], ACT.Square, bias=y_neg[:, i:i + 1], accum_out=y_sq[:, i:i + 1]))
                    st.wait()
                a.activation(mv[:, tiles, 1], y_sq[:, tiles], ACT.Copy, scale=1.0 / DI).then_inc(s_ln_y, 1)

            act.wait_ge(s_dt, 2 * NG)
            for i in range(2):
                act.wait_ge(s_b_st[i], 32 * NG // 2)
                act.wait_ge(s_stack[i], 48 * NG // 2)
            for g in range(NG):
                for k in range(PER_QUAD):
                    exps(k, g, NQ * g)
                    if g and k == DB:
                        keep_y(g - 1)
                if g:
                    moments_y(g - 1)
                if g == NG - 1:
                    rstd(0, TG * g, mv, rs, s_ln_y, g, s_rstd_y)
                with act.Fori(NQ * g + 1, NQ * (g + 1)) as G:
                    for k in range(PER_QUAD):
                        exps(k, g, G)

            def load_gate(g):
                act.dma_start(gate_back[g].rearrange("p a b c -> p (a b c)"), gates_dram[g]).then_inc(s_gate_ld[g], 16)

            act.wait_ge(s_sum, SUM0 + NG * NQ * PER_QUAD)
            act.dma_start(w_out_sb, w_out).then_inc(s_w_out, 16)
            load_gate(1)
            load_gate(2)
            keep_y(NG - 1)
            rstd(TG * (NG - 1), TG, mv, rs, s_ln_y, NG, s_rstd_y)
            def keep_y_t(g):
                act.wait_ge(s_yt_ps, g + 1)
                if g >= 2:
                    act.wait_ge(s_o_ps, g - 1)
                a.activation(y_t[g % 2], ps[:, 0:DB, :], ACT.Copy).then_inc(s_yt, 1)
                if g == 1:
                    act.wait_ge(s_yn, g + 1)
                    load_gate(g + 2)

            def route(g):
                act.wait_ge(s_xg, g + 1)
                act.dma_start(x_rows[GT * g:GT * (g + 1), :].rearrange("(t p) c -> p t c", p=P), x_g[g % 2]).then_inc(s_xs[g % 2], 16)
                act.wait_ge(s_xg_ps, g + 1)
                if g >= 2:
                    act.wait_ge(s_r_ps, g - 1)
                a.activation(x_g_t[g % 2], ps[0:KC, 5:5 + KT, :], ACT.Copy).then_inc(s_xg_t, 1)

            def keep_routed(g):
                act.wait_ge(s_r_ps, g + 1)
                a.activation(routed[:, TG * g:TG * (g + 1), :],
                             ps[:, 7, :].rearrange("p (t c) -> p t c", t=TG)[:, :, 0:RC], ACT.Copy).then_inc(s_r, 1)

            keep_y_t(0)
            for g in range(NG):
                if g + 1 < NG:
                    keep_y_t(g + 1)
                if g == NG - 1:
                    route(g - 1)
                rstd(TG * g, TG, mv2, rs2, s_ln2, g + 1, s_rstd2)
                if g == NG - 1:
                    act.wait_ge(s_wr, 1)
                    a.activation(gain[:], gain_1[:], ACT.Sqrt).then_inc(s_nrm_r, 1)
                elif g:
                    route(g - 1)
                if g:
                    keep_routed(g - 1)
            route(NG - 1)
            keep_routed(NG - 1)
            act.dma_start(w1[KC:KC + 1, :, 1, :], b1).then_inc(s_bias, 16)
            act.wait_ge(s_r, NG)
            a.activation(rt_sq, routed[:, :, E:E + DR], ACT.Square).then_inc(s_nrm, 1)
            act.wait_ge(s_nrm_r, 2)
            a.activation(rt_1["n"][:], rt_1["n2"][:], ACT.Sqrt).then_inc(s_nrm_r, 1)
            act.wait_ge(s_gd, 1)
            a.activation(rt_1["e"][:], rt_1["d"][:], ACT.Exp).then_inc(s_ge, 1)
            for part in range(4):
                act.wait_ge(s_gt_ps, part + 1)
                a.activation(gate_t[:, GT * part:GT * (part + 1)], ps[0:E, 3 + part, :], ACT.Copy).then_inc(s_gt, 1)

            def copy_x(s, half):
                act.wait_ge(s_slot_in, s + 1)
                if not isinstance(s, int) or s >= 2:
                    act.wait_ge(s_xt_ps, s - 1)
                a.activation(x_cur[half], slot_rows[:, bass.ds(s, 1), :].rearrange("p a c -> p (a c)"), ACT.Copy).then_inc(s_xc, 1)

            def keep_x_t(s, half):
                act.wait_ge(s_xt_ps, s + 1)
                if not isinstance(s, int) or s >= 2:
                    act.wait_ge(s_h_ps, s - 1)
                a.activation(slot_x_t[half][0:KC], ps[0:KC, 2, 0:KT * P].rearrange("p (k t) -> p k t", t=P), ACT.Copy).then_inc(s_xt, 1)

            def square(s, half):
                act.wait_ge(s_ht_ps, s + 3)
                if not isinstance(s, int) or s >= 2:
                    act.wait_ge(s_o2, s)
                a.activation(h_t[half].rearrange("p (a b) c -> p a (b c)", a=2), ps[:, 4:6, 0:HH], ACT.Square).then_inc(s_h, 1)
            copy_x(0, 0)
            copy_x(1, 1)
            keep_x_t(0, 0)
            copy_x(2, 0)
            keep_x_t(1, 1)
            square(0, 0)
            with act.Fori(0, (SLOTS - 3) // 2) as pair:
                for i in range(2):
                    s = 2 * pair + 1 + i
                    copy_x(s + 2, 1 - i)
                    keep_x_t(s + 1, i)
                    square(s, 1 - i)
            keep_x_t(SLOTS - 1, 0)
            square(SLOTS - 2, 1)
            square(SLOTS - 1, 0)

            for g in range(1, NG):
                act.wait_ge(s_back[g], 16)
                for t in range(TG):
                    y = y_back(g)[:, t, C:2 * C]
                    last = a.activation(y, y, ACT.Copy, scale=rt_1["g1"][:, TG * g + t:TG * g + t + 1])
                last.then_inc(s_scaled, 1)

        @block.tensor
        def _(pe):
            t_ = nc.tensor
            mm = t_.matmul

            def transpose(o, src, parts, start=True):
                return mm(o, src, ident[0:parts, 0:parts], start=start, stop=True, is_transpose=True, skip_group_check=True)

            pe.wait_ge(s_ident, 1)
            pe.wait_ge(s_par, 16 * (PAR_LOADS))
            def norm_transposes(g):
                pe.wait_ge(s_xn, g + 1)
                for t in range(TG):
                    for k in range(KT):
                        last = transpose(ps[0:KC, k, P * t:P * t + P], xn[g % 2][:, t, KC * k:KC * k + KC], P)
                last.then_inc(s_xn_ps, 1)

            norm_transposes(0)
            for g in range(NG):
                x = xn_t[g % 2]
                pe.wait_ge(s_xn_t, KT * (g + 1))
                for blk in range(DB):
                    if g:
                        pe.wait_ge(s_conv, DB * (g - 1) + blk + 1)
                    for k in range(KT):
                        last = mm(ps[:, 2 + blk, :], w_in_sb[:, k, P * blk:P * blk + P], x[:, k, :], start=k == 0, stop=k == KT - 1)
                    last.then_inc(s_xi, 1)
                if g + 1 < NG:
                    norm_transposes(g + 1)
                for t in range(TG):
                    n = TG * g + t
                    if n >= 3:
                        pe.wait_ge(s_sz, n - 2)
                    for k in range(KT):
                        last = mm(ps[:, 5 + n % 3, 0:DI], x[:, k, P * t:P * t + P], w_in_sb[:, k, DI:2 * DI], start=k == 0, stop=k == KT - 1)
                    last.then_inc(s_z, 1)

            def projections(g):
                pe.wait_ge(s_u, DB * (g + 1))
                if g:
                    pe.wait_ge(s_lb, g)
                    pe.wait_ge(s_split, g)
                for blk in range(DB):
                    last = mm(ps[:, 0, :], w_x[:, blk, :], u_all[g][:, blk, :], start=blk == 0, stop=blk == DB - 1)
                last.then_inc(s_lb_ps, 1)

            projections(0)
            pe.wait_ge(s_conv, NG * DB)
            pe.wait_ge(s_sz, NG * TG)
            for g in range(NG):
                pe.wait_ge(s_lb, g + 1)
                for d in range(2):
                    for blk in range(DB):
                        if g:
                            pe.wait_ge(s_pos, DB * (2 * (g - 1) + d) + blk + 1)
                        mm(ps[:, DT_BANK + DB * d + blk, :], dt_w_sb[32 * d:32 * d + RANK, P * blk:P * blk + P],
                           lb[g % 2][32 * d:32 * d + RANK, :], start=True, stop=True).then_inc(s_dt_ps, 1)
                if g + 1 < NG:
                    projections(g + 1)

            def c_rows(g, G, d):
                pe.wait_ge(s_mul, DB * (2 * G + d) + MUL0)
                for n in range(QN):
                    j = (G - NQ * g) * QN + n + NS * d
                    last = mm(ps[:, BCAST + n, :], pick[:, bass.ds(j, 1)].to_broadcast([96, P]), c_all[:, g, :], start=True, stop=True)
                last.then_inc(s_c_ps, 1)

            def add(k, G, opens=False):
                blk = k % DB
                pe.wait_ge(s_mul, PER_QUAD * G + k + 1 + MUL0)
                for n in range(QN):
                    for t in range(TG):
                        c = t * DB + blk
                        first = opens and n == 0 and (t == 0 or c // 4 != (c - DB) // 4)
                        last = transpose(y_ps[:, P * c:P * c + P], prod[k % 2][:, n, P * t:P * t + P], P, start=first)
                last.then_inc(s_sum, 1)

            def skip_term(g, tiles):
                for t in tiles:
                    for blk in range(DB):
                        c = t * DB + blk
                        mm(y_ps[:, P * c:P * c + P], u_all[g][:, blk, P * t:P * t + P], skip[:, blk, :], start=False, stop=True,
                           skip_group_check=True)

            def quad(g, G, first=False, tiles=()):
                c_rows(g, G, 0)
                if not (first and g == 0):
                    add(PER_QUAD - 1, G - 1)
                if first and g:
                    pe.wait_ge(s_yv, g)
                add(0, G, opens=first)
                add(1, G)
                c_rows(g, G, 1)
                add(2, G)
                add(3, G)
                skip_term(g, tiles)
                add(4, G)

            pe.wait_ge(s_lb, NG)
            for i in range(2):
                pe.wait_ge(s_stack[i], 48 * NG // 2)
            pe.wait_ge(s_pos, 2 * NG * DB)
            pe.wait_ge(s_skip, 1)
            pe.wait_ge(s_esq, 1)
            mm(ps[:, 7, 0:E], ones[0:DR, :], emb_sq[:], start=True, stop=True)
            for k in range(KT):
                last = mm(ps[0:KC, 7, (1 + k) * E:(2 + k) * E], w_probe[:, KC * k:KC * k + KC], emb_t_sb[:], start=True, stop=True)
            last.then_inc(s_rset, 1)
            pe.sem_inc(s_sum, SUM0)
            for g in range(NG):
                quad(g, NQ * g, first=True, tiles=(0, 1))
                with pe.Fori(NQ * g + 1, NQ * g + NQ - 1) as G:
                    quad(g, G)
                quad(g, NQ * g + NQ - 1, tiles=(2, 3))
            add(PER_QUAD - 1, NG * NQ - 1)

            pe.wait_ge(s_yv, NG)
            pe.wait_ge(s_w_out, 16)
            pe.wait_ge(s_wr, 1)

            def y_transposes(g):
                pe.wait_ge(s_yn, g + 1)
                if g:
                    pe.wait_ge(s_yt, g)
                for t in range(TG):
                    for blk in range(DB):
                        last = transpose(ps[:, blk, P * t:P * t + P], y_all[g][:, t, P * blk:P * blk + P], P)
                last.then_inc(s_yt_ps, 1)

            def out_product(g):
                pe.wait_ge(s_yt, g + 1)
                if g:
                    pe.wait_ge(s_added, g)
                for t in range(TG):
                    for blk in range(DB):
                        last = mm(ps[:, 3 + t // 2, C * (t % 2):C * (t % 2) + C], y_t[g % 2][:, blk, P * t:P * t + P], w_out_sb[:, blk, :],
                                  start=blk == 0, stop=blk == DB - 1)
                last.then_inc(s_o_ps, 1)

            def route(g):
                pe.wait_ge(s_xg, g + 1)
                if g:
                    pe.wait_ge(s_xg_t, g)
                for t in range(TG):
                    for k in range(KT):
                        last = transpose(ps[0:KC, 5 + k, P * t:P * t + P], x_g[g % 2][:, t, KC * k:KC * k + KC], P)
                last.then_inc(s_xg_ps, 1)
                pe.wait_ge(s_xg_t, g + 1)
                if g:
                    pe.wait_ge(s_r, g)
                for t in range(TG):
                    for k in range(KT):
                        last = mm(ps[:, 7, P * t:P * t + RC], x_g_t[g % 2][:, k, P * t:P * t + P], w_route_sb[:, k, :],
                                  start=k == 0, stop=k == KT - 1)
                last.then_inc(s_r_ps, 1)

            y_transposes(0)
            for g in range(NG):
                out_product(g)
                if g + 1 < NG:
                    y_transposes(g + 1)
                if g:
                    route(g - 1)
            route(NG - 1)
            pe.wait_ge(s_hots, 1)
            hot_cols = hots.rearrange("p t e -> p (t e)")
            mm(ps[:, 0, 0:TILES * E], before[:], hot_cols, start=True, stop=True)
            mm(ps[:, 1, 0:TILES * E], ones[:], hot_cols, start=True, stop=True).then_inc(s_cnt, 1)
            pe.wait_ge(s_gate, 1)
            for part in range(4):
                for t in range(TG):
                    last = transpose(ps[0:E, 3 + part, P * t:P * t + P], rt["gate"][:, TG * part + t, :], P)
                last.then_inc(s_gt_ps, 1)
            pe.wait_ge(s_gt, 4)
            pe.wait_ge(s_counted, 1)
            for i in range(TILES):
                bank = B2_BANKS[i // 2]
                mm(ps[:, bank, B2_AT + C * (i % 2):B2_AT + C * (i % 2 + 1)], gate_t[:, P * i:P * i + P], b2_sb[:], start=True, stop=True,
                   skip_group_check=True)
            for i in range(TOP * TILES):
                if i % PART == 0:
                    pe.wait_ge(s_place, i // PART + 1)
                last = mm(ps[:, 2, 0:2 * SLOTS], hot_b[:, i, :], hot_a[:, i, :, :].rearrange("p h b -> p (h b)"), start=i == 0, stop=i == TOP * TILES - 1)
            last.then_inc(s_held, 1)
            pe.wait_ge(s_acc, 1)
            w1_flat = w1.rearrange("p e a b -> p (e a b)")
            w2_all = w2.rearrange("p e a b -> p (e a b)")

            def expert_of(s):
                return t_.value_load(slot_expert[0:1, bass.ds(s, 1)], min_val=0, max_val=E - 1)

            def x_transposes(s, half):
                pe.wait_ge(s_xc, s + 1)
                for k in range(KT):
                    last = transpose(ps[0:KC, 2, P * k:P * k + P], x_cur[half][:, KC * k:KC * k + KC], P)
                last.then_inc(s_xt_ps, 1)

            def first_product(s, half, e):
                pe.wait_ge(s_w1, e + 1)
                pe.wait_ge(s_xt, s + 1)
                if not isinstance(s, int) or s:
                    pe.wait_ge(s_hr, s)
                for h in range(2):
                    for k in range(KT):
                        last = mm(ps[:, h, 0:HH], slot_x_t[half][0:KC + k, k, :],
                                  w1_flat[0:KC + k, bass.ds(e * (KT * H) + (k * H + h * HH), HH)], start=k == 0, stop=k == KT - 1)
                last.then_inc(s_h_ps, 1)

            def second_product(s, half, e):
                pe.wait_ge(s_w2, e + 1)
                pe.wait_ge(s_h, s + 1)
                pe.wait_ge(s_y, s + 1)
                for j in range(HB):
                    last = mm(ps[:, 3, 0:C], h_t[half][:, j, :], w2_all[:, bass.ds(e * (HB * C) + j * C, C)], start=j == 0, stop=j == HB - 1)
                last.then_inc(s_o2, 1)

            def h_transposes(s, half):
                pe.wait_ge(s_hr, s + 1)
                if not isinstance(s, int) or s:
                    pe.wait_ge(s_h, s)
                for j in range(HB):
                    last = transpose(ps[:, 4 + j // 3, P * (j % 3):P * (j % 3) + P], h_pos[half][:, P * j:P * j + P], P)
                last.then_inc(s_ht_ps, 1)
            pe.wait_ge(s_dst, 1)
            pe.wait_ge(s_one, 1)
            pe.wait_ge(s_bias, 16)
            pe.sem_inc(s_ht_ps, 2)
            pe.sem_inc(s_o2, 1)
            x_transposes(0, 0)
            first_product(0, 0, expert_of(0))
            x_transposes(1, 1)
            h_transposes(0, 0)

            def slot(s, half):
                first_product(s, half, expert_of(s))
                if not (isinstance(s, int) and s == SLOTS - 1):
                    x_transposes(s + 1, 1 - half)
                second_product(s - 1, 1 - half, expert_of(s - 1))
                h_transposes(s, half)
            with pe.Fori(0, (SLOTS - 3) // 2) as pair:
                for i in range(2):
                    slot(2 * pair + 1 + i, 1 - i)
            slot(SLOTS - 2, 1)
            slot(SLOTS - 1, 0)
            second_product(SLOTS - 1, 0, expert_of(SLOTS - 1))


def _positions():
    import numpy as np
    depth = C // 2
    depths = (np.arange(depth, dtype=np.float32) / np.float32(depth))[None, :]
    rates = (np.float32(1.0) / np.power(np.float32(10000.0), depths)).astype(np.float32)
    rad = np.arange(SEQ, dtype=np.float32)[:, None] * rates
    table = np.concatenate([np.sin(rad), np.cos(rad)], axis=-1).astype(np.float32)
    return np.ascontiguousarray(table.reshape(SEQ // P, P, C).transpose(1, 0, 2))


def kernel(**inputs):
    import numpy as np
    import concourse.bacc as bacc
    from concourse.bass_utils import run_bass_kernel_spmd

    a = {k.replace("L0_", ""): np.asarray(v) for k, v in inputs.items()}

    def per_channel(m, blocks):
        return m.reshape((blocks, m.shape[0] // blocks) + m.shape[1:]).swapaxes(0, 1)

    def per_expert(m, blocks):
        return m.reshape(E, blocks, m.shape[1] // blocks, m.shape[2]).transpose(0, 2, 1, 3)

    chan = np.concatenate([a["attn_conv_w"], a["attn_conv_b"][:, None], a["attn_dt_b"].T,
                           a["attn_A_log"].transpose(1, 0, 2).reshape(DI, 2 * NS), a["attn_D_skip"].T], axis=1)
    arrays = {
        "tok": a["x"].reshape(TILES, P).T,
        "emb": a["tok_emb_table"],
        "spos": np.stack([a["tok_spos0"], a["tok_spos1"]]).reshape(1, -1),
        "pos": _positions(),
        "chan": per_channel(chan, DB),
        "w_in": per_channel(a["attn_W_in"], KT),
        "gb_in": per_channel(np.stack([a["attn_gamma_in"], a["attn_beta_in"]], axis=1), KT),
        "xproj": a["attn_x_proj_w"].reshape(2, DB, P, RANK + 2 * NS).transpose(2, 0, 1, 3),
        "dt_w": a["attn_dt_w"],
        "gb_out": np.concatenate([a["attn_gamma_out"], a["attn_beta_out"]]).reshape(1, -1),
        "w_out": per_channel(a["attn_W_out"], DB),
        "merge": a["attn_merge_w"].reshape(1, 2),
        "w_route": per_channel(np.concatenate([a["ffn_router_w"].T, a["ffn_probe_w"].T], axis=1), KT),
        "emb_t": np.concatenate([a["ffn_router_emb"].T, a["ffn_probe_w"]], axis=1),
        "energy": a["ffn_energy"].reshape(1, E),
        "fatigue": a["ffn_fatigue"].reshape(1, E),
        "gates12": np.concatenate([a["ffn_m_gate1"], a["ffn_m_gate2"]]).reshape(1, 2 * E),
        "b1": a["ffn_b1"].reshape(1, E, H),
        "b2": a["ffn_b2"],
        "wf1": per_expert(a["ffn_w_fast1"], KT),
        "ws1": per_expert(a["ffn_w_slow1"], KT),
        "hf1": per_expert(a["ffn_h_fast1"], KT),
        "wf2": per_expert(a["ffn_w_fast2"], HB),
        "ws2": per_expert(a["ffn_w_slow2"], HB),
        "hf2": per_expert(a["ffn_h_fast2"], HB),
    }
    arrays = {k: np.ascontiguousarray(m) for k, m in arrays.items()}
    nc = bacc.Bacc("TRN2", target_bir_lowering=False, num_devices=1)
    aps = {k: nc.dram_tensor(k, m.shape, mybir.dt.from_np(m.dtype), kind="ExternalInput").ap() for k, m in arrays.items()}
    out = nc.dram_tensor("out", (TOK, C), FP32, kind="ExternalOutput").ap()
    gates_dram = nc.dram_tensor("gates_dram", (NG, P, GATE_W), FP32, kind="Internal").ap()
    b_rows = nc.dram_tensor("b_rows", (2, NG * NS, GT), FP32, kind="Internal").ap()
    x_rows = nc.dram_tensor("x_rows", (TOK, C), FP32, kind="Internal").ap()
    y_rows = nc.dram_tensor("y_rows", (TOP * TOK + SLOTS * P, C), FP32, kind="Internal").ap()
    build(nc, gates_dram=gates_dram, b_rows=b_rows, x_rows=x_rows, y_rows=y_rows, out=out, **aps)
    r = run_bass_kernel_spmd(nc, [arrays], core_ids=[0])
    return r.results[0]["out"].reshape(BATCH, SEQ, C)
```
